# Optimizing a Trainium2 kernel written in Bass

```python
import numpy as np
import jax
import jax.numpy as jnp

def _softmax(x, axis=-1):
    return jax.nn.softmax(x, axis=axis)

def _gelu(x):
    return jax.nn.gelu(x, approximate=True)

def _silu(x):
    return jax.nn.silu(x)

def _sigmoid(x):
    return jax.nn.sigmoid(x)

def _layernorm(x, axis=-1, eps=1e-05):
    m = jnp.mean(x, axis=axis, keepdims=True)
    v = jnp.var(x, axis=axis, keepdims=True)
    return (x - m) / jnp.sqrt(v + eps)

def _scatter_add(tgt, idx, src, axis=0):
    return tgt.at[idx].add(src)

def _segment_sum(src, seg, n):
    return jax.ops.segment_sum(src, seg, n)
kernel_name = 'mk_gps_d2_gnn_r8_11e3b3'

def setup_inputs(seed: int=0):
    np.random.seed(seed)
    _w = jnp.asarray

    def _rec_inputs():
        import jax
        import jax.numpy as jnp
        _gk = jax.random.key(seed)
        x = -8.776e-05 + 1 * jax.random.normal(jax.random.fold_in(_gk, 1), (1250, 512), jnp.float32)
        _s = jax.random.randint(jax.random.fold_in(_gk, 2), (10000,), 0, 1250, jnp.int32)
        _d = jax.random.randint(jax.random.fold_in(_gk, 3), (10000,), 0, 1250, jnp.int32)
        _loop = jnp.arange(1250, dtype=jnp.int32)
        src = jnp.concatenate([_s, _d, _loop])
        dst = jnp.concatenate([_d, _s, _loop])
        _o = jnp.argsort(dst, stable=True)
        src = src[_o]
        dst = dst[_o]
        edge_attr_4 = 0.00171547 + 0.999346 * jax.random.normal(jax.random.fold_in(_gk, 12), (21250, 4), jnp.float32)
        edge_attr_8 = 0.000126197 + 0.999763 * jax.random.normal(jax.random.fold_in(_gk, 13), (21250, 8), jnp.float32)
        return (x, src, dst, edge_attr_4, edge_attr_8)
    x, src, dst, edge_attr_4, edge_attr_8 = _rec_inputs()

    def _L0_gnn_setup():
        import jax, jax.numpy as jnp
        import numpy as np
        MUL = 128
        N_NODES = 1250
        N_EDGES = 20000
        R_BASIS = 8
        HIDDEN = 64
        W_NUMEL = 4 * MUL
        SQRT3 = 3.0 ** 0.5
        SILU_2MOM = 1.679177
        AVG_NUM_NEIGHBORS = 10.0

        def _lin_irreps(x0, x1, W0, W1):
            y0 = x0 @ W0 / jnp.sqrt(jnp.float32(W0.shape[0]))
            y1 = jnp.einsum('num,uv->nvm', x1, W1) / jnp.sqrt(jnp.float32(W1.shape[0]))
            return (y0, y1)

        def _forward(node_feats, edge_attrs, edge_feats, edge_index, W_up0, W_up1, W_mlp1, W_mlp2, W_mlp3, W_mlp4, W_out0, W_out1):
            num_nodes = node_feats.shape[0]
            sender, receiver = (edge_index[0], edge_index[1])
            x0 = node_feats[:, :MUL]
            x1 = node_feats[:, MUL:].reshape(num_nodes, MUL, 3)
            x0, x1 = _lin_irreps(x0, x1, W_up0, W_up1)
            h = edge_feats
            for W in (W_mlp1, W_mlp2, W_mlp3):
                h = SILU_2MOM * jax.nn.silu(h @ W / jnp.sqrt(jnp.float32(W.shape[0])))
            tpw = h @ W_mlp4 / jnp.sqrt(jnp.float32(W_mlp4.shape[0]))
            w1, w2, w3, w4 = jnp.split(tpw, 4, axis=-1)
            s0 = x0[sender]
            s1 = x1[sender]
            y0 = edge_attrs[:, 0:1]
            y1 = edge_attrs[:, 1:4]
            p1 = w1 * s0 * y0
            p2 = (w2 * s0)[:, :, None] * y1[:, None, :]
            p3 = w3[:, :, None] * s1 * y0[:, None, :]
            p4 = w4 * jnp.einsum('eum,em->eu', s1, y1) / SQRT3
            m0 = jnp.concatenate([p1, p4], axis=-1)
            m1 = jnp.concatenate([p2, p3], axis=1)
            msg0 = jax.ops.segment_sum(m0, receiver, num_segments=num_nodes)
            msg1 = jax.ops.segment_sum(m1, receiver, num_segments=num_nodes)
            o0, o1 = _lin_irreps(msg0, msg1, W_out0, W_out1)
            out = jnp.concatenate([o0, o1.reshape(num_nodes, 3 * MUL)], axis=-1)
            return out / AVG_NUM_NEIGHBORS
        key = jax.random.key(seed)
        ks = jax.random.split(key, 12)
        rn = lambda k, s: jax.random.normal(k, s, dtype=jnp.float32)
        return {'node_feats': rn(ks[0], (N_NODES, 4 * MUL)), 'edge_attrs': rn(ks[1], (N_EDGES, 4)), 'edge_feats': rn(ks[2], (N_EDGES, R_BASIS)), 'edge_index': jax.random.randint(ks[3], (2, N_EDGES), 0, N_NODES), 'W_up0': rn(ks[4], (MUL, MUL)), 'W_up1': rn(ks[5], (MUL, MUL)), 'W_mlp1': rn(ks[6], (R_BASIS, HIDDEN)), 'W_mlp2': rn(ks[7], (HIDDEN, HIDDEN)), 'W_mlp3': rn(ks[8], (HIDDEN, HIDDEN)), 'W_mlp4': rn(ks[9], (HIDDEN, W_NUMEL)), 'W_out0': rn(ks[10], (2 * MUL, MUL)), 'W_out1': rn(ks[11], (2 * MUL, MUL))}
    _L0_gnn_all = _L0_gnn_setup()
    _L0_gnn_in = {k: v for k, v in _L0_gnn_all.items() if k in ('W_up0', 'W_up1', 'W_mlp1', 'W_mlp2', 'W_mlp3', 'W_mlp4', 'W_out0', 'W_out1')}
    del _L0_gnn_all

    def _L0_mix_setup():
        import jax, jax.numpy as jnp
        import numpy as np
        DIM = 512
        HEADS = 8
        DIM_HEAD = 64
        KEY_RATIO = 4
        INNER = HEADS * DIM_HEAD
        B, N = (8, 2048)
        key = jax.random.key(seed)
        ks = jax.random.split(key, 8)
        s_in = 1.0 / np.sqrt(DIM)
        s_h = 1.0 / np.sqrt(DIM_HEAD)
        s_out = 1.0 / np.sqrt(INNER)
        return {'x': jax.random.normal(ks[0], (B, N, DIM), dtype=jnp.float32), 'W_in': jax.random.uniform(ks[1], (DIM, INNER), jnp.float32, -s_in, s_in), 'b_in': jax.random.uniform(ks[2], (INNER,), jnp.float32, -s_in, s_in), 'W_q': jax.random.uniform(ks[3], (DIM_HEAD, KEY_RATIO), jnp.float32, -s_h, s_h), 'W_k': jax.random.uniform(ks[4], (DIM_HEAD, KEY_RATIO), jnp.float32, -s_h, s_h), 'W_v': jax.random.uniform(ks[5], (DIM_HEAD, DIM_HEAD), jnp.float32, -s_h, s_h), 'W_out': jax.random.uniform(ks[6], (INNER, DIM), jnp.float32, -s_out, s_out), 'b_out': jax.random.uniform(ks[7], (DIM,), jnp.float32, -s_out, s_out)}
    _L0_mix_all = _L0_mix_setup()
    _L0_mix_in = {k: v for k, v in _L0_mix_all.items() if k in ('W_in', 'b_in', 'W_q', 'W_k', 'W_v', 'W_out', 'b_out')}
    del _L0_mix_all

    def _L0_ffn_setup():
        import jax, jax.numpy as jnp
        import numpy as np
        SINKHORN_ITERS = 8
        TEMPERATURE = 1.0
        EPS = 1e-10

        def sinkhorn(gates):
            t = jnp.log(jnp.clip(gates, EPS)) / TEMPERATURE

            def body(t, _):
                t = t - jax.nn.logsumexp(t, axis=-2, keepdims=True)
                t = t - jax.nn.logsumexp(t, axis=-1, keepdims=True)
                return (t, None)
            t, _ = jax.lax.scan(body, t, None, length=SINKHORN_ITERS)
            return jnp.exp(t)
        key = jax.random.key(seed)
        k1, k2, k3 = jax.random.split(key, 3)
        b, n, d, e, h = (4, 1024, 512, 8, 1)
        x = jax.random.normal(k1, (b, n, d), dtype=jnp.float32)
        gate_w = jax.random.normal(k2, (h, d, e), dtype=jnp.float32)
        experts = jax.random.normal(k3, (e, d, d), dtype=jnp.float32) / np.sqrt(d)
        return {'x': x, 'gate_w': gate_w, 'experts': experts}
    _L0_ffn_all = _L0_ffn_setup()
    _L0_ffn_in = {k: v for k, v in _L0_ffn_all.items() if k in ('gate_w', 'experts')}
    del _L0_ffn_all

    def _L1_gnn_setup():
        import jax, jax.numpy as jnp
        import numpy as np
        N, E, DM, H, DFF = (2500, 80000, 512, 8, 256)
        DK = DM // H

        def _layernorm(x, g, b, eps=1e-05):
            mu = jnp.mean(x, axis=-1, keepdims=True)
            var = jnp.mean(jnp.square(x - mu), axis=-1, keepdims=True)
            return (x - mu) * jax.lax.rsqrt(var + eps) * g + b
        key = jax.random.key(seed)
        ks = jax.random.split(key, 12)
        s = 0.02
        h = jax.random.normal(ks[0], (N, DM), dtype=jnp.float32)
        src = jax.random.randint(ks[1], (E,), 0, N, dtype=jnp.int32)
        dst = jnp.sort(jax.random.randint(ks[2], (E,), 0, N, dtype=jnp.int32))
        return {'h': h, 'src': src, 'dst': dst, 'Wq': jax.random.normal(ks[3], (DM, DM), dtype=jnp.float32) * s, 'Wk': jax.random.normal(ks[4], (DM, DM), dtype=jnp.float32) * s, 'Wv': jax.random.normal(ks[5], (DM, DM), dtype=jnp.float32) * s, 'Wo': jax.random.normal(ks[6], (DM, DM), dtype=jnp.float32) * s, 'ln1_g': jnp.ones((DM,), jnp.float32), 'ln1_b': jnp.zeros((DM,), jnp.float32), 'ln2_g': jnp.ones((DM,), jnp.float32), 'ln2_b': jnp.zeros((DM,), jnp.float32), 'W1': jax.random.normal(ks[7], (DM, DFF), dtype=jnp.float32) * s, 'b1': jnp.zeros((DFF,), jnp.float32), 'W2': jax.random.normal(ks[8], (DFF, DM), dtype=jnp.float32) * s, 'b2': jnp.zeros((DM,), jnp.float32)}
    _L1_gnn_all = _L1_gnn_setup()
    _L1_gnn_in = {k: v for k, v in _L1_gnn_all.items() if k in ('Wq', 'Wk', 'Wv', 'Wo', 'ln1_g', 'ln1_b', 'ln2_g', 'ln2_b', 'W1', 'b1', 'W2', 'b2')}
    del _L1_gnn_all

    def _L1_mix_setup():
        import jax, jax.numpy as jnp
        import numpy as np
        import math
        B, N, DIM = (4, 512, 512)
        HEADS, DH, NBF = (8, 64, 256)
        MLP_H = DIM * 2

        def layernorm(x, g, b, eps=1e-05):
            mu = jnp.mean(x, axis=-1, keepdims=True)
            var = jnp.mean(jnp.square(x - mu), axis=-1, keepdims=True)
            return (x - mu) * jax.lax.rsqrt(var + eps) * g + b

        def softmax_kernel(x, pmat):
            xp = jnp.einsum('bhnd,df->bhnf', x, pmat)
            xp = xp - jnp.max(xp, axis=-1, keepdims=True)
            return jnp.exp(xp) / math.sqrt(pmat.shape[-1])
        key = jax.random.key(seed)
        ks = jax.random.split(key, 8)
        s = lambda d: 1.0 / math.sqrt(d)
        return {'x': jax.random.normal(ks[0], (B, N, DIM), jnp.float32), 'Wqkv': jax.random.normal(ks[1], (DIM, 3 * HEADS * DH), jnp.float32) * s(DIM), 'bqkv': jnp.zeros((3 * HEADS * DH,), jnp.float32), 'Pmat': jax.random.normal(ks[2], (DH, NBF), jnp.float32), 'Wproj': jax.random.normal(ks[3], (HEADS * DH, DIM), jnp.float32) * s(HEADS * DH), 'bproj': jnp.zeros((DIM,), jnp.float32), 'W1': jax.random.normal(ks[4], (DIM, MLP_H), jnp.float32) * s(DIM), 'b1': jnp.zeros((MLP_H,), jnp.float32), 'W2': jax.random.normal(ks[5], (MLP_H, DIM), jnp.float32) * s(MLP_H), 'b2': jnp.zeros((DIM,), jnp.float32), 'g1': jnp.ones((DIM,), jnp.float32), 'be1': jnp.zeros((DIM,), jnp.float32), 'g2': jnp.ones((DIM,), jnp.float32), 'be2': jnp.zeros((DIM,), jnp.float32)}
    _L1_mix_all = _L1_mix_setup()
    _L1_mix_in = {k: v for k, v in _L1_mix_all.items() if k in ('Wqkv', 'bqkv', 'Pmat', 'Wproj', 'bproj', 'W1', 'b1', 'W2', 'b2', 'g1', 'be1', 'g2', 'be2')}
    del _L1_mix_all

    def _L1_ffn_setup():
        import jax, jax.numpy as jnp
        import numpy as np
        HEADS = 8
        DIM_HEAD = 64
        TOPK = 2
        B, N, D = (8, 1024, 512)
        L = 4
        E = 8
        H = 256
        INNER = HEADS * DIM_HEAD

        def _ln(x, w, b, eps=1e-05):
            m = jnp.mean(x, -1, keepdims=True)
            v = jnp.var(x, -1, keepdims=True)
            return (x - m) * jax.lax.rsqrt(v + eps) * w + b

        def _attn(x, qkv_w, out_w, out_b):
            b, n, _ = x.shape
            q, k, v = jnp.split(x @ qkv_w, 3, axis=-1)
            sh = lambda t: t.reshape(b, n, HEADS, DIM_HEAD).transpose(0, 2, 1, 3)
            q, k, v = (sh(q), sh(k), sh(v))
            dots = jnp.einsum('bhid,bhjd->bhij', q, k) * DIM_HEAD ** (-0.5)
            a = jax.nn.softmax(dots, axis=-1)
            o = jnp.einsum('bhij,bhjd->bhid', a, v)
            o = o.transpose(0, 2, 1, 3).reshape(b, n, -1)
            return o @ out_w + out_b

        def _moe(xf, wg, w1, b1, w2, b2):
            T = xf.shape[0]
            logits = xf @ wg
            top_v, top_i = jax.lax.top_k(logits, TOPK)
            gv = jax.nn.softmax(top_v, axis=-1)
            gates = jnp.zeros_like(logits).at[jnp.arange(T)[:, None], top_i].set(gv)
            y = jnp.zeros_like(xf)
            for e in range(w1.shape[0]):
                h = jax.nn.gelu(xf @ w1[e] + b1[e], approximate=False)
                y = y + gates[:, e:e + 1] * (h @ w2[e] + b2[e])
            return y
        key = jax.random.key(seed)
        ks = jax.random.split(key, 8)
        s = 0.02
        return {'x': jax.random.normal(ks[0], (B, N, D), jnp.float32), 'ln1_w': jnp.ones((L, D), jnp.float32), 'ln1_b': jnp.zeros((L, D), jnp.float32), 'qkv_w': jax.random.normal(ks[1], (L, D, 3 * INNER), jnp.float32) * s, 'out_w': jax.random.normal(ks[2], (L, INNER, D), jnp.float32) * s, 'out_b': jnp.zeros((L, D), jnp.float32), 'ln2_w': jnp.ones((L, D), jnp.float32), 'ln2_b': jnp.zeros((L, D), jnp.float32), 'w_gate': jax.random.normal(ks[3], (L, D, E), jnp.float32) * s, 'ew1': jax.random.normal(ks[4], (L, E, D, H), jnp.float32) * s, 'eb1': jnp.zeros((L, E, H), jnp.float32), 'ew2': jax.random.normal(ks[5], (L, E, H, D), jnp.float32) * s, 'eb2': jnp.zeros((L, E, D), jnp.float32), 'fln_w': jnp.ones((D,), jnp.float32), 'fln_b': jnp.zeros((D,), jnp.float32)}
    _L1_ffn_all = _L1_ffn_setup()
    _L1_ffn_in = {k: v for k, v in _L1_ffn_all.items() if k in ('ln1_w', 'ln1_b', 'qkv_w', 'out_w', 'out_b', 'ln2_w', 'ln2_b', 'w_gate', 'ew1', 'eb1', 'ew2', 'eb2', 'fln_w', 'fln_b')}
    del _L1_ffn_all
    return {'x': x, 'src': src, 'dst': dst, 'edge_attr_4': edge_attr_4, 'edge_attr_8': edge_attr_8, 'L0_gnn_W_up0': _L0_gnn_in['W_up0'], 'L0_gnn_W_up1': _L0_gnn_in['W_up1'], 'L0_gnn_W_mlp1': _L0_gnn_in['W_mlp1'], 'L0_gnn_W_mlp2': _L0_gnn_in['W_mlp2'], 'L0_gnn_W_mlp3': _L0_gnn_in['W_mlp3'], 'L0_gnn_W_mlp4': _L0_gnn_in['W_mlp4'], 'L0_gnn_W_out0': _L0_gnn_in['W_out0'], 'L0_gnn_W_out1': _L0_gnn_in['W_out1'], 'L0_mix_W_in': _L0_mix_in['W_in'], 'L0_mix_b_in': _L0_mix_in['b_in'], 'L0_mix_W_q': _L0_mix_in['W_q'], 'L0_mix_W_k': _L0_mix_in['W_k'], 'L0_mix_W_v': _L0_mix_in['W_v'], 'L0_mix_W_out': _L0_mix_in['W_out'], 'L0_mix_b_out': _L0_mix_in['b_out'], 'L0_ffn_gate_w': _L0_ffn_in['gate_w'], 'L0_ffn_experts': _L0_ffn_in['experts'], 'L1_gnn_Wq': _L1_gnn_in['Wq'], 'L1_gnn_Wk': _L1_gnn_in['Wk'], 'L1_gnn_Wv': _L1_gnn_in['Wv'], 'L1_gnn_Wo': _L1_gnn_in['Wo'], 'L1_gnn_ln1_g': _L1_gnn_in['ln1_g'], 'L1_gnn_ln1_b': _L1_gnn_in['ln1_b'], 'L1_gnn_ln2_g': _L1_gnn_in['ln2_g'], 'L1_gnn_ln2_b': _L1_gnn_in['ln2_b'], 'L1_gnn_W1': _L1_gnn_in['W1'], 'L1_gnn_b1': _L1_gnn_in['b1'], 'L1_gnn_W2': _L1_gnn_in['W2'], 'L1_gnn_b2': _L1_gnn_in['b2'], 'L1_mix_Wqkv': _L1_mix_in['Wqkv'], 'L1_mix_bqkv': _L1_mix_in['bqkv'], 'L1_mix_Pmat': _L1_mix_in['Pmat'], 'L1_mix_Wproj': _L1_mix_in['Wproj'], 'L1_mix_bproj': _L1_mix_in['bproj'], 'L1_mix_W1': _L1_mix_in['W1'], 'L1_mix_b1': _L1_mix_in['b1'], 'L1_mix_W2': _L1_mix_in['W2'], 'L1_mix_b2': _L1_mix_in['b2'], 'L1_mix_g1': _L1_mix_in['g1'], 'L1_mix_be1': _L1_mix_in['be1'], 'L1_mix_g2': _L1_mix_in['g2'], 'L1_mix_be2': _L1_mix_in['be2'], 'L1_ffn_ln1_w': _L1_ffn_in['ln1_w'], 'L1_ffn_ln1_b': _L1_ffn_in['ln1_b'], 'L1_ffn_qkv_w': _L1_ffn_in['qkv_w'], 'L1_ffn_out_w': _L1_ffn_in['out_w'], 'L1_ffn_out_b': _L1_ffn_in['out_b'], 'L1_ffn_ln2_w': _L1_ffn_in['ln2_w'], 'L1_ffn_ln2_b': _L1_ffn_in['ln2_b'], 'L1_ffn_w_gate': _L1_ffn_in['w_gate'], 'L1_ffn_ew1': _L1_ffn_in['ew1'], 'L1_ffn_eb1': _L1_ffn_in['eb1'], 'L1_ffn_ew2': _L1_ffn_in['ew2'], 'L1_ffn_eb2': _L1_ffn_in['eb2'], 'L1_ffn_fln_w': _L1_ffn_in['fln_w'], 'L1_ffn_fln_b': _L1_ffn_in['fln_b']}

def reference(x, src, dst, edge_attr_4, edge_attr_8, L0_gnn_W_up0, L0_gnn_W_up1, L0_gnn_W_mlp1, L0_gnn_W_mlp2, L0_gnn_W_mlp3, L0_gnn_W_mlp4, L0_gnn_W_out0, L0_gnn_W_out1, L0_mix_W_in, L0_mix_b_in, L0_mix_W_q, L0_mix_W_k, L0_mix_W_v, L0_mix_W_out, L0_mix_b_out, L0_ffn_gate_w, L0_ffn_experts, L1_gnn_Wq, L1_gnn_Wk, L1_gnn_Wv, L1_gnn_Wo, L1_gnn_ln1_g, L1_gnn_ln1_b, L1_gnn_ln2_g, L1_gnn_ln2_b, L1_gnn_W1, L1_gnn_b1, L1_gnn_W2, L1_gnn_b2, L1_mix_Wqkv, L1_mix_bqkv, L1_mix_Pmat, L1_mix_Wproj, L1_mix_bproj, L1_mix_W1, L1_mix_b1, L1_mix_W2, L1_mix_b2, L1_mix_g1, L1_mix_be1, L1_mix_g2, L1_mix_be2, L1_ffn_ln1_w, L1_ffn_ln1_b, L1_ffn_qkv_w, L1_ffn_out_w, L1_ffn_out_b, L1_ffn_ln2_w, L1_ffn_ln2_b, L1_ffn_w_gate, L1_ffn_ew1, L1_ffn_eb1, L1_ffn_ew2, L1_ffn_eb2, L1_ffn_fln_w, L1_ffn_fln_b):
    import jax
    import jax.numpy as jnp

    def _L0_gnn_ref(node_feats, edge_attrs, edge_feats, edge_index, W_up0, W_up1, W_mlp1, W_mlp2, W_mlp3, W_mlp4, W_out0, W_out1):
        import jax, jax.numpy as jnp
        import numpy as np
        MUL = 128
        N_NODES = 1250
        N_EDGES = 20000
        R_BASIS = 8
        HIDDEN = 64
        W_NUMEL = 4 * MUL
        SQRT3 = 3.0 ** 0.5
        SILU_2MOM = 1.679177
        AVG_NUM_NEIGHBORS = 10.0

        def _lin_irreps(x0, x1, W0, W1):
            y0 = x0 @ W0 / jnp.sqrt(jnp.float32(W0.shape[0]))
            y1 = jnp.einsum('num,uv->nvm', x1, W1) / jnp.sqrt(jnp.float32(W1.shape[0]))
            return (y0, y1)

        def _forward(node_feats, edge_attrs, edge_feats, edge_index, W_up0, W_up1, W_mlp1, W_mlp2, W_mlp3, W_mlp4, W_out0, W_out1):
            num_nodes = node_feats.shape[0]
            sender, receiver = (edge_index[0], edge_index[1])
            x0 = node_feats[:, :MUL]
            x1 = node_feats[:, MUL:].reshape(num_nodes, MUL, 3)
            x0, x1 = _lin_irreps(x0, x1, W_up0, W_up1)
            h = edge_feats
            for W in (W_mlp1, W_mlp2, W_mlp3):
                h = SILU_2MOM * jax.nn.silu(h @ W / jnp.sqrt(jnp.float32(W.shape[0])))
            tpw = h @ W_mlp4 / jnp.sqrt(jnp.float32(W_mlp4.shape[0]))
            w1, w2, w3, w4 = jnp.split(tpw, 4, axis=-1)
            s0 = x0[sender]
            s1 = x1[sender]
            y0 = edge_attrs[:, 0:1]
            y1 = edge_attrs[:, 1:4]
            p1 = w1 * s0 * y0
            p2 = (w2 * s0)[:, :, None] * y1[:, None, :]
            p3 = w3[:, :, None] * s1 * y0[:, None, :]
            p4 = w4 * jnp.einsum('eum,em->eu', s1, y1) / SQRT3
            m0 = jnp.concatenate([p1, p4], axis=-1)
            m1 = jnp.concatenate([p2, p3], axis=1)
            msg0 = jax.ops.segment_sum(m0, receiver, num_segments=num_nodes)
            msg1 = jax.ops.segment_sum(m1, receiver, num_segments=num_nodes)
            o0, o1 = _lin_irreps(msg0, msg1, W_out0, W_out1)
            out = jnp.concatenate([o0, o1.reshape(num_nodes, 3 * MUL)], axis=-1)
            return out / AVG_NUM_NEIGHBORS
        return _forward(node_feats, edge_attrs, edge_feats, edge_index, W_up0, W_up1, W_mlp1, W_mlp2, W_mlp3, W_mlp4, W_out0, W_out1)

    def _L0_mix_ref(x, W_in, b_in, W_q, W_k, W_v, W_out, b_out):
        import jax, jax.numpy as jnp
        import numpy as np
        DIM = 512
        HEADS = 8
        DIM_HEAD = 64
        KEY_RATIO = 4
        INNER = HEADS * DIM_HEAD
        B, N = (8, 2048)
        Bx, Nx, _ = x.shape
        x_mid = x @ W_in + b_in
        x_mid = x_mid.reshape(Bx, Nx, HEADS, DIM_HEAD).transpose(0, 2, 1, 3)
        q = jnp.einsum('bhnd,dr->bhnr', x_mid, W_q)
        k = jnp.einsum('bhnd,dr->bhnr', x_mid, W_k)
        v = jnp.einsum('bhnd,dc->bhnc', x_mid, W_v)
        q = jax.nn.softmax(q, axis=-1)
        k = jax.nn.softmax(k, axis=-2)
        kv = jnp.einsum('bhnr,bhnc->bhrc', k, v)
        qkv = jnp.einsum('bhnr,bhrc->bhnc', q, kv)
        qkv = qkv.transpose(0, 2, 1, 3).reshape(Bx, Nx, INNER)
        return qkv @ W_out + b_out

    def _L0_ffn_ref(x, gate_w, experts):
        import jax, jax.numpy as jnp
        import numpy as np
        SINKHORN_ITERS = 8
        TEMPERATURE = 1.0
        EPS = 1e-10

        def sinkhorn(gates):
            t = jnp.log(jnp.clip(gates, EPS)) / TEMPERATURE

            def body(t, _):
                t = t - jax.nn.logsumexp(t, axis=-2, keepdims=True)
                t = t - jax.nn.logsumexp(t, axis=-1, keepdims=True)
                return (t, None)
            t, _ = jax.lax.scan(body, t, None, length=SINKHORN_ITERS)
            return jnp.exp(t)
        b, n, d = x.shape
        h = gate_w.shape[0]
        e = experts.shape[0]
        N = b * n
        m = n // e
        x4 = x[:, None]
        gates = jnp.einsum('bhnd,hde->bhne', x4, gate_w)
        xf = jnp.transpose(x4, (1, 0, 2, 3)).reshape(h, N, d)
        gf = jnp.transpose(gates, (1, 0, 2, 3)).reshape(h, N, e)
        cg = sinkhorn(gf)
        vals, idx = jax.lax.top_k(jnp.transpose(cg, (0, 2, 1)), m)
        gate_values = (vals > 0.5).astype(x.dtype)
        gate_values = jnp.transpose(gate_values, (0, 2, 1))
        idx = jnp.transpose(idx, (0, 2, 1))
        routed = xf[jnp.arange(h)[:, None, None], idx]
        outputs = jnp.einsum('hmei,eio->hmeo', routed, experts)
        outputs = outputs * gate_values[..., None]
        o_dim = outputs.shape[-1]
        src = outputs.reshape(h, m * e, o_dim)
        idx_flat = idx.reshape(h, m * e)

        def combine(idxf, srcf):
            s = jnp.zeros((N, o_dim), srcf.dtype).at[idxf].add(srcf)
            c = jnp.zeros((N,), srcf.dtype).at[idxf].add(1.0)
            return s / (c + 1.0)[:, None]
        out = jax.vmap(combine)(idx_flat, src)
        out = out.reshape(h, b, n, o_dim)
        out = jnp.transpose(out, (1, 0, 2, 3))[:, 0]
        return out

    def _L1_gnn_ref(h, src, dst, Wq, Wk, Wv, Wo, ln1_g, ln1_b, ln2_g, ln2_b, W1, b1, W2, b2):
        import jax, jax.numpy as jnp
        import numpy as np
        N, E, DM, H, DFF = (2500, 80000, 512, 8, 256)
        DK = DM // H

        def _layernorm(x, g, b, eps=1e-05):
            mu = jnp.mean(x, axis=-1, keepdims=True)
            var = jnp.mean(jnp.square(x - mu), axis=-1, keepdims=True)
            return (x - mu) * jax.lax.rsqrt(var + eps) * g + b
        n = h.shape[0]
        q = (h @ Wq).reshape(n, H, DK)
        k = (h @ Wk).reshape(n, H, DK)
        v = (h @ Wv).reshape(n, H, DK)
        e = jnp.einsum('ehd,ehd->eh', k[src], q[dst]) / np.sqrt(DK).astype(np.float32)
        m = jax.ops.segment_max(e, dst, num_segments=n)
        ex = jnp.exp(e - m[dst])
        z = jax.ops.segment_sum(ex, dst, num_segments=n)
        attn = ex / z[dst]
        a = jax.ops.segment_sum(attn[:, :, None] * v[src], dst, num_segments=n)
        a = a.reshape(n, DM)
        o = a @ Wo
        x = _layernorm(h + o, ln1_g, ln1_b)
        f = jax.nn.relu(x @ W1 + b1) @ W2 + b2
        return _layernorm(x + f, ln2_g, ln2_b)

    def _L1_mix_ref(x, Wqkv, bqkv, Pmat, Wproj, bproj, W1, b1, W2, b2, g1, be1, g2, be2):
        import jax, jax.numpy as jnp
        import numpy as np
        import math
        B, N, DIM = (4, 512, 512)
        HEADS, DH, NBF = (8, 64, 256)
        MLP_H = DIM * 2

        def layernorm(x, g, b, eps=1e-05):
            mu = jnp.mean(x, axis=-1, keepdims=True)
            var = jnp.mean(jnp.square(x - mu), axis=-1, keepdims=True)
            return (x - mu) * jax.lax.rsqrt(var + eps) * g + b

        def softmax_kernel(x, pmat):
            xp = jnp.einsum('bhnd,df->bhnf', x, pmat)
            xp = xp - jnp.max(xp, axis=-1, keepdims=True)
            return jnp.exp(xp) / math.sqrt(pmat.shape[-1])
        b, n, d = x.shape
        h = layernorm(x, g1, be1)
        qkv = h @ Wqkv + bqkv
        q, k, v = jnp.split(qkv, 3, axis=-1)
        to_heads = lambda t: t.reshape(b, n, HEADS, DH).transpose(0, 2, 1, 3)
        q, k, v = (to_heads(q), to_heads(k), to_heads(v))
        q_prime = softmax_kernel(q, Pmat)
        k_prime = softmax_kernel(k, Pmat)
        kv = jnp.einsum('bhnf,bhne->bhfe', k_prime, v)
        k_sum = jnp.sum(k_prime, axis=2) + 1e-06
        z = 1.0 / jnp.einsum('bhnf,bhf->bhn', q_prime, k_sum)[..., None]
        attn = jnp.einsum('bhnf,bhfe->bhne', q_prime, kv) * z
        attn = attn.transpose(0, 2, 1, 3).reshape(b, n, HEADS * DH)
        x = x + attn @ Wproj + bproj
        h2 = layernorm(x, g2, be2)
        mlp = jax.nn.gelu(h2 @ W1 + b1, approximate=False) @ W2 + b2
        return x + mlp

    def _L1_ffn_ref(x, ln1_w, ln1_b, qkv_w, out_w, out_b, ln2_w, ln2_b, w_gate, ew1, eb1, ew2, eb2, fln_w, fln_b):
        import jax, jax.numpy as jnp
        import numpy as np
        HEADS = 8
        DIM_HEAD = 64
        TOPK = 2
        B, N, D = (8, 1024, 512)
        L = 4
        E = 8
        H = 256
        INNER = HEADS * DIM_HEAD

        def _ln(x, w, b, eps=1e-05):
            m = jnp.mean(x, -1, keepdims=True)
            v = jnp.var(x, -1, keepdims=True)
            return (x - m) * jax.lax.rsqrt(v + eps) * w + b

        def _attn(x, qkv_w, out_w, out_b):
            b, n, _ = x.shape
            q, k, v = jnp.split(x @ qkv_w, 3, axis=-1)
            sh = lambda t: t.reshape(b, n, HEADS, DIM_HEAD).transpose(0, 2, 1, 3)
            q, k, v = (sh(q), sh(k), sh(v))
            dots = jnp.einsum('bhid,bhjd->bhij', q, k) * DIM_HEAD ** (-0.5)
            a = jax.nn.softmax(dots, axis=-1)
            o = jnp.einsum('bhij,bhjd->bhid', a, v)
            o = o.transpose(0, 2, 1, 3).reshape(b, n, -1)
            return o @ out_w + out_b

        def _moe(xf, wg, w1, b1, w2, b2):
            T = xf.shape[0]
            logits = xf @ wg
            top_v, top_i = jax.lax.top_k(logits, TOPK)
            gv = jax.nn.softmax(top_v, axis=-1)
            gates = jnp.zeros_like(logits).at[jnp.arange(T)[:, None], top_i].set(gv)
            y = jnp.zeros_like(xf)
            for e in range(w1.shape[0]):
                h = jax.nn.gelu(xf @ w1[e] + b1[e], approximate=False)
                y = y + gates[:, e:e + 1] * (h @ w2[e] + b2[e])
            return y
        b, n, d = x.shape
        depth = qkv_w.shape[0]
        for l in range(depth):
            x = x + _attn(_ln(x, ln1_w[l], ln1_b[l]), qkv_w[l], out_w[l], out_b[l])
            xf = _ln(x, ln2_w[l], ln2_b[l]).reshape(-1, d)
            x = x + _moe(xf, w_gate[l], ew1[l], eb1[l], ew2[l], eb2[l]).reshape(b, n, d)
        return _ln(x, fln_w, fln_b)
    edge_index = jnp.stack([src, dst])
    xn = _layernorm(x, axis=-1)
    x = x + _L0_gnn_ref(xn, edge_attr_4, edge_attr_8, edge_index, L0_gnn_W_up0, L0_gnn_W_up1, L0_gnn_W_mlp1, L0_gnn_W_mlp2, L0_gnn_W_mlp3, L0_gnn_W_mlp4, L0_gnn_W_out0, L0_gnn_W_out1) + _L0_mix_ref(xn[None], L0_mix_W_in, L0_mix_b_in, L0_mix_W_q, L0_mix_W_k, L0_mix_W_v, L0_mix_W_out, L0_mix_b_out)[0]
    x = x + _L0_ffn_ref(_layernorm(x, axis=-1)[None], L0_ffn_gate_w, L0_ffn_experts)[0]
    xn = _layernorm(x, axis=-1)
    x = x + _L1_gnn_ref(xn, src, dst, L1_gnn_Wq, L1_gnn_Wk, L1_gnn_Wv, L1_gnn_Wo, L1_gnn_ln1_g, L1_gnn_ln1_b, L1_gnn_ln2_g, L1_gnn_ln2_b, L1_gnn_W1, L1_gnn_b1, L1_gnn_W2, L1_gnn_b2) + _L1_mix_ref(xn[None], L1_mix_Wqkv, L1_mix_bqkv, L1_mix_Pmat, L1_mix_Wproj, L1_mix_bproj, L1_mix_W1, L1_mix_b1, L1_mix_W2, L1_mix_b2, L1_mix_g1, L1_mix_be1, L1_mix_g2, L1_mix_be2)[0]
    x = x + _L1_ffn_ref(_layernorm(x, axis=-1)[None], L1_ffn_ln1_w, L1_ffn_ln1_b, L1_ffn_qkv_w, L1_ffn_out_w, L1_ffn_out_b, L1_ffn_ln2_w, L1_ffn_ln2_b, L1_ffn_w_gate, L1_ffn_ew1, L1_ffn_eb1, L1_ffn_ew2, L1_ffn_eb2, L1_ffn_fln_w, L1_ffn_fln_b)[0]
    return x

_drawn_inputs = setup_inputs


def setup_inputs(seed=0):
    import zlib

    import numpy as np

    out = dict(_drawn_inputs(seed))
    spreads = {'L1_gnn_ln1_g': (1.0, 0.2),
     'L1_gnn_ln1_b': (0.0, 0.1),
     'L1_gnn_ln2_g': (1.0, 0.2),
     'L1_gnn_ln2_b': (0.0, 0.1),
     'L1_gnn_b1': (0.0, 0.8),
     'L1_gnn_b2': (0.0, 0.1),
     'L1_mix_bqkv': (0.0, 0.1),
     'L1_mix_bproj': (0.0, 0.1),
     'L1_mix_b1': (0.0, 0.365),
     'L1_mix_b2': (0.0, 0.1),
     'L1_mix_g1': (1.0, 0.2),
     'L1_mix_be1': (0.0, 0.1),
     'L1_mix_g2': (1.0, 0.2),
     'L1_mix_be2': (0.0, 0.362),
     'L1_ffn_ln1_w': (1.0, 0.6),
     'L1_ffn_ln1_b': (0.0, 0.64),
     'L1_ffn_out_b': (0.0, 0.1),
     'L1_ffn_ln2_w': (1.0, 0.6),
     'L1_ffn_ln2_b': (0.0, 0.566),
     'L1_ffn_eb1': (0.0, 0.8),
     'L1_ffn_eb2': (0.0, 0.1),
     'L1_ffn_fln_w': (1.0, 0.2),
     'L1_ffn_fln_b': (0.0, 0.338)}
    factors = {'L0_mix_W_in': 3.451,
     'L0_mix_W_q': 7.625,
     'L0_mix_W_k': 4.041,
     'L1_gnn_Wq': 8.0,
     'L1_gnn_Wk': 8.0,
     'L1_gnn_Wv': 3.258,
     'L1_gnn_Wo': 3.27}
    for name, (base, spread) in spreads.items():
        noise = np.random.default_rng([zlib.crc32(name.encode()), seed]).standard_normal(out[name].shape)
        drawn = base * np.exp(spread * noise) if base else spread * noise
        out[name] = jnp.asarray(drawn.astype(out[name].dtype))
    for name, factor in factors.items():
        out[name] = (out[name] * factor).astype(out[name].dtype)
    return out
```

```python
from contextlib import ExitStack, contextmanager

import concourse.bass as bass
from concourse import mybir

F32 = mybir.dt.float32
F32R = mybir.dt.float32r
BF16 = mybir.dt.bfloat16
I32 = mybir.dt.int32
U32 = mybir.dt.uint32
ALU = mybir.AluOpType
ACT = mybir.ActivationFunctionType
AX = mybir.AxisListType
RMAX = bass.bass_isa.ReduceOp.max

N, D = 1250, 512
P, T = 125, 10
KB = D // 128
E = 21250
G = 5
SB = E // (P * G)
W = 64
NPAD = N + W
MUL = 128
HID = 64
HEADS, DH = 8, 64
SILU_2MOM = 1.679177
CH = [(0, 500), (500, 500), (1000, 250)]
EPS = 1e-5
BIG = 3.0e38


class Tensors:
    pass


@contextmanager
def phase(nc, *names, drain_pool=True, held=()):
    with ExitStack() as ctx:
        sems = [ctx.enter_context(nc.semaphore(n)) for n in names]
        with nc.Block(no_gpsimd_drain=not drain_pool) as block:
            yield (block, *sems)
        for s in sems:
            nc.sync.sem_clear(s)
        if held:
            nc.gpsimd.dma_reset(range(held[0].num, held[-1].num + 1))
            for s in held:
                nc.gpsimd.sem_clear(s)
        nc.all_engine_barrier()


def sb(nc, ctx, name, shape, dt=F32):
    return ctx.enter_context(nc.sbuf_tensor(name, shape, dt))


def tile(i):
    return slice(i * P, (i + 1) * P)



def load_phase(nc, pairs):
    with phase(nc, "loaded") as (block, loaded):
        @block.sync
        def _(sp):
            for dst, src in pairs:
                sp.dma_start(dst, src).then_inc(loaded, 16)
            sp.wait_ge(loaded, 16 * len(pairs))


def layernorm_phase(nc, m, src, normed, transposed=None, cols=None, gain_col=None, bias_col=None,
                    gain_row=None, bias_row=None, loads=()):
    cols = cols or (lambda ap, k: ap[:, k * 128:(k + 1) * 128])
    with phase(nc, "loaded", "stats", "moments", "spread", "inverse", "centred", "scaled", "ready",
               "turned", "kept") as (block, loaded, stats, moments, spread, inverse, centred, scaled,
                                     ready, turned, kept):
        @block.sync
        def _(sp):
            for dst, s in loads:
                sp.dma_start(dst, s).then_inc(loaded, 16)

        @block.vector
        def _(dve):
            for i in range(T):
                dve.bn_stats(m.bn[:, i, :], src[:, i, :]).then_inc(stats, 1)
            for i in range(T):
                dve.wait_ge(stats, i + 1)
                dve.bn_aggr(m.mv[:, i, :], m.bn[:, i, :]).then_inc(moments, 1)
            dve.wait_ge(spread, 1)
            dve.reciprocal(m.rstd[:, :], m.sd[:, :]).then_inc(inverse, 1)
            dve.wait_ge(inverse, 1)
            for i in range(T):
                if transposed is not None and i >= 2:
                    dve.wait_ge(turned, i - 1)
                out = normed(i) if gain_row is None else m.tmp[:, i % 2, :]
                if gain_row is not None and i >= 2:
                    dve.wait_ge(scaled, i - 1)
                ins = dve.tensor_scalar(out, src[:, i, :], m.mv[:, i, 0:1], m.rstd[:, i:i + 1],
                                        ALU.subtract, ALU.mult)
                if gain_row is None:
                    ins.then_inc(ready, 1)
                    continue
                ins.then_inc(centred, 1)
                dve.wait_ge(centred, i + 1)
                if i == 0:
                    dve.wait_ge(loaded, 16 * len(loads))
                dve.tensor_tensor(m.tmp2[:, i % 2, :], m.tmp[:, i % 2, :], gain_row, ALU.mult).then_inc(scaled, 1)
                dve.wait_ge(scaled, i + 1)
                dve.tensor_tensor(normed(i), m.tmp2[:, i % 2, :], bias_row, ALU.add).then_inc(ready, 1)

        @block.tensor
        def _(pe):
            if transposed is None:
                return
            for i in range(T):
                pe.wait_ge(ready, i + 1)
                if i >= 4:
                    pe.wait_ge(kept, i - 3)
                for k in range(KB):
                    ins = pe.transpose(m.ps[:, i % 4, k * P:(k + 1) * P], cols(normed(i), k), m.ident[0:P, 0:P])
                ins.then_inc(turned, 1)

        @block.scalar
        def _(act):
            act.wait_ge(moments, T)
            act.activation(m.sd[:, :], m.mv[:, :, 1], ACT.Sqrt, bias=m.eps[0:P, 0:1]).then_inc(spread, 1)
            if transposed is None:
                return
            if gain_col is not None:
                act.wait_ge(loaded, 16 * len(loads))
            for i in range(T):
                act.wait_ge(turned, i + 1)
                view = m.ps[:, i % 4, 0:KB * P].rearrange("p (k t) -> p k t", k=KB)
                if gain_col is None:
                    act.activation(transposed[:, :, tile(i)], view, ACT.Copy).then_inc(kept, 1)
                else:
                    for k in range(KB):
                        ins = act.activation(transposed[:, k, tile(i)], view[:, k, :], ACT.Identity,
                                             bias=bias_col[:, k:k + 1], scale=gain_col[:, k:k + 1])
                    ins.then_inc(kept, 1)


def groups_phase(nc, m, n_groups, operands, evac, loads=(), slots=8, stores=None):
    with phase(nc, "loaded", "product", "taken_by_act", "taken_by_dve", "stored") as (
            block, loaded, product, taken_act, taken_dve, stored):
        taken = (taken_act, taken_dve)

        @block.sync
        def _(sp):
            for dst, src in loads:
                sp.dma_start(dst, src).then_inc(loaded, 16)
            if stores is not None:
                count = 0
                for n in range(n_groups):
                    for dst, src in stores(n):
                        sp.wait_ge(taken[n % 2], n // 2 + 1)
                        if n % 2:
                            sp.wait_ge(taken[0], n // 2 + 1)
                        sp.dma_start(dst, src).then_inc(stored, 16)
                        count += 16
                sp.wait_ge(stored, count)

        @block.tensor
        def _(pe):
            if loads:
                pe.wait_ge(loaded, 16 * len(loads))
            for n in range(n_groups):
                if n >= slots:
                    pe.wait_ge(taken[n % 2], (n - slots) // 2 + 1)
                ops = operands(n, m.ps[:, n % slots, :])
                for k, (out, lhsT, rhs) in enumerate(ops):
                    ins = pe.matmul(out, lhsT, rhs, start=k == 0, stop=k == len(ops) - 1, skip_group_check=True)
                ins.then_inc(product, 1)

        @block.scalar
        def _(act):
            if loads:
                act.wait_ge(loaded, 16 * len(loads))
            for n in range(0, n_groups, 2):
                act.wait_ge(product, n + 1)
                evac(n, act, m.ps[:, n % slots, :], True).then_inc(taken[0], 1)

        @block.vector
        def _(dve):
            if loads:
                dve.wait_ge(loaded, 16 * len(loads))
            for n in range(1, n_groups, 2):
                dve.wait_ge(product, n + 1)
                evac(n, dve, m.ps[:, n % slots, :], False).then_inc(taken[1], 1)


def copy_scaled(eng, out, in_, on_act, scale=1.0, bias=None):
    if on_act:
        if bias is None:
            return eng.activation(out, in_, ACT.Copy, scale=scale)
        return eng.activation(out, in_, ACT.Identity, bias=bias, scale=scale)
    if bias is None:
        return eng.tensor_scalar(out, in_, scale, None, ALU.mult)
    return eng.tensor_scalar(out, in_, scale, bias, ALU.mult, ALU.add)


def wview(w):
    return w.rearrange("(k p) f -> p k f", p=128)


def vector_groups_phase(nc, m, n_groups, operands, evac, loads=(), slots=8):
    with phase(nc, "loaded", "product", "taken") as (block, loaded, product, taken):
        @block.sync
        def _(sp):
            for dst, src in loads:
                sp.dma_start(dst, src).then_inc(loaded, 16)

        @block.tensor
        def _(pe):
            if loads:
                pe.wait_ge(loaded, 16 * len(loads))
            for n in range(n_groups):
                if n >= slots:
                    pe.wait_ge(taken, n - slots + 1)
                ops = operands(n, m.ps[:, n % slots, :])
                for k, (out, lhsT, rhs) in enumerate(ops):
                    ins = pe.matmul(out, lhsT, rhs, start=k == 0, stop=k == len(ops) - 1, skip_group_check=True)
                ins.then_inc(product, 1)

        @block.vector
        def _(dve):
            for n in range(n_groups):
                dve.wait_ge(product, n + 1)
                evac(n, dve, m.ps[:, n % slots, :]).then_inc(taken, 1)


def add_row_phase(nc, x, row, scratch, src):
    with phase(nc, "loaded", "added") as (block, loaded, added):
        @block.sync
        def _(sp):
            sp.dma_start(scratch, row).then_inc(loaded, 16)

        @block.vector
        def _(dve):
            dve.wait_ge(loaded, 16)
            for i in range(T):
                dve.tensor_tensor(x[:, i, :], src[:, i, :], scratch, ALU.add).then_inc(added, 1)


def spread_row(v, parts=P):
    return v.rearrange("(a n) -> a n", a=1).to_broadcast([parts, v.shape[0]])



def edge_mlp_phase(nc, m, ctx0, ef_t, w1, w2, w3, h3):
    CE = 425
    NCH = E // CE
    with ExitStack() as ctx:
        w1s = sb(nc, ctx, "mlp_w1", [128, 128])
        w2s = sb(nc, ctx, "mlp_w2", [128, 128])
        w3s = sb(nc, ctx, "mlp_w3", [128, 128])
        ef = sb(nc, ctx, "mlp_in", [128, 2, CE])
        ha = sb(nc, ctx, "mlp_h", [128, 2, 2, CE])
        ho = sb(nc, ctx, "mlp_out", [HID, 2, CE])
        with phase(nc, "zeroed", "weights", "in_a", "in_b", "mm_a", "mm_b", "act_a", "act_b", "out_a", "out_b") as (
                block, zeroed, weights, in_a, in_b, mm_a, mm_b, act_a, act_b, out_a, out_b):
            arrived, mm, acted, stored = (in_a, in_b), (mm_a, mm_b), (act_a, act_b), (out_a, out_b)

            @block.sync
            def _(sp):
                sp.wait_ge(zeroed, 5)
                for w, dram in ((w1s, w1), (w2s, w2), (w3s, w3)):
                    sp.dma_start(w[0:dram.shape[0], 0:HID], dram).then_inc(weights, 16)
                for c in range(2):
                    sp.dma_start(ef[0:8, c, :], ef_t[:, c * CE:(c + 1) * CE]).then_inc(arrived[c], 16)
                with sp.Fori(0, NCH // 2 - 1) as it:
                    for c in range(2):
                        sp.wait_ge(mm[c], 3 * it + 1)
                        sp.dma_start(ef[0:8, c, :], ef_t[:, bass.ds((2 * it + 2 + c) * CE, CE)]).then_inc(arrived[c], 16)

            @block.tensor
            def _(pe):
                pe.wait_ge(weights, 48)
                pe.wait_ge(zeroed, 5)
                with pe.Fori(0, NCH // 2) as it:
                    for layer, w in enumerate((w1s, w2s, w3s)):
                        for c in range(2):
                            if layer == 0:
                                pe.wait_ge(arrived[c], 16 * it + 16)
                                rhs = ef[:, c, :]
                            else:
                                pe.wait_ge(acted[c], 3 * it + layer)
                                rhs = ha[:, c, layer - 1, :]
                            pe.matmul(m.ps[:, 4 * c + layer, 0:CE], w[:, :], rhs, start=True,
                                      stop=True).then_inc(mm[c], 1)

            @block.vector
            def _(dve):
                for unfilled in (w1s[:, :], w2s[:, :], w3s[:, :], ef[:, :, :], ha[HID:128, :, :, :]):
                    dve.memset(unfilled, 0.0).then_inc(zeroed, 1)

            @block.scalar
            def _(act):
                scales = (8 ** -0.5, SILU_2MOM * HID ** -0.5, SILU_2MOM * HID ** -0.5)
                for c in range(2):
                    act.sem_inc(stored[c], 16)
                with act.Fori(0, NCH // 2) as it:
                    for layer in range(3):
                        for c in range(2):
                            act.wait_ge(mm[c], 3 * it + layer + 1)
                            if layer == 2:
                                act.wait_ge(stored[c], 16 * it + 16)
                            out = ho[:, c, :] if layer == 2 else ha[0:HID, c, layer, :]
                            act.activation(out, m.ps[0:HID, 4 * c + layer, 0:CE], ACT.Silu,
                                           scale=scales[layer]).then_inc(acted[c], 1)
                    for c in range(2):
                        act.wait_ge(acted[c], 3 * it + 3)
                        act.dma_start(h3[:, bass.ds((2 * it + c) * CE, CE)], ho[:, c, :]).then_inc(stored[c], 16)
                for c in range(2):
                    act.wait_ge(stored[c], 16 * (NCH // 2) + 16)


def edge_base_phase(nc, m, ctx, src_l, dst_l, ea4_l):
    t = sb
    m.src_i = t(nc, ctx, "src_i", [P, SB + 1, G], I32)
    m.dst_i = t(nc, ctx, "dst_i", [P, SB, G], I32)
    m.src_f = t(nc, ctx, "src_f", [P, SB, G])
    m.dst_f = t(nc, ctx, "dst_f", [P, SB, G])
    m.dst_rel = t(nc, ctx, "dst_rel", [P, SB, G])
    m.ea4 = t(nc, ctx, "ea4", [P, SB, G, 4])
    m.base_f = t(nc, ctx, "base_f", [P, SB])
    m.base_i = t(nc, ctx, "base_i", [P, SB], I32)
    lo = t(nc, ctx, "lo", [P, SB])
    hi = t(nc, ctx, "hi", [P, SB])
    lo_all = t(nc, ctx, "lo_all", [P, SB])
    hi_all = t(nc, ctx, "hi_all", [P, SB])
    span = t(nc, ctx, "span", [P, SB])
    widest = t(nc, ctx, "widest", [P, 1])
    m.wide = t(nc, ctx, "wide", [P, 1], I32)
    with phase(nc, "loaded", "chain", "reduced") as (block, loaded, chain, reduced):
        @block.sync
        def _(sp):
            sp.dma_start(m.src_i[:, 0:SB, :], src_l).then_inc(loaded, 16)
            sp.dma_start(m.dst_i[:, :, :], dst_l).then_inc(loaded, 16)
            sp.dma_start(m.ea4[:, :, :, :], ea4_l).then_inc(loaded, 16)

        @block.gpsimd
        def _(pool):
            pool.wait_ge(chain, 5)
            pool.partition_all_reduce(lo_all[:, :], lo[:, :], P, RMAX).then_inc(reduced, 1)
            pool.partition_all_reduce(hi_all[:, :], hi[:, :], P, RMAX).then_inc(reduced, 1)

        @block.vector
        def _(dve):
            dve.memset(m.src_i[:, SB, :], 0)
            dve.wait_ge(loaded, 48)
            dve.tensor_copy(m.src_f[:, :, :], m.src_i[:, 0:SB, :]).then_inc(chain, 1)
            dve.tensor_copy(m.dst_f[:, :, :], m.dst_i[:, :, :]).then_inc(chain, 1)
            dve.wait_ge(chain, 2)
            dve.tensor_reduce(span[:, :], m.dst_f[:, :, :], AX.X, ALU.min).then_inc(chain, 1)
            dve.tensor_reduce(hi[:, :], m.dst_f[:, :, :], AX.X, ALU.max).then_inc(chain, 1)
            dve.wait_ge(chain, 4)
            dve.tensor_scalar(lo[:, :], span[:, :], -1.0, None, ALU.mult).then_inc(chain, 1)
            dve.wait_ge(reduced, 2)
            dve.tensor_scalar(m.base_f[:, :], lo_all[:, :], -1.0, None, ALU.mult).then_inc(chain, 1)
            dve.tensor_tensor(span[:, :], hi_all[:, :], lo_all[:, :], ALU.add).then_inc(chain, 1)
            dve.wait_ge(chain, 7)
            dve.tensor_copy(m.base_i[:, :], m.base_f[:, :]).then_inc(chain, 1)
            dve.tensor_reduce(widest[:, :], span[:, :], AX.X, ALU.max).then_inc(chain, 1)
            dve.wait_ge(chain, 9)
            dve.tensor_scalar(m.wide[:, :], widest[:, :], float(W), None, ALU.is_ge).then_inc(chain, 1)


def edge_sum_phase(nc, m, b, h3, xup):
    NI, U, AHEAD = SB // 2, 2 * G, 2
    done = lambda it, u: U * it + u + 1 + AHEAD
    free = lambda it, u: U * it + u - 1 + AHEAD
    gathered = m.gathered
    with phase(nc, "rel", "turn", "h_a", "h_b", "index", "even_senders", "odd_senders", "path", "window", "weighed", "prod",
               "seg", "counted", "flushed", held=gathered) as (
            block, rel, turn, h_a, h_b, index, even_senders, odd_senders, path, window, weighed, prod, seg, counted, flushed):
        h_in = (h_a, h_b)

        @block.sync
        def _(sp):
            for c in range(2):
                sp.dma_start(b.h3[0:HID, c, :], h3[:, c * 625:(c + 1) * 625]).then_inc(h_in[c], 16)
            with sp.Fori(0, NI - 1) as it:
                for c in range(2):
                    sp.wait_ge(path, U * it + G * (c + 1))
                    sp.dma_start(b.h3[0:HID, c, :], h3[:, bass.ds((2 * it + 2 + c) * 625, 625)]).then_inc(h_in[c], 16)

        @block.gpsimd
        def _(pool):
            def gather(u):
                pool.indirect_dma_start(b.rows[:, u, :], None, xup,
                                        bass.IndirectOffsetOnAxis(ap=b.idx[:, u // G, u % G:u % G + 1].bitcast(U32), axis=0)
                                        ).then_inc(gathered[u], 16)

            def senders(it, u):
                pool.wait_ge(counted, free(it, u))
                pool.sem_inc(turn, 1)
                pool.tensor_scalar(b.hot_src[:, 0, 0:N], m.iota[0:P, 0:N], b.sender[:, u // G, u % G:u % G + 1], None,
                                   ALU.is_equal).then_inc(even_senders, 1)

            flat = "p a g -> p (a g)"
            pool.sem_inc(even_senders, AHEAD)
            pool.tensor_copy(b.idx[:, 0, :], m.src_i[:, 0:1, :].rearrange(flat)).then_inc(index, 1)
            pool.wait_ge(index, 1)
            for g in range(G):
                gather(g)
            with pool.Fori(0, NI) as it:
                for c in (0, 1):
                    pool.wait_ge(even_senders, G * it + 3 * c + AHEAD)
                    pool.tensor_copy(b.sender[:, c, :], m.src_f[:, bass.ds(2 * it + c, 1), :].rearrange(flat)).then_inc(index, 1)
                    pool.wait_ge(prod, done(it, G * c - 1))
                    other, ahead = (1, 1) if c == 0 else (0, 2)
                    pool.tensor_copy(b.idx[:, other, :], m.src_i[:, bass.ds(2 * it + ahead, 1), :].rearrange(flat)).then_inc(index, 1)
                    pool.wait_ge(index, 4 * it + 2 * c + 3)
                    pool.sem_inc(turn, 1)
                    for g in range(G):
                        if (G * c + g) % 2 == 0:
                            senders(it, G * c + g)
                        gather(G * other + g)
            for g in range(U):
                pool.wait_ge(gathered[g], 16 * (NI + (1 if g < G else 0)))

        @block.tensor
        def _(pe):
            def segment(it, u):
                c, first, last = u // G, u % G == 0, u % G == G - 1
                ps = m.ps[:, 2 + c, :]
                pr, sy = b.prod[:, u % 2, :], b.sy[:, u % 2, :]

                def add(out, messages, windows, start=False):
                    return pe.matmul(out, messages, windows, start=start, stop=last, skip_group_check=True)
                if first:
                    pe.wait_ge(flushed, 2 * it + c - 1 + AHEAD)
                pe.wait_ge(weighed, done(it, u))
                pe.wait_ge(prod, done(it, u))
                add(ps[:, 0:3 * W], pr[:, 128:256], sy[:, 0:3 * W], start=first)
                add(ps[:, 3 * W:4 * W], pr[:, 0:128], sy[:, 3 * W:4 * W])
                for k in range(3):
                    add(ps[:, 4 * W:5 * W], pr[:, 640 + 128 * k:768 + 128 * k], sy[:, k * W:(k + 1) * W])
                for k in range(3):
                    ins = add(ps[:, (5 + k) * W:(6 + k) * W], pr[:, 256 + 128 * k:384 + 128 * k], sy[:, 3 * W:4 * W])
                ins.then_inc(seg, 1)
                if u % 2 == 0:
                    pe.wait_ge(even_senders, G * it + u // 2 + 1 + AHEAD)
                else:
                    pe.wait_ge(odd_senders, G * it + u // 2 + 1)
                for j in range(T):
                    ins = pe.matmul(m.ps[:, 4 + 2 * c + j // 5, (j % 5) * W:(j % 5 + 1) * W], b.hot_src[:, u % 2, j * P:j * P + 128],
                                    b.hot[:, u % 2, :], start=first and j % 5 == 0, stop=last, skip_group_check=True)
                ins.then_inc(counted, 1)

            pe.sem_inc(seg, AHEAD)
            pe.sem_inc(counted, AHEAD)
            with pe.Fori(0, NI) as it:
                for u in range(U):
                    if u % G == 0:
                        pe.wait_ge(h_in[u // G], 16 * it + 16)
                    pe.wait_ge(prod, free(it, u))
                    pe.matmul(m.ps[0:P, u % 2, :], b.h3[:, u // G, (u % G) * P:(u % G + 1) * P], b.w4[:, :], start=True,
                              stop=True).then_inc(path, 1)
                    if u >= 1:
                        segment(it, u - 1)
                segment(it, U - 1)

        @block.scalar
        def _(act):
            act.sem_inc(weighed, AHEAD)
            with act.Fori(0, NI) as it:
                for u in range(U):
                    act.wait_ge(window, U * it + u + 1)
                    act.wait_ge(seg, free(it, u))
                    for k, y in enumerate((1, 2, 3, 0)):
                        ins = act.activation(b.sy[:, u % 2, k * W:(k + 1) * W], b.hot[:, u % 2, :], ACT.Copy,
                                             scale=m.ea4[:, bass.ds(2 * it + u // G, 1), u % G, y])
                    ins.then_inc(weighed, 1)

        @block.vector
        def _(dve):
            def flush(it, c):
                base = dve.value_load(m.base_i[0:1, bass.ds(2 * it + c, 1)], min_val=0, max_val=N)
                acc = m.acc[:, :, bass.ds(base, W)]
                cnt = m.cnt[:, :, bass.ds(base, W)]
                dve.wait_ge(counted, done(it, G * c + G - 1))
                dve.wait_ge(flushed, 2 * it + c + AHEAD)
                dve.tensor_tensor(acc, m.ps[:, 2 + c, :].rearrange("p (a w) -> p a w", w=W), acc, ALU.add)
                for a in range(2):
                    view = m.ps[0:P, 4 + 2 * c + a, 0:5 * W].rearrange("p (a w) -> p a w", w=W)
                    part = cnt[:, 5 * a:5 * a + 5, :]
                    ins = dve.tensor_tensor(part, view, part, ALU.add)
                ins.then_inc(flushed, 1)

            dve.sem_inc(prod, AHEAD)
            dve.sem_inc(flushed, AHEAD)
            dve.tensor_tensor(m.dst_rel[:, :, :], m.dst_f[:, :, :],
                              m.base_f[:, :].rearrange("p (s a) -> p s a", a=1).to_broadcast([P, SB, G]),
                              ALU.subtract).then_inc(rel, 1)
            dve.wait_ge(rel, 1)
            with dve.Fori(0, NI) as it:
                for u in range(U):
                    dve.wait_ge(counted, free(it, u))
                    dve.wait_ge(weighed, free(it, u))
                    dve.tensor_scalar(b.hot[:, u % 2, :], m.iota[0:P, 0:W], m.dst_rel[:, bass.ds(2 * it + u // G, 1), u % G], None,
                                      ALU.is_equal).then_inc(window, 1)
                    dve.wait_ge(path, U * it + u + 1)
                    dve.wait_ge(gathered[u], 16 * it + 16)
                    dve.wait_ge(seg, free(it, u))
                    w, row, pr = m.ps[0:P, u % 2, :], b.rows[:, u, :], b.prod[:, u % 2, :]
                    dve.tensor_tensor(pr[:, 0:256].rearrange("p (a c) -> p a c", a=2), w[:, 0:256].rearrange("p (a c) -> p a c", a=2),
                                      row[:, 0:128].rearrange("p (a c) -> p a c", a=1).to_broadcast([P, 2, 128]), ALU.mult)
                    for a in range(2):
                        ins = dve.tensor_tensor(pr[:, 256 + 384 * a:640 + 384 * a].rearrange("p (a c) -> p a c", a=3),
                                                w[:, 256 + 128 * a:384 + 128 * a].rearrange("p (a c) -> p a c", a=1).to_broadcast([P, 3, 128]),
                                                row[:, 128:512].rearrange("p (a c) -> p a c", a=3), ALU.mult)
                    ins.then_inc(prod, 1)
                    if u % 2:
                        dve.tensor_scalar(b.hot_src[:, 1, 0:N], m.iota[0:P, 0:N], m.src_f[:, bass.ds(2 * it + u // G, 1), u % G], None,
                                          ALU.is_equal).then_inc(odd_senders, 1)
                    if u == G + 1:
                        flush(it, 0)
                flush(it, 1)


def edges(nc, m, a, ctx):
    edge_base_phase(nc, m, ctx, a["src_l"], a["dst_l"], a["ea4_l"])
    b = Tensors()
    b.h3 = sb(nc, ctx, "edge_hidden", [128, 2, 625])
    b.w4r = sb(nc, ctx, "w4_raw", [HID, 4 * MUL])
    b.w4 = sb(nc, ctx, "w4", [128, 4 * MUL])
    b.idx = sb(nc, ctx, "edge_index", [P, 2, G], I32)
    b.sender = sb(nc, ctx, "sender", [P, 2, G])
    b.rows = sb(nc, ctx, "sender_rows", [P, 2 * G, D])
    b.hot_src = sb(nc, ctx, "hot_src", [P, 2, N + 3], BF16)
    b.hot = sb(nc, ctx, "hot_dst", [P, 2, W], BF16)
    b.sy = sb(nc, ctx, "weighed_hot", [P, 2, 4 * W])
    b.prod = sb(nc, ctx, "edge_products", [P, 2, 8 * MUL])
    with phase(nc, "loaded", "done") as (block, loaded, done):
        @block.sync
        def _(sp):
            sp.dma_start(b.w4r[:, :], a["L0_gnn_W_mlp4"]).then_inc(loaded, 16)

        @block.vector
        def _(dve):
            dve.wait_ge(loaded, 16)
            c = SILU_2MOM * HID ** -0.5
            dve.tensor_scalar(b.w4[0:HID, 0:384], b.w4r[:, 0:384], c, None, ALU.mult).then_inc(done, 1)
            dve.tensor_scalar(b.w4[0:HID, 384:512], b.w4r[:, 384:512], c * 3 ** -0.5, None, ALU.mult).then_inc(done, 1)
            dve.memset(b.w4[HID:128, :], 0.0).then_inc(done, 1)
            dve.memset(b.h3[HID:128, :, :], 0.0).then_inc(done, 1)
            dve.memset(b.hot_src[:, :, N:N + 3], 0.0).then_inc(done, 1)
            dve.memset(m.acc[:, :, :], 0.0).then_inc(done, 1)
            dve.memset(m.cnt[:, :, :], 0.0).then_inc(done, 1)
    wide = nc.values_load(m.wide[0:1, 0:1], min_val=0, max_val=1)
    with nc.If(wide == 0):
        edge_sum_phase(nc, m, b, a["h3"], a["xup"])
    with nc.Else():
        with phase(nc, "done") as (block, done):
            @block.vector
            def _(dve):
                dve.memset(m.base_f[:, :], 0.0).then_inc(done, 1)
                dve.memset(m.base_i[:, :], 0).then_inc(done, 1)
        with nc.Fori(0, -(-N // W)) as _w:
            edge_sum_phase(nc, m, b, a["h3"], a["xup"])
            with phase(nc, "moved") as (block, moved):
                @block.vector
                def _(dve):
                    dve.tensor_scalar(b.sy[0:P, 0, 0:SB], m.base_f[:, :], float(W), None, ALU.add).then_inc(moved, 1)
                    dve.wait_ge(moved, 1)
                    dve.tensor_copy(m.base_f[:, :], b.sy[0:P, 0, 0:SB]).then_inc(moved, 1)
                    dve.tensor_copy(m.base_i[:, :], b.sy[0:P, 0, 0:SB]).then_inc(moved, 1)



def l0_mix(nc, m, a):
    R = 4
    with ExitStack() as ctx:
        w_in = sb(nc, ctx, "mix_w_in", [128, KB, D])
        b_in = sb(nc, ctx, "mix_b_in", [128, KB])
        xm = sb(nc, ctx, "mix_mid", [128, KB, N])
        bd = sb(nc, ctx, "mix_heads", [128, 144])
        qk = sb(nc, ctx, "mix_qk", [P, 2, T, 32])
        v = sb(nc, ctx, "mix_v", [P, T, D])
        w_out = sb(nc, ctx, "mix_w_out", [128, KB, D])
        b_out = sb(nc, ctx, "mix_b_out", [P, D])

        with phase(nc, "zeroed", "loaded") as (block, zeroed, loaded):
            @block.vector
            def _(dve):
                dve.memset(bd[:, :], 0.0).then_inc(zeroed, 1)

            @block.sync
            def _(sp):
                sp.wait_ge(zeroed, 1)
                for h in range(2):
                    rows = slice(64 * h, 64 * h + 64)
                    sp.dma_start(bd[rows, R * h:R * h + R], a["L0_mix_W_q"]).then_inc(loaded, 16)
                    sp.dma_start(bd[rows, 8 + R * h:8 + R * h + R], a["L0_mix_W_k"]).then_inc(loaded, 16)
                    sp.dma_start(bd[rows, 16 + 64 * h:80 + 64 * h], a["L0_mix_W_v"]).then_inc(loaded, 16)
                sp.wait_ge(loaded, 96)

        def mid_products(n, bank):
            f, (c0, cn) = n // 3, CH[n % 3]
            return [(bank[:, 0:cn], w_in[:, k, f * 128:(f + 1) * 128], m.xt[:, k, c0:c0 + cn]) for k in range(KB)]

        def mid_take(n, eng, bank, on_act):
            f, (c0, cn) = n // 3, CH[n % 3]
            return copy_scaled(eng, xm[:, f, c0:c0 + cn], bank[:, 0:cn], on_act, bias=b_in[:, f:f + 1])

        groups_phase(nc, m, 12, mid_products, mid_take,
                     loads=[(w_in[:, :, :], wview(a["L0_mix_W_in"])), (b_in[:, :], a["L0_mix_b_in"])])

        def head_products(n, bank):
            i, half = n // 2, n % 2
            return [(bank[0:P, 144 * k:144 * k + 144], xm[:, 2 * half + k, tile(i)], bd[:, :]) for k in range(2)]

        def head_take(n, eng, bank, on_act):
            i, half = n // 2, n % 2
            two = bank[0:P, 0:288].rearrange("p (k c) -> p k c", k=2)
            for j in range(2):
                out = qk[:, j, i, 16 * half:16 * half + 16].rearrange("p (k c) -> p k c", k=2)
                copy_scaled(eng, out, two[:, :, 8 * j:8 * j + 8], on_act)
            out = v[:, i, 256 * half:256 * half + 256].rearrange("p (k c) -> p k c", k=2)
            return copy_scaled(eng, out, two[:, :, 16:144], on_act)

        groups_phase(nc, m, 2 * T, head_products, head_take,
                     loads=[(w_out[:, :, :], wview(a["L0_mix_W_out"])), (b_out[:, :], spread_row(a["L0_mix_b_out"]))])

        qmax = sb(nc, ctx, "mix_qmax", [P, T, HEADS])
        qsum = sb(nc, ctx, "mix_qsum", [P, T, HEADS])
        qinv = sb(nc, ctx, "mix_qinv", [P, T, HEADS])
        kmax = sb(nc, ctx, "mix_kmax", [P, 32])
        kmax_all = sb(nc, ctx, "mix_kmax_all", [P, 32])
        sh = sb(nc, ctx, "mix_shifted", [P, 2, T, 32])
        ex = sb(nc, ctx, "mix_exp", [P, 2, T, 32])
        qs = sb(nc, ctx, "mix_q_soft", [P, T, 32])
        qt = sb(nc, ctx, "mix_qt", [32, N])
        mask = sb(nc, ctx, "mix_mask", [32, HEADS, DH])
        dinv = sb(nc, ctx, "mix_dinv", [32, 1])
        kv = sb(nc, ctx, "mix_kv", [32, D])
        kvt = sb(nc, ctx, "mix_kvt", [128, KB, 32])
        kvw = sb(nc, ctx, "mix_kvw", [32, D])
        with phase(nc, "masked", "v_step", "a_step", "p_step", "t_step") as (block, masked, v_step, a_step, p_step, t_step):
            @block.gpsimd
            def _(pool):
                pool.memset(mask[:, :, :], 1.0).then_inc(masked, 1)
                pool.wait_ge(masked, 1)
                pool.affine_select(out=mask[:, :, :], in_=mask[:, :, :], compare_op=ALU.is_ge, fill=0.0, base=0,
                                   pattern=[[-R, HEADS], [0, DH]], channel_multiplier=1).then_inc(masked, 1)
                pool.wait_ge(masked, 2)
                pool.affine_select(out=mask[:, :, :], in_=mask[:, :, :], compare_op=ALU.is_ge, fill=0.0, base=R - 1,
                                   pattern=[[R, HEADS], [0, DH]], channel_multiplier=-1).then_inc(masked, 1)
                pool.wait_ge(v_step, 1)
                pool.partition_all_reduce(kmax_all[:, :], kmax[:, :], P, RMAX).then_inc(p_step, 1)

            @block.vector
            def _(dve):
                heads = lambda ap: ap.rearrange("p t (h r) -> p t h r", r=R)
                wide = lambda ap: ap.rearrange("p t (h a) -> p t h a", a=1).to_broadcast([P, T, HEADS, R])
                dve.tensor_reduce(kmax[:, :], qk[:, 1, :, :].rearrange("p t c -> p c t"), AX.X, ALU.max).then_inc(v_step, 1)
                dve.tensor_reduce(qmax[:, :, :], heads(qk[:, 0, :, :]), AX.X, ALU.max).then_inc(v_step, 1)
                dve.wait_ge(v_step, 2)
                dve.tensor_tensor(heads(sh[:, 0, :, :]), heads(qk[:, 0, :, :]), wide(qmax[:, :, :]), ALU.subtract).then_inc(v_step, 1)
                dve.wait_ge(p_step, 1)
                dve.tensor_tensor(sh[:, 1, :, :], qk[:, 1, :, :],
                                  kmax_all[:, :].rearrange("p (a c) -> p a c", a=1).to_broadcast([P, T, 32]), ALU.subtract).then_inc(v_step, 1)
                dve.wait_ge(a_step, 1)
                dve.tensor_reduce(qsum[:, :, :], heads(ex[:, 0, :, :]), AX.X, ALU.add).then_inc(v_step, 1)
                dve.wait_ge(v_step, 5)
                dve.reciprocal(qinv[:, :, :], qsum[:, :, :]).then_inc(v_step, 1)
                dve.wait_ge(v_step, 6)
                dve.tensor_tensor(heads(qs[:, :, :]), heads(ex[:, 0, :, :]), wide(qinv[:, :, :]), ALU.mult).then_inc(v_step, 1)
                dve.wait_ge(t_step, 1)
                dve.reciprocal(dinv[:, :], m.ps[0:32, 1, 0:1]).then_inc(v_step, 1)
                dve.wait_ge(v_step, 8)
                dve.wait_ge(masked, 3)
                dve.scalar_tensor_tensor(kv[:, :], m.ps[0:32, 0, :], dinv[:, 0:1], mask[:, :, :].rearrange("p h c -> p (h c)"),
                                         ALU.mult, ALU.mult).then_inc(v_step, 1)
                dve.wait_ge(t_step, 3)
                dve.tensor_copy(kvt[:, :, :], m.ps[:, 5, 0:128].rearrange("p (k c) -> p k c", k=KB)).then_inc(v_step, 1)
                dve.wait_ge(t_step, 4)
                dve.tensor_copy(kvw[:, :], m.ps[0:32, 6, :]).then_inc(v_step, 1)

            @block.scalar
            def _(act):
                act.wait_ge(v_step, 4)
                act.activation(ex[:, :, :, :], sh[:, :, :, :], ACT.Exp).then_inc(a_step, 1)
                act.wait_ge(t_step, 2)
                for c0, cn in CH:
                    ins = act.activation(qt[:, c0:c0 + cn], m.ps[0:32, 2 + c0 // 500, 0:cn], ACT.Copy)
                ins.then_inc(a_step, 1)

            @block.tensor
            def _(pe):
                pe.wait_ge(a_step, 1)
                for i in range(T):
                    pe.matmul(m.ps[0:32, 0, :], ex[:, 1, i, :], v[:, i, :], start=i == 0, stop=i == T - 1)
                for i in range(T):
                    ins = pe.matmul(m.ps[0:32, 1, 0:1], ex[:, 1, i, :], m.ones[0:P, 0:1], start=i == 0, stop=i == T - 1)
                ins.then_inc(t_step, 1)
                pe.wait_ge(v_step, 7)
                for i in range(T):
                    ins = pe.transpose(m.ps[0:32, 2 + i // 4, (i % 4) * P:(i % 4 + 1) * P], qs[:, i, :], m.ident[0:P, 0:P])
                ins.then_inc(t_step, 1)
                pe.wait_ge(v_step, 9)
                for k in range(KB):
                    ins = pe.transpose(m.ps[:, 5, k * 32:(k + 1) * 32], kv[:, k * 128:(k + 1) * 128], m.ident[0:32, 0:32])
                ins.then_inc(t_step, 1)
                pe.wait_ge(v_step, 10)
                for k in range(KB):
                    ins = pe.matmul(m.ps[0:32, 6, :], kvt[:, k, :], w_out[:, k, :], start=k == 0, stop=k == KB - 1)
                ins.then_inc(t_step, 1)

        def out_products(n, bank):
            return [(bank[0:P, :], qt[:, tile(n)], kvw[:, :])]

        def out_take(n, dve, bank):
            return dve.tensor_tensor(m.x[:, n, :], bank[0:P, :], m.x[:, n, :], ALU.add)

        vector_groups_phase(nc, m, T, out_products, out_take)
        add_rows(nc, m, b_out)


def add_rows(nc, m, row):
    with phase(nc, "added") as (block, added):
        @block.vector
        def _(dve):
            for i in range(T):
                dve.tensor_tensor(m.x[:, i, :], m.x[:, i, :], row[:, :], ALU.add).then_inc(added, 1)



def l0_ffn(nc, m, a):
    NE = 8
    KEEP = N // NE
    with ExitStack() as ctx:
        layernorm_phase(nc, m, m.x, lambda i: m.tmp[:, i % 2, :], m.xt)
        gw = sb(nc, ctx, "gate_w", [128, KB, NE])
        g0 = sb(nc, ctx, "gates", [P, T, NE])
        t = sb(nc, ctx, "sink_t", [P, T, NE])
        cg = sb(nc, ctx, "sink_weights", [P, T, NE])
        coef = sb(nc, ctx, "combine", [P, T, NE])

        def gate_products(n, bank):
            return [(bank[0:P, 0:NE], m.xt[:, k, tile(n)], gw[:, k, :]) for k in range(KB)]

        def gate_take(n, dve, bank):
            return dve.tensor_scalar(g0[:, n, :], bank[0:P, 0:NE], 1e-10, None, ALU.max)

        vector_groups_phase(nc, m, T, gate_products, gate_take, loads=[(gw[:, :, :], wview(a["L0_ffn_gate_w"][0]))])
        with phase(nc, "logged") as (block, logged):
            @block.scalar
            def _(act):
                act.activation(t[:, :, :], g0[:, :, :], ACT.Ln).then_inc(logged, 1)

        mt = sb(nc, ctx, "sink_max", [P, NE])
        mall = sb(nc, ctx, "sink_max_all", [P, NE])
        d1 = sb(nc, ctx, "sink_d1", [P, T, NE])
        e1 = sb(nc, ctx, "sink_e1", [P, T, NE])
        s1 = sb(nc, ctx, "sink_s1", [P, NE])
        l1 = sb(nc, ctx, "sink_l1", [P, NE])
        d2 = sb(nc, ctx, "sink_d2", [P, T, NE])
        m2 = sb(nc, ctx, "sink_m2", [P, T])
        d3 = sb(nc, ctx, "sink_d3", [P, T, NE])
        e2 = sb(nc, ctx, "sink_e2", [P, T, NE])
        s2 = sb(nc, ctx, "sink_s2", [P, T])
        l2 = sb(nc, ctx, "sink_l2", [P, T])
        by_expert = lambda ap: ap.rearrange("p (a e) -> p a e", a=1).to_broadcast([P, T, NE])
        by_token = lambda ap: ap.rearrange("p (t a) -> p t a", a=1).to_broadcast([P, T, NE])
        with nc.Fori(0, 8):
            with phase(nc, "v_step", "a_step", "p_step", "t_step") as (block, v_step, a_step, p_step, t_step):
                @block.vector
                def _(dve):
                    dve.tensor_reduce(mt[:, :], t[:, :, :].rearrange("p t e -> p e t"), AX.X, ALU.max).then_inc(v_step, 1)
                    dve.wait_ge(p_step, 1)
                    dve.tensor_tensor(d1[:, :, :], t[:, :, :], by_expert(mall[:, :]), ALU.subtract).then_inc(v_step, 1)
                    dve.wait_ge(a_step, 1)
                    dve.tensor_reduce(s1[:, :], e1[:, :, :].rearrange("p t e -> p e t"), AX.X, ALU.add).then_inc(v_step, 1)
                    dve.wait_ge(a_step, 2)
                    dve.tensor_tensor(d2[:, :, :], d1[:, :, :], by_expert(l1[:, :]), ALU.subtract).then_inc(v_step, 1)
                    dve.wait_ge(v_step, 4)
                    dve.tensor_reduce(m2[:, :], d2[:, :, :], AX.X, ALU.max).then_inc(v_step, 1)
                    dve.wait_ge(v_step, 5)
                    dve.tensor_tensor(d3[:, :, :], d2[:, :, :], by_token(m2[:, :]), ALU.subtract).then_inc(v_step, 1)
                    dve.wait_ge(a_step, 3)
                    dve.tensor_reduce(s2[:, :], e2[:, :, :], AX.X, ALU.add).then_inc(v_step, 1)
                    dve.wait_ge(a_step, 4)
                    dve.tensor_tensor(t[:, :, :], d3[:, :, :], by_token(l2[:, :]), ALU.subtract).then_inc(v_step, 1)

                @block.gpsimd
                def _(pool):
                    pool.wait_ge(v_step, 1)
                    pool.partition_all_reduce(mall[:, :], mt[:, :], P, RMAX).then_inc(p_step, 1)

                @block.tensor
                def _(pe):
                    pe.wait_ge(v_step, 3)
                    pe.matmul(m.ps[0:P, 0, 0:NE], m.ones[0:P, 0:P], s1[:, :], start=True, stop=True).then_inc(t_step, 1)

                @block.scalar
                def _(act):
                    act.wait_ge(v_step, 2)
                    act.activation(e1[:, :, :], d1[:, :, :], ACT.Exp).then_inc(a_step, 1)
                    act.wait_ge(t_step, 1)
                    act.activation(l1[:, :], m.ps[0:P, 0, 0:NE], ACT.Ln).then_inc(a_step, 1)
                    act.wait_ge(v_step, 6)
                    act.activation(e2[:, :, :], d3[:, :, :], ACT.Exp).then_inc(a_step, 1)
                    act.wait_ge(v_step, 7)
                    act.activation(l2[:, :], s2[:, :], ACT.Ln).then_inc(a_step, 1)

        cgt = sb(nc, ctx, "weights_by_expert", [NE, 2, N + 8])
        best = sb(nc, ctx, "best", [NE, 2, 8])
        chosen_t = sb(nc, ctx, "chosen_by_expert", [NE, N])
        chosen = sb(nc, ctx, "chosen", [P, T, NE])
        count = sb(nc, ctx, "chosen_by", [P, T])
        inv = sb(nc, ctx, "share", [P, T])
        half = sb(nc, ctx, "over_half", [P, T, NE])
        ROUNDS = -(-KEEP // 8)
        REST = KEEP - 8 * (ROUNDS - 1)
        TAKEN, PAD = -2.0, -1.0
        with phase(nc, "v_step", "a_step", "t_step", "found", "struck") as (block, v_step, a_step, t_step, found, struck):
            @block.scalar
            def _(act):
                act.activation(cg[:, :, :], t[:, :, :], ACT.Exp).then_inc(a_step, 1)
                act.wait_ge(t_step, 1)
                for c0, cn in CH:
                    ins = act.activation(cgt[:, 0, c0:c0 + cn], m.ps[0:NE, c0 // 500, 0:cn], ACT.Copy)
                ins.then_inc(a_step, 1)

            @block.tensor
            def _(pe):
                pe.wait_ge(a_step, 1)
                for i in range(T):
                    ins = pe.transpose(m.ps[0:NE, i // 4, (i % 4) * P:(i % 4 + 1) * P], cg[:, i, :], m.ident[0:P, 0:P])
                ins.then_inc(t_step, 1)
                pe.wait_ge(v_step, 3)
                for i in range(T):
                    ins = pe.transpose(m.ps[0:P, 4, i * NE:(i + 1) * NE], chosen_t[:, tile(i)], m.ident[0:NE, 0:NE])
                ins.then_inc(t_step, 1)

            @block.vector
            def _(dve):
                dve.memset(cgt[:, :, N:N + 8], PAD).then_inc(v_step, 1)
                dve.memset(best[:, 1, :], PAD).then_inc(v_step, 1)
                dve.wait_ge(v_step, 2)
                dve.wait_ge(a_step, 2)
                for r in range(ROUNDS):
                    last = r == ROUNDS - 1
                    if r:
                        dve.wait_ge(struck, r)
                    dve.max(best[:, 0, :], cgt[:, r % 2, :]).then_inc(found, 1)
                    dve.wait_ge(found, r + 1)
                    if last:
                        dve.tensor_copy(best[:, 1, 0:REST], best[:, 0, 0:REST]).then_inc(found, 1)
                        dve.wait_ge(found, r + 2)
                    dve.match_replace(cgt[:, (r + 1) % 2, :], best[:, int(last), :], cgt[:, r % 2, :], TAKEN).then_inc(struck, 1)
                dve.wait_ge(struck, ROUNDS)
                dve.tensor_scalar(chosen_t[:, :], cgt[:, ROUNDS % 2, 0:N], (TAKEN + PAD) / 2, None, ALU.is_le).then_inc(v_step, 1)
                dve.wait_ge(t_step, 2)
                dve.tensor_copy(chosen[:, :, :], m.ps[0:P, 4, 0:T * NE].rearrange("p (t e) -> p t e", e=NE)).then_inc(v_step, 1)
                dve.tensor_scalar(half[:, :, :], cg[:, :, :], 0.5, None, ALU.is_gt).then_inc(v_step, 1)
                dve.wait_ge(v_step, 5)
                dve.tensor_reduce(count[:, :], chosen[:, :, :], AX.X, ALU.add).then_inc(v_step, 1)
                dve.tensor_tensor(half[:, :, :], half[:, :, :], chosen[:, :, :], ALU.mult).then_inc(v_step, 1)
                dve.wait_ge(v_step, 7)
                dve.tensor_scalar(s2[:, :], count[:, :], 1.0, None, ALU.add).then_inc(v_step, 1)
                dve.wait_ge(v_step, 8)
                dve.reciprocal(inv[:, :], s2[:, :]).then_inc(v_step, 1)
                dve.wait_ge(v_step, 9)
                dve.tensor_tensor(coef[:, :, :], half[:, :, :], by_token(inv[:, :]), ALU.mult).then_inc(v_step, 1)

        w = sb(nc, ctx, "expert_w", [128, 2, KB, D])
        SLOTS, AHEAD = 5, T
        with phase(nc, "w_a", "w_b", "product", "taken") as (block, w_a, w_b, product, taken):
            loaded = (w_a, w_b)
            experts = a["L0_ffn_experts"].rearrange("e (k p) f -> e p k f", p=128)

            @block.sync
            def _(sp):
                for c in range(2):
                    sp.dma_start(w[:, c, :, :], experts[c]).then_inc(loaded[c], 16)
                with sp.Fori(0, NE // 2 - 1) as it:
                    for c in range(2):
                        sp.wait_ge(product, 2 * T * it + T * (c + 1))
                        sp.dma_start(w[:, c, :, :], experts[bass.ds(2 * it + 2 + c, 1)].rearrange("a p k f -> (a p) k f")).then_inc(loaded[c], 16)

            @block.tensor
            def _(pe):
                with pe.Fori(0, NE // 2) as it:
                    for c in range(2):
                        pe.wait_ge(loaded[c], 16 * it + 16)
                        for i in range(T):
                            n = T * c + i
                            pe.wait_ge(taken, 2 * T * it + n + 1 - SLOTS + AHEAD)
                            for k in range(KB):
                                ins = pe.matmul(m.ps[0:P, n % SLOTS, :], m.xt[:, k, tile(i)], w[:, c, k, :], start=k == 0, stop=k == KB - 1)
                            ins.then_inc(product, 1)

            @block.vector
            def _(dve):
                dve.sem_inc(taken, AHEAD)
                with dve.Fori(0, NE // 2) as it:
                    for c in range(2):
                        for i in range(T):
                            n = T * c + i
                            dve.wait_ge(product, 2 * T * it + n + 1)
                            dve.wait_ge(taken, 2 * T * it + n - T + AHEAD + 1)
                            dve.scalar_tensor_tensor(m.x[:, i, :], m.ps[0:P, n % SLOTS, :], coef[:, i, bass.ds(2 * it + c, 1)], m.x[:, i, :],
                                                     ALU.mult, ALU.add).then_inc(taken, 1)



def attention(nc, m, tag, qt, kt, v, ot, mask=None, cnt=None):
    own = lambda h: slice(64 * (h % 2), 64 * (h % 2) + 64)
    other = lambda h: own(h + 1)
    C = len(CH)
    UNITS = HEADS * C
    with ExitStack() as ctx:
        per = 2 if mask is None else 3
        part = sb(nc, ctx, tag + "row_max_parts", [P, HEADS * T, per])
        rmax = sb(nc, ctx, tag + "row_max", [P, HEADS * T])
        ks = sb(nc, ctx, tag + "k_split", [128, 2, N], F32R)
        qs = sb(nc, ctx, tag + "q_split", [128, 2, 2, 512], F32R)
        z = m.tmp4

        def round_parts(act, u, q_rounded, k_rounded):
            h, (c0, cn) = u // C, CH[u % C]
            if u % C == 0:
                act.activation(ks[own(h), h % 2, :], kt[own(h), h // 2, :], ACT.Copy)
                act.activation(ks[other(h), h % 2, :], kt[own(h), h // 2, :], ACT.Copy).then_inc(k_rounded, 1)
            act.activation(qs[own(h), u % 2, 0, 0:cn], qt[own(h), h // 2, c0:c0 + cn], ACT.Copy)
            act.activation(qs[other(h), u % 2, 0, 0:cn], qt[own(h), h // 2, c0:c0 + cn], ACT.Copy).then_inc(q_rounded, 1)

        def rest_parts(pool, u, q_rounded, k_rounded, q_rest, k_ready):
            h, (c0, cn) = u // C, CH[u % C]
            if u % C == 0:
                pool.wait_ge(k_rounded, h + 1)
                pool.tensor_tensor(ks[own(h), h % 2, :], kt[own(h), h // 2, :], ks[own(h), h % 2, :].bitcast(F32), ALU.subtract).then_inc(k_ready, 1)
            pool.wait_ge(q_rounded, u + 1)
            pool.tensor_tensor(qs[own(h), u % 2, 1, 0:cn], qt[own(h), h // 2, c0:c0 + cn], qs[own(h), u % 2, 0, 0:cn].bitcast(F32),
                               ALU.subtract).then_inc(q_rest, 1)

        def double_rest(act, u, q_rest, q_ready):
            h, (c0, cn) = u // C, CH[u % C]
            act.wait_ge(q_rest, u + 1)
            act.activation(qs[other(h), u % 2, 1, 0:cn], qs[own(h), u % 2, 1, 0:cn].bitcast(F32), ACT.Copy).then_inc(q_ready, 1)

        tiles_to = lambda u: T * (u // C) + (4, 8, 10)[u % C]
        with phase(nc, "scores", "maxed", "row", "q_rounded", "k_rounded", "q_rest", "k_ready", "q_ready") as (
                block, scores, maxed, row, q_rounded, k_rounded, q_rest, k_ready, q_ready):
            @block.tensor
            def _(pe):
                for n in range(HEADS * T):
                    h, i = n // T, n % T
                    u = C * h + i // 4
                    if i % 4 == 0:
                        pe.wait_ge(q_ready, u + 1)
                        pe.wait_ge(k_ready, h + 1)
                    if n >= 2:
                        pe.wait_ge(maxed, per * (n - 1))
                    for j, (c0, cn) in enumerate(CH):
                        for r in range(2):
                            ins = pe.matmul(m.ps[0:P, 4 * (n % 2) + j, 0:cn], qs[:, u % 2, r, (i % 4) * P:(i % 4 + 1) * P],
                                            ks[:, h % 2, c0:c0 + cn], start=r == 0, stop=r == 1)
                    ins.then_inc(scores, 1)

            @block.gpsimd
            def _(pool):
                for u in range(UNITS):
                    rest_parts(pool, u, q_rounded, k_rounded, q_rest, k_ready)

            @block.scalar
            def _(act):
                for u in range(UNITS):
                    if u >= 2:
                        act.wait_ge(scores, tiles_to(u - 2))
                    if u % C == 0 and u >= 2 * C:
                        act.wait_ge(scores, T * (u // C - 1))
                    round_parts(act, u, q_rounded, k_rounded)
                    double_rest(act, u, q_rest, q_ready)

            @block.vector
            def _(dve):
                for n in range(HEADS * T):
                    dve.wait_ge(scores, n + 1)
                    bank = 4 * (n % 2)
                    if mask is None:
                        dve.tensor_reduce(part[:, n, 0:1], m.ps[0:P, bank:bank + 2, 0:500], AX.XY, ALU.max).then_inc(maxed, 1)
                        dve.tensor_reduce(part[:, n, 1:2], m.ps[0:P, bank + 2, 0:250], AX.X, ALU.max).then_inc(maxed, 1)
                        continue
                    for j, (c0, cn) in enumerate(CH):
                        if n:
                            dve.wait_ge(maxed, 3 * n - 2 + j)
                        dve.tensor_tensor_reduce(z[:, j, 0:cn], m.ps[0:P, bank + j, 0:cn], mask[:, n % T, c0:c0 + cn],
                                                 1.0, -BIG, ALU.add, ALU.max, part[:, n, j:j + 1]).then_inc(maxed, 1)
                dve.wait_ge(maxed, per * HEADS * T)
                dve.tensor_reduce(rmax[:, :], part[:, :, :], AX.X, ALU.max).then_inc(row, 1)

        RING = 4
        mb = sb(nc, ctx, tag + "max_by_column", [P, 2, 512])
        rec = sb(nc, ctx, tag + "denominators", [128, 512])
        LAG = 2
        with phase(nc, "spread", "kept", "scores", "shift", "clip", "expd", "counted", "summed", "inverted",
                   "normed", "q_rounded", "k_rounded", "q_rest", "k_ready", "q_ready") as (
                block, spread, kept, scores, shift, clip, expd, counted, summed, inverted, normed,
                q_rounded, k_rounded, q_rest, k_ready, q_ready):
            weighed = expd if mask is None else counted

            @block.tensor
            def _(pe):
                def maxima(u):
                    h, (c0, cn) = u // C, CH[u % C]
                    if u >= 2:
                        pe.wait_ge(kept, u - 1)
                    for i in range(cn // P):
                        col = h * T + c0 // P + i
                        ins = pe.transpose(m.ps[0:P, 6 + u % 2, i * P:(i + 1) * P], rmax[:, col:col + 1].to_broadcast([P, P]),
                                           m.ident[0:P, 0:P])
                    ins.then_inc(spread, 1)

                def sums(n):
                    u, j = n // T, n % T
                    h, (c0, cn) = u // C, CH[u % C]
                    if j == 0 and u >= 2:
                        pe.wait_ge(normed, u - 1)
                    pe.wait_ge(weighed, n + 1)
                    w0 = 64 * (h % 2)
                    pe.matmul(m.ps[:, 4 + u % 2, 0:cn], v[:, j, h // 2, w0:w0 + 128], z[:, n % RING, 0:cn],
                              start=j == 0, stop=j == T - 1).then_inc(summed, 1)

                maxima(0)
                for n in range(UNITS * T + LAG):
                    if n < UNITS * T:
                        u, j = n // T, n % T
                        h, (c0, cn) = u // C, CH[u % C]
                        if j == 0:
                            pe.wait_ge(q_ready, u + 1)
                            pe.wait_ge(k_ready, h + 1)
                        if n >= 4:
                            pe.wait_ge(shift, n - 3)
                        for r in range(2):
                            ins = pe.matmul(m.ps[0:P, n % 4, 0:cn], ks[:, h % 2, tile(j)], qs[:, u % 2, r, 0:cn], start=r == 0, stop=r == 1)
                        ins.then_inc(scores, 1)
                        if j == 5 and u + 1 < UNITS:
                            maxima(u + 1)
                    if n >= LAG:
                        sums(n - LAG)

            @block.gpsimd
            def _(pool):
                for u in range(UNITS):
                    rest_parts(pool, u, q_rounded, k_rounded, q_rest, k_ready)

            @block.vector
            def _(dve):
                def norm(u):
                    h, (c0, cn) = u // C, CH[u % C]
                    num, den = own(h), other(h)
                    dve.wait_ge(summed, T * (u + 1))
                    if u:
                        dve.wait_ge(normed, u)
                    dve.reciprocal(rec[num, 0:cn], m.ps[den, 4 + u % 2, 0:cn]).then_inc(inverted, 1)
                    dve.wait_ge(inverted, u + 1)
                    dve.tensor_tensor(ot[num, h // 2, c0:c0 + cn], m.ps[num, 4 + u % 2, 0:cn], rec[num, 0:cn],
                                      ALU.mult).then_inc(normed, 1)

                def count(n):
                    u, j = n // T, n % T
                    c0, cn = CH[u % C]
                    dve.wait_ge(expd, n + 1)
                    dve.tensor_tensor(z[:, n % RING, 0:cn], z[:, n % RING, 0:cn], cnt[:, j, c0:c0 + cn], ALU.mult).then_inc(counted, 1)

                for n in range(UNITS * T):
                    u, j = n // T, n % T
                    c0, cn = CH[u % C]
                    if j == 0:
                        dve.wait_ge(kept, u + 1)
                    if n >= RING:
                        dve.wait_ge(summed, n - RING + 1)
                    dve.wait_ge(scores, n + 1)
                    dve.tensor_tensor(z[:, n % RING, 0:cn], m.ps[0:P, n % 4, 0:cn], mb[:, u % 2, 0:cn], ALU.subtract).then_inc(shift, 1)
                    if mask is not None and n >= 1:
                        count(n - 1)
                    if j == 4 and u >= 1:
                        norm(u - 1)
                if mask is not None:
                    count(UNITS * T - 1)
                norm(UNITS - 1)

            @block.scalar
            def _(act):
                def keep(u):
                    c0, cn = CH[u % C]
                    act.wait_ge(spread, u + 1)
                    if u >= 2:
                        act.wait_ge(shift, T * (u - 1))
                    act.activation(mb[:, u % 2, 0:cn], m.ps[0:P, 6 + u % 2, 0:cn], ACT.Copy).then_inc(kept, 1)

                def split(u):
                    if u >= 2:
                        act.wait_ge(scores, T * (u - 1))
                    round_parts(act, u, q_rounded, k_rounded)

                split(0)
                double_rest(act, 0, q_rest, q_ready)
                keep(0)
                for n in range(UNITS * T):
                    u, j = n // T, n % T
                    cn = CH[u % C][1]
                    slot = z[:, n % RING, 0:cn]
                    act.wait_ge(shift, n + 1)
                    if mask is None:
                        act.activation(slot, slot, ACT.Exp, scale=DH ** -0.5).then_inc(expd, 1)
                    else:
                        act.activation(slot, slot, ACT.Relu, scale=-(DH ** -0.5)).then_inc(clip, 1)
                        act.wait_ge(clip, n + 1)
                        act.activation(slot, slot, ACT.Exp, scale=-1.0).then_inc(expd, 1)
                    if u + 1 < UNITS:
                        if j == 1:
                            split(u + 1)
                        if j == 6:
                            double_rest(act, u + 1, q_rest, q_ready)
                            keep(u + 1)


def qkv_for_attention(nc, m, w, wq, wk, wv, qt, kt, v, loads):
    def products(n, bank):
        if n < 24:
            wx, f = (wq, n // 3) if n < 12 else (wk, n // 3 - 4)
            c0, cn = CH[n % 3]
            return [(bank[:, 0:cn], wx(k)[:, f * 128:(f + 1) * 128], m.xt[:, k, c0:c0 + cn]) for k in range(KB)]
        return [(bank[0:P, :], m.xt[:, k, tile(n - 24)], wv(k)) for k in range(KB)]

    def take(n, eng, bank, on_act):
        if n < 24:
            dst, f = (qt, n // 3) if n < 12 else (kt, n // 3 - 4)
            c0, cn = CH[n % 3]
            return copy_scaled(eng, dst[:, f, c0:c0 + cn], bank[:, 0:cn], on_act)
        i = n - 24
        pairs = bank[0:P, :].rearrange("p (b e c) -> p b e c", b=KB, e=2)
        copy_scaled(eng, v[:, i, :, 0:64], pairs[:, :, 0, :], on_act)
        return copy_scaled(eng, v[:, i, :, 128:192], pairs[:, :, 1, :], on_act)

    groups_phase(nc, m, 24 + T, products, take, loads=loads)


def ones_between(nc, v):
    with phase(nc, "filled") as (block, filled):
        @block.gpsimd
        def _(pool):
            for i in range(T):
                pool.memset(v[:, i, :, 64:128], 1.0).then_inc(filled, 1)


def move(nc, pairs):
    load_phase(nc, pairs)



def l1_gnn(nc, m, a, tok):
    layernorm_phase(nc, m, m.x, lambda i: m.tmp[:, i % 2, :], m.xt)
    with ExitStack() as ctx:
        with ExitStack() as c2:
            xn = sb(nc, c2, "xn_rows", [P, T, D])
            layernorm_phase(nc, m, m.x, lambda i: xn[:, i, :])
            move(nc, [(tok(a["xs"]), m.x[:, :, :]), (tok(a["xn"]), xn[:, :, :])])
        with ExitStack() as c2:
            qt = m.xraw[:, 0:KB * N].rearrange("p (k n) -> p k n", k=KB)
            kt = sb(nc, c2, "kt", [128, KB, N])
            v = sb(nc, c2, "v", [P, T, KB, 192])
            ones_between(nc, v)
            with ExitStack() as c3:
                w = sb(nc, c3, "wqkv", [128, 3, KB, D])
                qkv_for_attention(nc, m, w, lambda k: w[:, 0, k, :], lambda k: w[:, 1, k, :], lambda k: w[:, 2, k, :], qt, kt, v,
                                  [(w[:, j, :, :], wview(x)) for j, x in enumerate((a["L1_gnn_Wq"], a["L1_gnn_Wk"], a["L1_gnn_Wv"]))])
            mask = sb(nc, c2, "mask", [P, T, N], BF16)

            with phase(nc, "turned", "taken") as (block, turned, taken):
                @block.tensor
                def _(pe):
                    for n in range(T * 3):
                        i, (c0, cn) = n // 3, CH[n % 3]
                        if n >= 8:
                            pe.wait_ge(taken, n - 7)
                        for b in range(cn // P):
                            ins = pe.transpose(m.ps[0:P, n % 8, b * P:(b + 1) * P], m.cnt[:, c0 // P + b, tile(i)], m.ident[0:P, 0:P])
                        ins.then_inc(turned, 1)

                @block.vector
                def _(dve):
                    for n in range(T * 3):
                        i, (c0, cn) = n // 3, CH[n % 3]
                        dve.wait_ge(turned, n + 1)
                        dve.tensor_scalar(mask[:, i, c0:c0 + cn], m.ps[0:P, n % 8, 0:cn], 0.0, -1e30, ALU.is_equal, ALU.mult).then_inc(taken, 1)

            attention(nc, m, "gnn_", qt, kt, v, m.xt, mask, m.cnt)

    with ExitStack() as ctx:
        y = sb(nc, ctx, "gnn_y", [P, T, D])
        rows = sb(nc, ctx, "gnn_rows", [P, 5, D])
        wo = sb(nc, ctx, "gnn_wo", [128, KB, D])
        w1 = sb(nc, ctx, "gnn_w1", [128, KB, 256])
        w2 = sb(nc, ctx, "gnn_w2", [128, 2, D])
        b1 = sb(nc, ctx, "gnn_b1", [128, 2])
        hid = sb(nc, ctx, "gnn_hidden", [128, 2, N])
        names = (a["L1_gnn_ln1_g"], a["L1_gnn_ln1_b"], a["L1_gnn_ln2_g"], a["L1_gnn_ln2_b"], a["L1_gnn_b2"])
        move(nc, [(m.x[:, :, :], tok(a["xn"])), (wo[:, :, :], wview(a["L1_gnn_Wo"])), (w1[:, :, :], wview(a["L1_gnn_W1"])),
                  (w2[:, :, :], wview(a["L1_gnn_W2"])), (b1[:, :], a["L1_gnn_b1"])]
             + [(rows[:, j, :], spread_row(r)) for j, r in enumerate(names)])
        vector_groups_phase(nc, m, T, lambda n, bank: [(bank[0:P, :], m.xt[:, k, tile(n)], wo[:, k, :]) for k in range(KB)],
                            lambda n, dve, bank: dve.tensor_tensor(m.x[:, n, :], bank[0:P, :], m.x[:, n, :], ALU.add))
        layernorm_phase(nc, m, m.x, lambda i: y[:, i, :], m.xt, gain_row=rows[:, 0, :], bias_row=rows[:, 1, :])

        def hidden_products(n, bank):
            f, (c0, cn) = n // 3, CH[n % 3]
            return [(bank[:, 0:cn], w1[:, k, f * 128:(f + 1) * 128], m.xt[:, k, c0:c0 + cn]) for k in range(KB)]

        def hidden_take(n, dve, bank):
            f, (c0, cn) = n // 3, CH[n % 3]
            return dve.tensor_scalar(hid[:, f, c0:c0 + cn], bank[:, 0:cn], b1[:, f:f + 1], 0.0, ALU.add, ALU.max)

        vector_groups_phase(nc, m, 6, hidden_products, hidden_take)
        vector_groups_phase(nc, m, T, lambda n, bank: [(bank[0:P, :], hid[:, k, tile(n)], w2[:, k, :]) for k in range(2)],
                            lambda n, dve, bank: dve.tensor_tensor(y[:, n, :], bank[0:P, :], y[:, n, :], ALU.add))
        with phase(nc, "added") as (block, added):
            @block.vector
            def _(dve):
                for i in range(T):
                    dve.tensor_tensor(y[:, i, :], y[:, i, :], rows[:, 4, :], ALU.add).then_inc(added, 1)
        layernorm_phase(nc, m, y, lambda i: m.x[:, i, :], None, gain_row=rows[:, 2, :], bias_row=rows[:, 3, :])
        add_into_saved(nc, m, a, tok, y)


def add_into_saved(nc, m, a, tok, y):
    with phase(nc, "loaded", "added", "stored") as (block, loaded, added, stored):
        @block.sync
        def _(sp):
            sp.dma_start(y[:, :, :], tok(a["xs"])).then_inc(loaded, 16)
            sp.wait_ge(added, T)
            sp.dma_start(tok(a["xs"]), m.x[:, :, :]).then_inc(stored, 16)
            sp.wait_ge(stored, 16)

        @block.vector
        def _(dve):
            dve.wait_ge(loaded, 16)
            for i in range(T):
                dve.tensor_tensor(m.x[:, i, :], m.x[:, i, :], y[:, i, :], ALU.add).then_inc(added, 1)



def l1_mix(nc, m, a, tok):
    F = 256
    H2 = 2 * D
    head = lambda h: slice(64 * (h % 2), 64 * (h % 2) + 64)
    with ExitStack() as ctx:
        cols = sb(nc, ctx, "mixer_cols", [128, 4, KB])
        move(nc, [(m.x[:, :, :], tok(a["xn"]))] + [(cols[:, j, :], c) for j, c in enumerate(
            (a["L1_mix_g1"], a["L1_mix_be1"], a["L1_mix_g2"], a["L1_mix_be2"]))])
        layernorm_phase(nc, m, m.x, lambda i: m.tmp[:, i % 2, :], m.xt, gain_col=cols[:, 0, :], bias_col=cols[:, 1, :])
        attn = sb(nc, ctx, "mixer_attn", [P, T, D])
        with ExitStack() as c2:
            qt = sb(nc, c2, "mixer_q", [128, KB, N])
            kt = sb(nc, c2, "mixer_k", [128, KB, N])
            v = sb(nc, c2, "mixer_v", [P, T, HEADS, 65])
            with ExitStack() as c3:
                w = sb(nc, c3, "mixer_wqkv", [128, KB, 3 * D])
                bqk = sb(nc, c3, "mixer_bqk", [128, 12])
                bv = sb(nc, c3, "mixer_bv", [P, 3 * D])

                def products(n, bank):
                    if n < 24:
                        f, (c0, cn) = n // 3, CH[n % 3]
                        return [(bank[:, 0:cn], w[:, k, f * 128:(f + 1) * 128], m.xt[:, k, c0:c0 + cn]) for k in range(KB)]
                    return [(bank[0:P, :], m.xt[:, k, tile(n - 24)], w[:, k, 2 * D:3 * D]) for k in range(KB)]

                def take(n, dve, bank):
                    if n < 24:
                        f, (c0, cn) = n // 3, CH[n % 3]
                        dst = qt if f < 4 else kt
                        return dve.tensor_scalar(dst[:, f % 4, c0:c0 + cn], bank[:, 0:cn], bqk[:, f:f + 1], None, ALU.add)
                    return dve.tensor_tensor(v[:, n - 24, :, 0:64], bank[0:P, :].rearrange("p (h c) -> p h c", h=HEADS),
                                             bv[:, 2 * D:3 * D].rearrange("p (h c) -> p h c", h=HEADS), ALU.add)

                move(nc, [(bqk[:, :], a["L1_mix_bqk"]), (bv[:, :], spread_row(a["L1_mix_bqkv"])), (w[:, :, :], wview(a["L1_mix_Wqkv"]))])
                vector_groups_phase(nc, m, 24 + T, products, take)
                with phase(nc, "filled") as (block, filled):
                    @block.vector
                    def _(dve):
                        dve.memset(v[:, :, :, 64:65], 1.0).then_inc(filled, 1)
            pm = sb(nc, c2, "mixer_pmat", [128, F])
            kvs = sb(nc, c2, "mixer_kv", [128, HEADS, 2, 65])
            nm = sb(nc, c2, "mixer_neg_max", [P, 4])
            feat = sb(nc, c2, "mixer_features", [P, 3, F])
            feat_t = sb(nc, c2, "mixer_features_t", [128, 2, 2, P])
            inv = sb(nc, c2, "mixer_inverse", [P, 4])
            NU = HEADS * T
            with phase(nc, "loaded", "product", "maxed", "expd", "added", "taken", "shifted") as (
                    block, loaded, product, maxed, expd, added, taken, shifted):
                @block.sync
                def _(sp):
                    for h in range(2):
                        sp.dma_start(pm[head(h), :], a["L1_mix_Pmat"]).then_inc(loaded, 16)

                @block.tensor
                def _(pe):
                    def sums(n):
                        h, i = n // T, n % T
                        if i == 0 and h >= 2:
                            pe.wait_ge(taken, h - 1)
                        pe.wait_ge(expd, n + 1)
                        for f in range(2):
                            ins = pe.matmul(m.ps[:, 4 + h % 2, 65 * f:65 * f + 65], feat[:, n % 3, f * 128:(f + 1) * 128], v[:, i, h, :],
                                            start=i == 0 and f == 0, stop=i == T - 1, skip_group_check=True)
                        ins.then_inc(added, 1)

                    pe.wait_ge(loaded, 32)
                    for n in range(NU + 2):
                        if n < NU:
                            h, i = n // T, n % T
                            if n >= 4:
                                pe.wait_ge(expd, n - 3)
                            pe.matmul(m.ps[0:P, n % 4, 0:F], kt[head(h), h // 2, tile(i)], pm[head(h), :], start=True, stop=True).then_inc(product, 1)
                        if n >= 2:
                            sums(n - 2)

                @block.vector
                def _(dve):
                    def take(h):
                        dve.wait_ge(added, T * (h + 1))
                        dve.tensor_scalar(kvs[:, h, :, :], m.ps[:, 4 + h % 2, 0:130].rearrange("p (f c) -> p f c", f=2),
                                          F ** -0.5, None, ALU.mult).then_inc(taken, 1)

                    for n in range(NU):
                        dve.wait_ge(product, n + 1)
                        if n >= 4:
                            dve.wait_ge(expd, n - 3)
                        dve.tensor_reduce(nm[:, n % 4:n % 4 + 1], m.ps[0:P, n % 4, 0:F], AX.X, ALU.max, negate=True).then_inc(maxed, 1)
                        if n % T == 4 and n > T:
                            take(n // T - 1)
                    take(HEADS - 1)
                    dve.wait_ge(taken, HEADS)
                    dve.tensor_scalar(kvs[:, :, :, 64:65], kvs[:, :, :, 64:65], 1e-6, None, ALU.add).then_inc(shifted, 1)

                @block.scalar
                def _(act):
                    for n in range(NU):
                        act.wait_ge(maxed, n + 1)
                        if n >= 3:
                            act.wait_ge(added, n - 2)
                        act.activation(feat[:, n % 3, :], m.ps[0:P, n % 4, 0:F], ACT.Exp, bias=nm[:, n % 4:n % 4 + 1]).then_inc(expd, 1)

            with phase(nc, "product", "maxed", "expd", "turned", "kept", "out", "inverted", "done") as (
                    block, product, maxed, expd, turned, kept, out, inverted, done):
                @block.tensor
                def _(pe):
                    for n in range(NU + 4):
                        if n < NU:
                            h, i = n // T, n % T
                            if n >= 4:
                                pe.wait_ge(expd, n - 3)
                            pe.matmul(m.ps[0:P, n % 4, 0:F], qt[head(h), h // 2, tile(i)], pm[head(h), :], start=True, stop=True).then_inc(product, 1)
                        if 2 <= n < NU + 2:
                            u = n - 2
                            pe.wait_ge(expd, u + 1)
                            if u >= 2:
                                pe.wait_ge(kept, u - 1)
                            for f in range(2):
                                ins = pe.transpose(m.ps[:, 4 + u % 2, f * P:(f + 1) * P], feat[:, u % 3, f * 128:(f + 1) * 128], m.ident[0:P, 0:P])
                            ins.then_inc(turned, 1)
                        if n >= 4:
                            u = n - 4
                            pe.wait_ge(kept, u + 1)
                            if u >= 2:
                                pe.wait_ge(done, u - 1)
                            for f in range(2):
                                ins = pe.matmul(m.ps[0:P, 6 + u % 2, 0:65], feat_t[:, u % 2, f, :], kvs[:, u // T, f, :], start=f == 0, stop=f == 1)
                            ins.then_inc(out, 1)

                @block.vector
                def _(dve):
                    def finish(u):
                        h, i = u // T, u % T
                        dve.wait_ge(out, u + 1)
                        dve.reciprocal(inv[:, u % 4:u % 4 + 1], m.ps[0:P, 6 + u % 2, 64:65]).then_inc(inverted, 1)
                        dve.wait_ge(inverted, u + 1)
                        dve.tensor_scalar(attn[:, i, 64 * h:64 * h + 64], m.ps[0:P, 6 + u % 2, 0:64], inv[:, u % 4:u % 4 + 1], None,
                                          ALU.mult).then_inc(done, 1)

                    for n in range(NU + 4):
                        if n < NU:
                            dve.wait_ge(product, n + 1)
                            if n >= 4:
                                dve.wait_ge(expd, n - 3)
                            dve.tensor_reduce(nm[:, n % 4:n % 4 + 1], m.ps[0:P, n % 4, 0:F], AX.X, ALU.max, negate=True).then_inc(maxed, 1)
                        if n >= 4:
                            finish(n - 4)

                @block.scalar
                def _(act):
                    for n in range(NU + 2):
                        if n < NU:
                            act.wait_ge(maxed, n + 1)
                            if n >= 3:
                                act.wait_ge(turned, n - 2)
                            act.activation(feat[:, n % 3, :], m.ps[0:P, n % 4, 0:F], ACT.Exp, bias=nm[:, n % 4:n % 4 + 1]).then_inc(expd, 1)
                        if n >= 2:
                            u = n - 2
                            act.wait_ge(turned, u + 1)
                            if u >= 2:
                                act.wait_ge(out, u - 1)
                            act.activation(feat_t[:, u % 2, :, :], m.ps[:, 4 + u % 2, 0:2 * P].rearrange("p (f t) -> p f t", f=2),
                                           ACT.Copy).then_inc(kept, 1)

        transpose_rows_phase(nc, m, attn, m.xt)
        wp = sb(nc, ctx, "mixer_wproj", [128, KB, D])
        w1 = sb(nc, ctx, "mixer_w1", [128, KB, H2])
        w2 = sb(nc, ctx, "mixer_w2", [128, H2 // 128, D])
        b1 = sb(nc, ctx, "mixer_b1", [128, H2 // 128])
        rows = sb(nc, ctx, "mixer_rows", [P, 2, D])
        hid = sb(nc, ctx, "mixer_hidden", [128, H2 // 128, N])
        vector_groups_phase(nc, m, T, lambda n, bank: [(bank[0:P, :], m.xt[:, k, tile(n)], wp[:, k, :]) for k in range(KB)],
                            lambda n, dve, bank: dve.tensor_tensor(m.x[:, n, :], bank[0:P, :], m.x[:, n, :], ALU.add),
                            loads=[(wp[:, :, :], wview(a["L1_mix_Wproj"]))])
        move(nc, [(w1[:, :, :], wview(a["L1_mix_W1"])), (w2[:, :, :], wview(a["L1_mix_W2"])), (b1[:, :], a["L1_mix_b1"]),
                  (rows[:, 0, :], spread_row(a["L1_mix_bproj"])), (rows[:, 1, :], spread_row(a["L1_mix_b2"]))])
        add_rows(nc, m, rows[:, 0, :])
        layernorm_phase(nc, m, m.x, lambda i: m.tmp[:, i % 2, :], m.xt, gain_col=cols[:, 2, :], bias_col=cols[:, 3, :])

        with phase(nc, "product", "taken") as (block, product, taken):
            NG = H2 // 128 * 3

            @block.tensor
            def _(pe):
                for n in range(NG):
                    f, (c0, cn) = n // 3, CH[n % 3]
                    if n >= 8:
                        pe.wait_ge(taken, n - 7)
                    for k in range(KB):
                        ins = pe.matmul(m.ps[:, n % 8, 0:cn], w1[:, k, f * 128:(f + 1) * 128], m.xt[:, k, c0:c0 + cn], start=k == 0, stop=k == KB - 1)
                    ins.then_inc(product, 1)

            @block.scalar
            def _(act):
                for n in range(NG):
                    f, (c0, cn) = n // 3, CH[n % 3]
                    act.wait_ge(product, n + 1)
                    act.activation(hid[:, f, c0:c0 + cn], m.ps[:, n % 8, 0:cn], ACT.Gelu, bias=b1[:, f:f + 1]).then_inc(taken, 1)

        vector_groups_phase(nc, m, T, lambda n, bank: [(bank[0:P, :], hid[:, k, tile(n)], w2[:, k, :]) for k in range(H2 // 128)],
                            lambda n, dve, bank: dve.tensor_tensor(m.x[:, n, :], bank[0:P, :], m.x[:, n, :], ALU.add))
        add_rows(nc, m, rows[:, 1, :])
        add_into_saved(nc, m, a, tok, attn)


def transpose_rows_phase(nc, m, src, dst):
    with phase(nc, "turned", "kept") as (block, turned, kept):
        @block.tensor
        def _(pe):
            for i in range(T):
                if i >= 4:
                    pe.wait_ge(kept, i - 3)
                for k in range(KB):
                    ins = pe.transpose(m.ps[:, i % 4, k * P:(k + 1) * P], src[:, i, k * 128:(k + 1) * 128], m.ident[0:P, 0:P])
                ins.then_inc(turned, 1)

        @block.scalar
        def _(act):
            for i in range(T):
                act.wait_ge(turned, i + 1)
                act.activation(dst[:, :, tile(i)], m.ps[:, i % 4, 0:KB * P].rearrange("p (k t) -> p k t", k=KB), ACT.Copy).then_inc(kept, 1)



def l1_ffn(nc, m, a, tok):
    L, NE, H = 4, 8, 256
    with ExitStack() as ctx:
        y = sb(nc, ctx, "y", [P, T, D])
        layernorm_phase(nc, m, m.x, lambda i: y[:, i, :])
        xs, m.x = m.x, y
        cols = sb(nc, ctx, "ln_cols", [128, 4, KB])
        rows = sb(nc, ctx, "row", [P, D])
        with nc.Fori(0, L) as l:
            at = lambda v, pat="a p k -> (a p) k": v[bass.ds(l, 1)].rearrange(pat)
            move(nc, [(cols[:, j, :], at(c)) for j, c in enumerate((a["L1_ffn_ln1_w"], a["L1_ffn_ln1_b"], a["L1_ffn_ln2_w"], a["L1_ffn_ln2_b"]))]
                 + [(rows[:, :], a["L1_ffn_out_b"][bass.ds(l, 1), :].to_broadcast([P, D]))])
            layernorm_phase(nc, m, m.x, lambda i: m.tmp[:, i % 2, :], m.xt, gain_col=cols[:, 0, :], bias_col=cols[:, 1, :])
            with ExitStack() as c2:
                qt = sb(nc, c2, "ffn_qt", [128, KB, N])
                kt = sb(nc, c2, "ffn_kt", [128, KB, N])
                v = sb(nc, c2, "ffn_v", [P, T, KB, 192])
                ones_between(nc, v)
                with ExitStack() as c3:
                    w = sb(nc, c3, "ffn_wqkv", [128, KB, 3 * D])
                    qkv_for_attention(nc, m, w, lambda k: w[:, k, 0:D], lambda k: w[:, k, D:2 * D], lambda k: w[:, k, 2 * D:3 * D],
                                      qt, kt, v, [(w[:, :, :], a["L1_ffn_qkv_w"][bass.ds(l, 1)].rearrange("a (k p) f -> p (a k) f", p=128))])
                attention(nc, m, "ffn_", qt, kt, v, m.xt)
            with ExitStack() as c2:
                wo = sb(nc, c2, "wo", [128, KB, D])
                vector_groups_phase(nc, m, T, lambda n, bank: [(bank[0:P, :], m.xt[:, k, tile(n)], wo[:, k, :]) for k in range(KB)],
                                    lambda n, dve, bank: dve.tensor_tensor(m.x[:, n, :], bank[0:P, :], m.x[:, n, :], ALU.add),
                                    loads=[(wo[:, :, :], a["L1_ffn_out_w"][bass.ds(l, 1)].rearrange("a (k p) f -> p (a k) f", p=128))])
                add_rows(nc, m, rows)
                layernorm_phase(nc, m, m.x, lambda i: m.tmp[:, i % 2, :], m.xt, gain_col=cols[:, 2, :], bias_col=cols[:, 3, :])
                moe(nc, m, a, l, c2, NE, H)
        row2 = sb(nc, ctx, "final_rows", [P, 2, D])
        layernorm_phase(nc, m, m.x, lambda i: m.xt_rows[:, i, :], None, gain_row=row2[:, 0, :], bias_row=row2[:, 1, :],
                        loads=[(row2[:, 0, :], spread_row(a["L1_ffn_fln_w"])), (row2[:, 1, :], spread_row(a["L1_ffn_fln_b"]))])
        with phase(nc, "added", "stored") as (block, added, stored):
            @block.vector
            def _(dve):
                for i in range(T):
                    dve.tensor_tensor(xs[:, i, :], xs[:, i, :], m.xt_rows[:, i, :], ALU.add).then_inc(added, 1)

            @block.sync
            def _(sp):
                out = tok(a["out"])
                for i in range(T):
                    sp.wait_ge(added, i + 1)
                    sp.dma_start(out[:, i, :], xs[:, i, :]).then_inc(stored, 16)
                sp.wait_ge(stored, 16 * T)


def moe(nc, m, a, l, ctx, NE, H):
    wg = sb(nc, ctx, "ffn_w_gate", [128, KB, NE])
    logit = sb(nc, ctx, "logits", [P, T, 2 * NE])
    struck = sb(nc, ctx, "struck", [P, T, 2 * NE])
    best = sb(nc, ctx, "top", [P, T, 8])
    only2 = sb(nc, ctx, "top2", [P, T, 8])
    d = sb(nc, ctx, "logit_shifted", [P, T, NE])
    e = sb(nc, ctx, "logit_exp", [P, T, NE])
    eg = sb(nc, ctx, "chosen_exp", [P, T, NE])
    den = sb(nc, ctx, "gate_sum", [P, T])
    inv = sb(nc, ctx, "gate_inv", [P, T])
    gates = sb(nc, ctx, "moe_gates", [P, T, NE])
    gates_t = sb(nc, ctx, "gates_t", [NE, N])
    eb1 = sb(nc, ctx, "eb1", [128, 2, H // 128])
    eb2 = sb(nc, ctx, "eb2", [NE, D])
    by_token = lambda ap: ap.rearrange("p (t a) -> p t a", a=1).to_broadcast([P, T, NE])
    with phase(nc, "loaded", "filled", "product", "taken", "maxed", "two", "strike", "v_step", "a_step", "t_step") as (
            block, loaded, filled, product, taken, maxed, two, strike, v_step, a_step, t_step):
        @block.sync
        def _(sp):
            sp.dma_start(wg[:, :, :], a["L1_ffn_w_gate"][bass.ds(l, 1)].rearrange("a (k p) f -> p (a k) f", p=128)).then_inc(loaded, 16)
            sp.dma_start(eb2[:, :], a["L1_ffn_eb2"][bass.ds(l, 1)].rearrange("a e f -> (a e) f")).then_inc(loaded, 16)

        @block.tensor
        def _(pe):
            pe.wait_ge(loaded, 32)
            for i in range(T):
                if i >= 4:
                    pe.wait_ge(taken, i - 3)
                for k in range(KB):
                    ins = pe.matmul(m.ps[0:P, i % 4, 0:NE], m.xt[:, k, tile(i)], wg[:, k, :], start=k == 0, stop=k == KB - 1)
                ins.then_inc(product, 1)
            pe.wait_ge(v_step, 5)
            for i in range(T):
                ins = pe.transpose(m.ps[0:NE, 4 + i // 4, (i % 4) * P:(i % 4 + 1) * P], gates[:, i, :], m.ident[0:P, 0:P])
            ins.then_inc(t_step, 1)

        @block.vector
        def _(dve):
            dve.memset(logit[:, :, NE:2 * NE], -BIG).then_inc(filled, 1)
            dve.memset(only2[:, :, :], -BIG).then_inc(filled, 1)
            for i in range(T):
                dve.wait_ge(product, i + 1)
                dve.tensor_copy(logit[:, i, 0:NE], m.ps[0:P, i % 4, 0:NE]).then_inc(taken, 1)
            dve.wait_ge(filled, 2)
            for i in range(T):
                dve.wait_ge(taken, i + 1)
                dve.max(best[:, i, :], logit[:, i, :]).then_inc(maxed, 1)
            dve.wait_ge(maxed, T)
            dve.tensor_copy(only2[:, :, 0:2], best[:, :, 0:2]).then_inc(two, 1)
            dve.tensor_tensor(d[:, :, :], logit[:, :, 0:NE], best[:, :, 0:1].to_broadcast([P, T, NE]), ALU.subtract).then_inc(v_step, 1)
            dve.wait_ge(two, 1)
            for i in range(T):
                dve.match_replace(struck[:, i, :], only2[:, i, :], logit[:, i, :], BIG).then_inc(strike, 1)
            dve.wait_ge(strike, T)
            dve.wait_ge(a_step, 1)
            dve.scalar_tensor_tensor(eg[:, :, :], struck[:, :, 0:NE], BIG, e[:, :, :], ALU.is_equal, ALU.mult).then_inc(v_step, 1)
            dve.wait_ge(v_step, 2)
            dve.tensor_reduce(den[:, :], eg[:, :, :], AX.X, ALU.add).then_inc(v_step, 1)
            dve.wait_ge(v_step, 3)
            dve.reciprocal(inv[:, :], den[:, :]).then_inc(v_step, 1)
            dve.wait_ge(v_step, 4)
            dve.tensor_tensor(gates[:, :, :], eg[:, :, :], by_token(inv[:, :]), ALU.mult).then_inc(v_step, 1)

        @block.scalar
        def _(act):
            act.wait_ge(v_step, 1)
            act.activation(e[:, :, :], d[:, :, :], ACT.Exp).then_inc(a_step, 1)
            act.wait_ge(t_step, 1)
            for c0, cn in CH:
                ins = act.activation(gates_t[:, c0:c0 + cn], m.ps[0:NE, 4 + c0 // 500, 0:cn], ACT.Copy)
            ins.then_inc(a_step, 1)

    vector_groups_phase(nc, m, T, lambda n, bank: [(bank[0:P, :], gates_t[:, tile(n)], eb2[:, :])],
                        lambda n, dve, bank: dve.tensor_tensor(m.x[:, n, :], bank[0:P, :], m.x[:, n, :], ALU.add))

    w1 = sb(nc, ctx, "ew1", [128, 2, KB, H])
    w2 = sb(nc, ctx, "ew2", [128, 2, H // 128, D])
    hid = sb(nc, ctx, "expert_hidden", [128, 2, H // 128, N])
    FB = H // 128
    NG = 3 * FB
    SLOTS = 5
    w1_all = a["L1_ffn_ew1"].rearrange("l e (k p) f -> (l e) p k f", p=128)
    eb1_all = a["L1_ffn_eb1"].rearrange("l e p k -> (l e) p k")
    w2_all = a["L1_ffn_ew2"].rearrange("l e (k p) f -> (l e) p k f", p=128)
    with phase(nc, "w_a", "w_b", "h_product", "h_taken", "y_product", "y_taken") as (block, w_a, w_b, h_product, h_taken, y_product, y_taken):
        loaded = (w_a, w_b)

        @block.sync
        def _(sp):
            def load(expert, c):
                for dst, src in ((w1, w1_all), (w2, w2_all)):
                    sp.dma_start(dst[:, c, :, :], src[bass.ds(expert, 1)].rearrange("a p k f -> (a p) k f")).then_inc(loaded[c], 16)
                sp.dma_start(eb1[:, c, :], eb1_all[bass.ds(expert, 1)].rearrange("a p k -> (a p) k")).then_inc(loaded[c], 16)

            for c in range(2):
                load(l * NE + c, c)
            with sp.Fori(0, NE // 2 - 1) as it:
                for c in range(2):
                    sp.wait_ge(y_product, 2 * T * it + T * (c + 1))
                    load(l * NE + 2 * it + 2 + c, c)

        @block.tensor
        def _(pe):
            with pe.Fori(0, NE // 2) as it:
                for c in range(2):
                    pe.wait_ge(loaded[c], 48 * it + 48)
                    for g in range(NG):
                        f, (c0, cn) = g % FB, CH[g // FB]
                        pe.wait_ge(h_taken, 2 * NG * it + NG * c + g + 1)
                        for k in range(KB):
                            ins = pe.matmul(m.ps[:, g % 3, 0:cn], w1[:, c, k, f * 128:(f + 1) * 128], m.xt[:, k, c0:c0 + cn],
                                            start=k == 0, stop=k == KB - 1)
                        ins.then_inc(h_product, 1)
                    for i in range(T):
                        n = T * c + i
                        pe.wait_ge(h_taken, 2 * NG * it + NG * c + FB * (i // 4 + 1) + 3)
                        pe.wait_ge(y_taken, 2 * T * it + n + 1 - SLOTS + T)
                        for k in range(FB):
                            ins = pe.matmul(m.ps[0:P, 3 + n % SLOTS, :], hid[:, c, k, tile(i)], w2[:, c, k, :], start=k == 0, stop=k == FB - 1)
                        ins.then_inc(y_product, 1)

        @block.scalar
        def _(act):
            act.sem_inc(h_taken, 3)
            with act.Fori(0, NE // 2) as it:
                for c in range(2):
                    act.wait_ge(loaded[c], 48 * it + 48)
                    for g in range(NG):
                        f, (c0, cn) = g % FB, CH[g // FB]
                        act.wait_ge(h_product, 2 * NG * it + NG * c + g + 1)
                        act.activation(hid[:, c, f, c0:c0 + cn], m.ps[:, g % 3, 0:cn], ACT.Gelu,
                                       bias=eb1[:, c, f:f + 1]).then_inc(h_taken, 1)

        @block.vector
        def _(dve):
            dve.sem_inc(y_taken, T)
            with dve.Fori(0, NE // 2) as it:
                for c in range(2):
                    for i in range(T):
                        n = T * c + i
                        dve.wait_ge(y_product, 2 * T * it + n + 1)
                        dve.wait_ge(y_taken, 2 * T * it + n + 1)
                        dve.scalar_tensor_tensor(m.x[:, i, :], m.ps[0:P, 3 + n % SLOTS, :], gates[:, i, bass.ds(2 * it + c, 1)], m.x[:, i, :],
                                                 ALU.mult, ALU.add).then_inc(y_taken, 1)



def program(nc, a, stop=None):
    ctx = ExitStack()
    with ctx:
        m = Tensors()
        m.ps = ctx.enter_context(nc.psum_tensor("ps", [128, 8, 512], F32))
        m.gathered = [ctx.enter_context(nc.semaphore(f"gathered{u}")) for u in range(2 * G)]
        m.ident = sb(nc, ctx, "ident", [128, 128])
        m.eps = sb(nc, ctx, "eps", [128, 1])
        m.ones = sb(nc, ctx, "ones", [128, 128])
        m.xraw = sb(nc, ctx, "x", [128, T * D])
        m.x = m.xraw[0:P, :].rearrange("p (t d) -> p t d", t=T)
        xt_raw = sb(nc, ctx, "xt", [128, T * D])
        m.xt = xt_raw[:, 0:KB * N].rearrange("p (k n) -> p k n", k=KB)
        m.xt_rows = xt_raw[0:P, :].rearrange("p (t d) -> p t d", t=T)
        m.bn = sb(nc, ctx, "bn", [P, T, 6])
        m.mv = sb(nc, ctx, "mv", [P, T, 2])
        m.sd = sb(nc, ctx, "sd", [P, T])
        m.rstd = sb(nc, ctx, "rstd", [P, T])
        m.tmp4 = sb(nc, ctx, "tmp", [P, 4, D])
        m.tmp = m.tmp4[:, 0:2, :]
        m.tmp2 = m.tmp4[:, 2:4, :]
        tok = lambda v: v.rearrange("(t p) d -> p t d", p=P)
        ring = lambda i: m.tmp[:, i % 2, :]

        with phase(nc, "made", "loaded") as (block, made, loaded):
            @block.gpsimd
            def _(pool):
                pool.memset(m.ident[:, :], 0.0).then_inc(made, 1)
                pool.memset(m.eps[:, :], EPS).then_inc(made, 1)
                pool.memset(m.ones[:, :], 1.0)
                pool.wait_ge(made, 2)
                pool.affine_select(out=m.ident[:, :], in_=m.ident[:, :], compare_op=ALU.not_equal, fill=1.0,
                                   base=0, pattern=[[-1, 128]], channel_multiplier=1).then_inc(made, 1)

            @block.sync
            def _(sp):
                sp.dma_start(m.x[:, :, :], tok(a["x"])).then_inc(loaded, 16)
                sp.wait_ge(loaded, 16)

        cctx = ctx.enter_context(ExitStack())
        m.cnt = sb(nc, cctx, "cnt", [P, T, NPAD])
        l0_gnn(nc, m, a, tok, ring)
        if stop == "gnn0":
            return
        l0_mix(nc, m, a)
        if stop == "mix0":
            return
        l0_ffn(nc, m, a)
        if stop == "ffn0":
            return
        l1_gnn(nc, m, a, tok)
        cctx.close()
        if stop == "gnn1":
            return
        l1_mix(nc, m, a, tok)
        if stop == "mix1":
            return
        l1_ffn(nc, m, a, tok)


def l0_gnn(nc, m, a, tok, ring):
    with ExitStack() as ctx:
        m.acc = sb(nc, ctx, "acc", [128, 8, NPAD])
        with ExitStack() as c2:
            up = sb(nc, c2, "w_up", [128, 2, MUL])
            res = sb(nc, c2, "up_rows", [P, 2, D])
            by_channel = lambda ap, k: ap[:, 0:128] if k == 0 else ap[:, 128 + k - 1:512:3]
            layernorm_phase(nc, m, m.x, ring, m.xt, cols=by_channel)

            def operands(n, bank):
                return [(bank[0:P, k * 128:(k + 1) * 128], m.xt[:, k, tile(n)], up[:, min(k, 1), :]) for k in range(KB)]

            with phase(nc, "loaded", "product", "taken", "st_a", "st_b") as (block, loaded, product, taken, st_a, st_b):
                stored = (st_a, st_b)

                @block.sync
                def _(sp):
                    sp.dma_start(up[:, 0, :], a["L0_gnn_W_up0"]).then_inc(loaded, 16)
                    sp.dma_start(up[:, 1, :], a["L0_gnn_W_up1"]).then_inc(loaded, 16)
                    for i in range(T):
                        sp.wait_ge(taken, i + 1)
                        sp.dma_start(a["xup"][tile(i), :], res[:, i % 2, :]).then_inc(stored[i % 2], 16)
                    for s in stored:
                        sp.wait_ge(s, 16 * T // 2)

                @block.tensor
                def _(pe):
                    pe.wait_ge(loaded, 32)
                    for i in range(T):
                        if i >= 8:
                            pe.wait_ge(taken, i - 7)
                        for out, lhsT, rhs in operands(i, m.ps[:, i % 8, :]):
                            ins = pe.matmul(out, lhsT, rhs, start=True, stop=True)
                        ins.then_inc(product, 1)

                @block.scalar
                def _(act):
                    for i in range(T):
                        act.wait_ge(product, i + 1)
                        if i >= 2:
                            act.wait_ge(stored[i % 2], 16 * (i // 2))
                        act.activation(res[:, i % 2, :], m.ps[0:P, i % 8, :], ACT.Copy, scale=MUL ** -0.5).then_inc(taken, 1)

        edge_mlp_phase(nc, m, None, a["ef_t"], a["L0_gnn_W_mlp1"], a["L0_gnn_W_mlp2"], a["L0_gnn_W_mlp3"], a["h3"])
        with ExitStack() as c2:
            m.iota = sb(nc, c2, "iota", [P, N])
            with phase(nc, "made") as (block, made):
                @block.gpsimd
                def _(pool):
                    pool.iota(m.iota[:, :], pattern=[[1, N]], base=0, channel_multiplier=0,
                              allow_small_or_imprecise_dtypes=True).then_inc(made, 1)
            edges(nc, m, a, c2)
        with ExitStack() as c2:
            wo = sb(nc, c2, "w_out", [128, 2, 2, MUL])

            def operands(n, bank):
                t = tile(n)
                blocks = [(4, 3, 0)] + [(k, 5 + k, 1) for k in range(3)]
                out = []
                for k in range(4):
                    first, second = (3, 4) if k == 0 else (k - 1, 4 + k)
                    for j, blk in enumerate((first, second)):
                        out.append((k, j, m.acc[:, blk, t], wo[:, min(k, 1), j, :]))
                return out

            with phase(nc, "loaded", "product", "taken") as (block, loaded, product, taken):
                @block.sync
                def _(sp):
                    for k, w in enumerate((a["L0_gnn_W_out0"], a["L0_gnn_W_out1"])):
                        sp.dma_start(wo[:, k, :, :], wview(w)).then_inc(loaded, 16)

                @block.tensor
                def _(pe):
                    pe.wait_ge(loaded, 32)
                    for i in range(T):
                        if i >= 8:
                            pe.wait_ge(taken, i - 7)
                        for k, j, lhsT, rhs in operands(i, None):
                            ins = pe.matmul(m.ps[0:P, i % 8, k * 128:(k + 1) * 128], lhsT, rhs, start=j == 0, stop=j == 1)
                        ins.then_inc(product, 1)

                @block.vector
                def _(dve):
                    scale = (2 * MUL) ** -0.5 / 10.0
                    for i in range(T):
                        dve.wait_ge(product, i + 1)
                        dve.scalar_tensor_tensor(m.x[:, i, 0:128], m.ps[0:P, i % 8, 0:128], scale, m.x[:, i, 0:128], ALU.mult, ALU.add)
                        vec = m.x[:, i, 128:512].rearrange("p (v k) -> p k v", k=3)
                        dve.scalar_tensor_tensor(vec, m.ps[0:P, i % 8, 128:512].rearrange("p (k v) -> p k v", k=3),
                                                 scale, vec, ALU.mult, ALU.add).then_inc(taken, 1)



COLUMNS = ("L0_mix_b_in", "L1_gnn_b1", "L1_mix_b1", "L1_mix_g1", "L1_mix_be1", "L1_mix_g2", "L1_mix_be2",
           "L1_ffn_ln1_w", "L1_ffn_ln1_b", "L1_ffn_ln2_w", "L1_ffn_ln2_b", "L1_ffn_eb1")


def layouts(inputs):
    import numpy as np
    out = {}
    for k, v in inputs.items():
        out[k] = np.asarray(v)
    by_super = lambda v: np.ascontiguousarray(np.asarray(v).reshape(SB, P, G, -1).transpose(1, 0, 2, 3))
    out["src_l"] = by_super(out.pop("src"))[..., 0].copy()
    out["dst_l"] = by_super(out.pop("dst"))[..., 0].copy()
    out["ea4_l"] = by_super(out.pop("edge_attr_4"))
    ef = out.pop("edge_attr_8").reshape(SB, P, G, 8)
    out["ef_t"] = np.ascontiguousarray(ef.transpose(3, 0, 2, 1).reshape(8, E))
    w = out["L0_mix_W_in"]
    out["L0_mix_W_in"] = np.concatenate([w[:MUL]] + [w[MUL + k::3] for k in range(3)])
    out["L1_mix_bqk"] = np.ascontiguousarray(out["L1_mix_bqkv"].reshape(12, 128).T)
    for k, v in list(out.items()):
        if k in COLUMNS:
            out[k] = np.ascontiguousarray(np.moveaxis(v.reshape(v.shape[:-1] + (-1, 128)), -1, -2))
    return out


def build(nc, arrays, stop=None):
    from concourse import mybir as _mybir
    a = {name: nc.dram_tensor(f"in_{name}", v.shape, _mybir.dt.from_np(v.dtype), kind="ExternalInput").ap()
         for name, v in arrays.items()}
    a["out"] = nc.dram_tensor("out", (N, D), F32, kind="ExternalOutput").ap()
    a["xs"] = nc.dram_tensor("xs", (N, D), F32).ap()
    a["xn"] = nc.dram_tensor("xn", (N, D), F32).ap()
    a["xup"] = nc.dram_tensor("xup", (N, D), F32).ap()
    a["h3"] = nc.dram_tensor("h3", (HID, E), F32).ap()
    program(nc, a, stop)


def kernel(**inputs):
    import concourse.bacc as _bacc
    from concourse.bass_utils import run_bass_kernel_spmd as _run
    nc = _bacc.Bacc("TRN2", target_bir_lowering=False, num_devices=1)
    arrays = layouts(inputs)
    build(nc, arrays)
    r = _run(nc, [{f"in_{k}": v for k, v in arrays.items()}], core_ids=[0])
    return r.results[0]["out"]
```

```python
from contextlib import ExitStack, contextmanager

import concourse.bass as bass
from concourse import mybir

F32 = mybir.dt.float32
F32R = mybir.dt.float32r
BF16 = mybir.dt.bfloat16
I32 = mybir.dt.int32
U32 = mybir.dt.uint32
ALU = mybir.AluOpType
ACT = mybir.ActivationFunctionType
AX = mybir.AxisListType
RMAX = bass.bass_isa.ReduceOp.max

N, D = 1250, 512
P, T = 125, 10
KB = D // 128
E = 21250
G = 5
SB = E // (P * G)
W = 64
NPAD = N + W
MUL = 128
HID = 64
HEADS, DH = 8, 64
SILU_2MOM = 1.679177
CH = [(0, 500), (500, 500), (1000, 250)]
EPS = 1e-5
BIG = 3.0e38


class Tensors:
    pass


@contextmanager
def phase(nc, *names, drain_pool=True, held=()):
    with ExitStack() as ctx:
        sems = [ctx.enter_context(nc.semaphore(n)) for n in names]
        with nc.Block(no_gpsimd_drain=not drain_pool) as block:
            yield (block, *sems)
        for s in sems:
            nc.sync.sem_clear(s)
        if held:
            nc.gpsimd.dma_reset(range(held[0].num, held[-1].num + 1))
            for s in held:
                nc.gpsimd.sem_clear(s)
        nc.all_engine_barrier()


def sb(nc, ctx, name, shape, dt=F32):
    return ctx.enter_context(nc.sbuf_tensor(name, shape, dt))


def tile(i):
    return slice(i * P, (i + 1) * P)



def load_phase(nc, pairs):
    with phase(nc, "loaded") as (block, loaded):
        @block.sync
        def _(sp):
            for dst, src in pairs:
                sp.dma_start(dst, src).then_inc(loaded, 16)
            sp.wait_ge(loaded, 16 * len(pairs))


def layernorm_phase(nc, m, src, normed, transposed=None, cols=None, gain_col=None, bias_col=None,
                    gain_row=None, bias_row=None, loads=()):
    cols = cols or (lambda ap, k: ap[:, k * 128:(k + 1) * 128])
    with phase(nc, "loaded", "stats", "moments", "spread", "inverse", "centred", "scaled", "ready",
               "turned", "kept") as (block, loaded, stats, moments, spread, inverse, centred, scaled,
                                     ready, turned, kept):
        @block.sync
        def _(sp):
            for dst, s in loads:
                sp.dma_start(dst, s).then_inc(loaded, 16)

        @block.vector
        def _(dve):
            for i in range(T):
                dve.bn_stats(m.bn[:, i, :], src[:, i, :]).then_inc(stats, 1)
            for i in range(T):
                dve.wait_ge(stats, i + 1)
                dve.bn_aggr(m.mv[:, i, :], m.bn[:, i, :]).then_inc(moments, 1)
            dve.wait_ge(spread, 1)
            dve.reciprocal(m.rstd[:, :], m.sd[:, :]).then_inc(inverse, 1)
            dve.wait_ge(inverse, 1)
            for i in range(T):
                if transposed is not None and i >= 2:
                    dve.wait_ge(turned, i - 1)
                out = normed(i) if gain_row is None else m.tmp[:, i % 2, :]
                if gain_row is not None and i >= 2:
                    dve.wait_ge(scaled, i - 1)
                ins = dve.tensor_scalar(out, src[:, i, :], m.mv[:, i, 0:1], m.rstd[:, i:i + 1],
                                        ALU.subtract, ALU.mult)
                if gain_row is None:
                    ins.then_inc(ready, 1)
                    continue
                ins.then_inc(centred, 1)
                dve.wait_ge(centred, i + 1)
                if i == 0:
                    dve.wait_ge(loaded, 16 * len(loads))
                dve.tensor_tensor(m.tmp2[:, i % 2, :], m.tmp[:, i % 2, :], gain_row, ALU.mult).then_inc(scaled, 1)
                dve.wait_ge(scaled, i + 1)
                dve.tensor_tensor(normed(i), m.tmp2[:, i % 2, :], bias_row, ALU.add).then_inc(ready, 1)

        @block.tensor
        def _(pe):
            if transposed is None:
                return
            for i in range(T):
                pe.wait_ge(ready, i + 1)
                if i >= 4:
                    pe.wait_ge(kept, i - 3)
                for k in range(KB):
                    ins = pe.transpose(m.ps[:, i % 4, k * P:(k + 1) * P], cols(normed(i), k), m.ident[0:P, 0:P])
                ins.then_inc(turned, 1)

        @block.scalar
        def _(act):
            act.wait_ge(moments, T)
            act.activation(m.sd[:, :], m.mv[:, :, 1], ACT.Sqrt, bias=m.eps[0:P, 0:1]).then_inc(spread, 1)
            if transposed is None:
                return
            if gain_col is not None:
                act.wait_ge(loaded, 16 * len(loads))
            for i in range(T):
                act.wait_ge(turned, i + 1)
                view = m.ps[:, i % 4, 0:KB * P].rearrange("p (k t) -> p k t", k=KB)
                if gain_col is None:
                    act.activation(transposed[:, :, tile(i)], view, ACT.Copy).then_inc(kept, 1)
                else:
                    for k in range(KB):
                        ins = act.activation(transposed[:, k, tile(i)], view[:, k, :], ACT.Identity,
                                             bias=bias_col[:, k:k + 1], scale=gain_col[:, k:k + 1])
                    ins.then_inc(kept, 1)


def groups_phase(nc, m, n_groups, operands, evac, loads=(), slots=8, stores=None):
    with phase(nc, "loaded", "product", "taken_by_act", "taken_by_dve", "stored") as (
            block, loaded, product, taken_act, taken_dve, stored):
        taken = (taken_act, taken_dve)

        @block.sync
        def _(sp):
            for dst, src in loads:
                sp.dma_start(dst, src).then_inc(loaded, 16)
            if stores is not None:
                count = 0
                for n in range(n_groups):
                    for dst, src in stores(n):
                        sp.wait_ge(taken[n % 2], n // 2 + 1)
                        if n % 2:
                            sp.wait_ge(taken[0], n // 2 + 1)
                        sp.dma_start(dst, src).then_inc(stored, 16)
                        count += 16
                sp.wait_ge(stored, count)

        @block.tensor
        def _(pe):
            if loads:
                pe.wait_ge(loaded, 16 * len(loads))
            for n in range(n_groups):
                if n >= slots:
                    pe.wait_ge(taken[n % 2], (n - slots) // 2 + 1)
                ops = operands(n, m.ps[:, n % slots, :])
                for k, (out, lhsT, rhs) in enumerate(ops):
                    ins = pe.matmul(out, lhsT, rhs, start=k == 0, stop=k == len(ops) - 1, skip_group_check=True)
                ins.then_inc(product, 1)

        @block.scalar
        def _(act):
            if loads:
                act.wait_ge(loaded, 16 * len(loads))
            for n in range(0, n_groups, 2):
                act.wait_ge(product, n + 1)
                evac(n, act, m.ps[:, n % slots, :], True).then_inc(taken[0], 1)

        @block.vector
        def _(dve):
            if loads:
                dve.wait_ge(loaded, 16 * len(loads))
            for n in range(1, n_groups, 2):
                dve.wait_ge(product, n + 1)
                evac(n, dve, m.ps[:, n % slots, :], False).then_inc(taken[1], 1)


def copy_scaled(eng, out, in_, on_act, scale=1.0, bias=None):
    if on_act:
        if bias is None:
            return eng.activation(out, in_, ACT.Copy, scale=scale)
        return eng.activation(out, in_, ACT.Identity, bias=bias, scale=scale)
    if bias is None:
        return eng.tensor_scalar(out, in_, scale, None, ALU.mult)
    return eng.tensor_scalar(out, in_, scale, bias, ALU.mult, ALU.add)


def wview(w):
    return w.rearrange("(k p) f -> p k f", p=128)


def vector_groups_phase(nc, m, n_groups, operands, evac, loads=(), slots=8):
    with phase(nc, "loaded", "product", "taken") as (block, loaded, product, taken):
        @block.sync
        def _(sp):
            for dst, src in loads:
                sp.dma_start(dst, src).then_inc(loaded, 16)

        @block.tensor
        def _(pe):
            if loads:
                pe.wait_ge(loaded, 16 * len(loads))
            for n in range(n_groups):
                if n >= slots:
                    pe.wait_ge(taken, n - slots + 1)
                ops = operands(n, m.ps[:, n % slots, :])
                for k, (out, lhsT, rhs) in enumerate(ops):
                    ins = pe.matmul(out, lhsT, rhs, start=k == 0, stop=k == len(ops) - 1, skip_group_check=True)
                ins.then_inc(product, 1)

        @block.vector
        def _(dve):
            for n in range(n_groups):
                dve.wait_ge(product, n + 1)
                evac(n, dve, m.ps[:, n % slots, :]).then_inc(taken, 1)


def add_row_phase(nc, x, row, scratch, src):
    with phase(nc, "loaded", "added") as (block, loaded, added):
        @block.sync
        def _(sp):
            sp.dma_start(scratch, row).then_inc(loaded, 16)

        @block.vector
        def _(dve):
            dve.wait_ge(loaded, 16)
            for i in range(T):
                dve.tensor_tensor(x[:, i, :], src[:, i, :], scratch, ALU.add).then_inc(added, 1)


def spread_row(v, parts=P):
    return v.rearrange("(a n) -> a n", a=1).to_broadcast([parts, v.shape[0]])



def edge_mlp_phase(nc, m, ef_t, w1, w2, w3, h3):
    CE, FLIGHT = 425, 5
    TURNS = E // (CE * FLIGHT)
    with ExitStack() as ctx:
        w1s = sb(nc, ctx, "mlp_w1", [128, 128])
        w2s = sb(nc, ctx, "mlp_w2", [128, 128])
        w3s = sb(nc, ctx, "mlp_w3", [128, 128])
        ef = sb(nc, ctx, "mlp_in", [128, FLIGHT, CE])
        ha = sb(nc, ctx, "mlp_h", [128, FLIGHT, 2, CE])
        ho = sb(nc, ctx, "mlp_out", [HID, FLIGHT, CE])
        names = [f"{what}_{c}" for what in ("in", "mm", "act", "out") for c in range(FLIGHT)]
        with phase(nc, "zeroed", "weights", *names) as (block, zeroed, weights, *by_chunk):
            arrived, mm, acted, stored = (by_chunk[FLIGHT * k:FLIGHT * (k + 1)] for k in range(4))

            @block.sync
            def _(sp):
                sp.wait_ge(zeroed, 5)
                for w, dram in ((w1s, w1), (w2s, w2), (w3s, w3)):
                    sp.dma_start(w[0:dram.shape[0], 0:HID], dram).then_inc(weights, 16)
                for c in range(FLIGHT):
                    sp.dma_start(ef[0:8, c, :], ef_t[:, c * CE:(c + 1) * CE]).then_inc(arrived[c], 16)
                with sp.Fori(0, TURNS - 1) as it:
                    for c in range(FLIGHT):
                        sp.wait_ge(mm[c], 3 * it + 1)
                        sp.dma_start(ef[0:8, c, :], ef_t[:, bass.ds((FLIGHT * it + FLIGHT + c) * CE, CE)]).then_inc(arrived[c], 16)

            @block.tensor
            def _(pe):
                pe.wait_ge(weights, 48)
                pe.wait_ge(zeroed, 5)
                with pe.Fori(0, TURNS) as it:
                    for layer, w in enumerate((w1s, w2s, w3s)):
                        for c in range(FLIGHT):
                            if layer == 0:
                                pe.wait_ge(arrived[c], 16 * it + 16)
                                rhs = ef[:, c, :]
                            else:
                                rhs = ha[:, c, layer - 1, :]
                            pe.wait_ge(acted[c], 3 * it + layer + 1)
                            pe.matmul(m.ps[:, c, 0:CE], w[:, :], rhs, start=True, stop=True).then_inc(mm[c], 1)

            @block.vector
            def _(dve):
                for unfilled in (w1s[:, :], w2s[:, :], w3s[:, :], ef[:, :, :], ha[HID:128, :, :, :]):
                    dve.memset(unfilled, 0.0).then_inc(zeroed, 1)

            @block.scalar
            def _(act):
                scales = (8 ** -0.5, SILU_2MOM * HID ** -0.5, SILU_2MOM * HID ** -0.5)
                for c in range(FLIGHT):
                    act.sem_inc(acted[c], 1)
                    act.sem_inc(stored[c], 16)
                with act.Fori(0, TURNS) as it:
                    for layer in range(3):
                        for c in range(FLIGHT):
                            act.wait_ge(mm[c], 3 * it + layer + 1)
                            if layer == 2:
                                act.wait_ge(stored[c], 16 * it + 16)
                            out = ho[:, c, :] if layer == 2 else ha[0:HID, c, layer, :]
                            act.activation(out, m.ps[0:HID, c, 0:CE], ACT.Silu, scale=scales[layer]).then_inc(acted[c], 1)
                    for c in range(FLIGHT):
                        act.wait_ge(acted[c], 3 * it + 4)
                        act.dma_start(h3[:, bass.ds((FLIGHT * it + c) * CE, CE)], ho[:, c, :]).then_inc(stored[c], 16)
                for c in range(FLIGHT):
                    act.wait_ge(stored[c], 16 * TURNS + 16)


def edge_base_phase(nc, m, ctx, src_l, dst_l, ea4_l):
    t = sb
    m.src_i = t(nc, ctx, "src_i", [P, SB + 1, G], I32)
    m.dst_i = t(nc, ctx, "dst_i", [P, SB, G], I32)
    m.src_f = t(nc, ctx, "src_f", [P, SB, G])
    m.dst_f = t(nc, ctx, "dst_f", [P, SB, G])
    m.dst_rel = t(nc, ctx, "dst_rel", [P, SB, G])
    m.ea4 = t(nc, ctx, "ea4", [P, SB, G, 4])
    m.base_f = t(nc, ctx, "base_f", [P, SB])
    m.base_i = t(nc, ctx, "base_i", [P, SB], I32)
    lo = t(nc, ctx, "lo", [P, SB])
    hi = t(nc, ctx, "hi", [P, SB])
    lo_all = t(nc, ctx, "lo_all", [P, SB])
    hi_all = t(nc, ctx, "hi_all", [P, SB])
    span = t(nc, ctx, "span", [P, SB])
    widest = t(nc, ctx, "widest", [P, 1])
    m.wide = t(nc, ctx, "wide", [P, 1], I32)
    with phase(nc, "loaded", "chain", "reduced") as (block, loaded, chain, reduced):
        @block.sync
        def _(sp):
            sp.dma_start(m.src_i[:, 0:SB, :], src_l).then_inc(loaded, 16)
            sp.dma_start(m.dst_i[:, :, :], dst_l).then_inc(loaded, 16)
            sp.dma_start(m.ea4[:, :, :, :], ea4_l).then_inc(loaded, 16)

        @block.gpsimd
        def _(pool):
            pool.wait_ge(chain, 5)
            pool.partition_all_reduce(lo_all[:, :], lo[:, :], P, RMAX).then_inc(reduced, 1)
            pool.partition_all_reduce(hi_all[:, :], hi[:, :], P, RMAX).then_inc(reduced, 1)

        @block.vector
        def _(dve):
            dve.memset(m.src_i[:, SB, :], 0)
            dve.wait_ge(loaded, 48)
            dve.tensor_copy(m.src_f[:, :, :], m.src_i[:, 0:SB, :]).then_inc(chain, 1)
            dve.tensor_copy(m.dst_f[:, :, :], m.dst_i[:, :, :]).then_inc(chain, 1)
            dve.wait_ge(chain, 2)
            dve.tensor_reduce(span[:, :], m.dst_f[:, :, :], AX.X, ALU.min).then_inc(chain, 1)
            dve.tensor_reduce(hi[:, :], m.dst_f[:, :, :], AX.X, ALU.max).then_inc(chain, 1)
            dve.wait_ge(chain, 4)
            dve.tensor_scalar(lo[:, :], span[:, :], -1.0, None, ALU.mult).then_inc(chain, 1)
            dve.wait_ge(reduced, 2)
            dve.tensor_scalar(m.base_f[:, :], lo_all[:, :], -1.0, None, ALU.mult).then_inc(chain, 1)
            dve.tensor_tensor(span[:, :], hi_all[:, :], lo_all[:, :], ALU.add).then_inc(chain, 1)
            dve.wait_ge(chain, 7)
            dve.tensor_copy(m.base_i[:, :], m.base_f[:, :]).then_inc(chain, 1)
            dve.tensor_reduce(widest[:, :], span[:, :], AX.X, ALU.max).then_inc(chain, 1)
            dve.wait_ge(chain, 9)
            dve.tensor_scalar(m.wide[:, :], widest[:, :], float(W), None, ALU.is_ge).then_inc(chain, 1)


def edge_sum_phase(nc, m, b, h3, xup):
    NI, U, AHEAD = SB // 2, 2 * G, 2
    done = lambda it, u: U * it + u + 1 + AHEAD
    free = lambda it, u: U * it + u - 1 + AHEAD
    gathered = m.gathered
    with phase(nc, "rel", "turn", "h_a", "h_b", "index", "even_senders", "odd_senders", "path", "window", "weighed", "prod",
               "seg", "counted", "flushed", held=gathered) as (
            block, rel, turn, h_a, h_b, index, even_senders, odd_senders, path, window, weighed, prod, seg, counted, flushed):
        h_in = (h_a, h_b)

        @block.sync
        def _(sp):
            for c in range(2):
                sp.dma_start(b.h3[0:HID, c, :], h3[:, c * 625:(c + 1) * 625]).then_inc(h_in[c], 16)
            with sp.Fori(0, NI - 1) as it:
                for c in range(2):
                    sp.wait_ge(path, U * it + G * (c + 1))
                    sp.dma_start(b.h3[0:HID, c, :], h3[:, bass.ds((2 * it + 2 + c) * 625, 625)]).then_inc(h_in[c], 16)

        @block.gpsimd
        def _(pool):
            def gather(u):
                pool.indirect_dma_start(b.rows[:, u, :], None, xup,
                                        bass.IndirectOffsetOnAxis(ap=b.idx[:, u // G, u % G:u % G + 1].bitcast(U32), axis=0)
                                        ).then_inc(gathered[u], 16)

            def senders(it, u):
                pool.wait_ge(counted, free(it, u))
                pool.sem_inc(turn, 1)
                pool.tensor_scalar(b.hot_src[:, 0, 0:N], m.iota[0:P, 0:N], b.sender[:, u // G, u % G:u % G + 1], None,
                                   ALU.is_equal).then_inc(even_senders, 1)

            flat = "p a g -> p (a g)"
            pool.sem_inc(even_senders, AHEAD)
            pool.tensor_copy(b.idx[:, 0, :], m.src_i[:, 0:1, :].rearrange(flat)).then_inc(index, 1)
            pool.wait_ge(index, 1)
            for g in range(G):
                gather(g)
            with pool.Fori(0, NI) as it:
                for c in (0, 1):
                    pool.wait_ge(even_senders, G * it + 3 * c + AHEAD)
                    pool.tensor_copy(b.sender[:, c, :], m.src_f[:, bass.ds(2 * it + c, 1), :].rearrange(flat)).then_inc(index, 1)
                    pool.wait_ge(prod, done(it, G * c - 1))
                    other, ahead = (1, 1) if c == 0 else (0, 2)
                    pool.tensor_copy(b.idx[:, other, :], m.src_i[:, bass.ds(2 * it + ahead, 1), :].rearrange(flat)).then_inc(index, 1)
                    pool.wait_ge(index, 4 * it + 2 * c + 3)
                    pool.sem_inc(turn, 1)
                    for g in range(G):
                        if (G * c + g) % 2 == 0:
                            senders(it, G * c + g)
                        gather(G * other + g)
            for g in range(U):
                pool.wait_ge(gathered[g], 16 * (NI + (1 if g < G else 0)))

        @block.tensor
        def _(pe):
            def segment(it, u):
                c, first, last = u // G, u % G == 0, u % G == G - 1
                ps = m.ps[:, 2 + c, :]
                pr, sy = b.prod[:, u % 2, :], b.sy[:, u % 2, :]

                def add(out, messages, windows, start=False):
                    return pe.matmul(out, messages, windows, start=start, stop=last, skip_group_check=True)
                if first:
                    pe.wait_ge(flushed, 2 * it + c - 1 + AHEAD)
                pe.wait_ge(weighed, done(it, u))
                pe.wait_ge(prod, done(it, u))
                add(ps[:, 0:3 * W], pr[:, 128:256], sy[:, 0:3 * W], start=first)
                add(ps[:, 3 * W:4 * W], pr[:, 0:128], sy[:, 3 * W:4 * W])
                for k in range(3):
                    add(ps[:, 4 * W:5 * W], pr[:, 640 + 128 * k:768 + 128 * k], sy[:, k * W:(k + 1) * W])
                for k in range(3):
                    ins = add(ps[:, (5 + k) * W:(6 + k) * W], pr[:, 256 + 128 * k:384 + 128 * k], sy[:, 3 * W:4 * W])
                ins.then_inc(seg, 1)
                if u % 2 == 0:
                    pe.wait_ge(even_senders, G * it + u // 2 + 1 + AHEAD)
                else:
                    pe.wait_ge(odd_senders, G * it + u // 2 + 1)
                for j in range(T):
                    ins = pe.matmul(m.ps[:, 4 + 2 * c + j // 5, (j % 5) * W:(j % 5 + 1) * W], b.hot_src[:, u % 2, j * P:j * P + 128],
                                    b.hot[:, u % 2, :], start=first and j % 5 == 0, stop=last, skip_group_check=True)
                ins.then_inc(counted, 1)

            pe.sem_inc(seg, AHEAD)
            pe.sem_inc(counted, AHEAD)
            with pe.Fori(0, NI) as it:
                for u in range(U):
                    if u % G == 0:
                        pe.wait_ge(h_in[u // G], 16 * it + 16)
                    pe.wait_ge(prod, free(it, u))
                    pe.matmul(m.ps[0:P, u % 2, :], b.h3[:, u // G, (u % G) * P:(u % G + 1) * P], b.w4[:, :], start=True,
                              stop=True).then_inc(path, 1)
                    if u >= 1:
                        segment(it, u - 1)
                segment(it, U - 1)

        @block.scalar
        def _(act):
            act.sem_inc(weighed, AHEAD)
            with act.Fori(0, NI) as it:
                for u in range(U):
                    act.wait_ge(window, U * it + u + 1)
                    act.wait_ge(seg, free(it, u))
                    for k, y in enumerate((1, 2, 3, 0)):
                        ins = act.activation(b.sy[:, u % 2, k * W:(k + 1) * W], b.hot[:, u % 2, :], ACT.Copy,
                                             scale=m.ea4[:, bass.ds(2 * it + u // G, 1), u % G, y])
                    ins.then_inc(weighed, 1)

        @block.vector
        def _(dve):
            def flush(it, c):
                base = dve.value_load(m.base_i[0:1, bass.ds(2 * it + c, 1)], min_val=0, max_val=N)
                acc = m.acc[:, :, bass.ds(base, W)]
                cnt = m.cnt[:, :, bass.ds(base, W)]
                dve.wait_ge(counted, done(it, G * c + G - 1))
                dve.wait_ge(flushed, 2 * it + c + AHEAD)
                dve.tensor_tensor(acc, m.ps[:, 2 + c, :].rearrange("p (a w) -> p a w", w=W), acc, ALU.add)
                for a in range(2):
                    view = m.ps[0:P, 4 + 2 * c + a, 0:5 * W].rearrange("p (a w) -> p a w", w=W)
                    part = cnt[:, 5 * a:5 * a + 5, :]
                    ins = dve.tensor_tensor(part, view, part, ALU.add)
                ins.then_inc(flushed, 1)

            dve.sem_inc(prod, AHEAD)
            dve.sem_inc(flushed, AHEAD)
            dve.tensor_tensor(m.dst_rel[:, :, :], m.dst_f[:, :, :],
                              m.base_f[:, :].rearrange("p (s a) -> p s a", a=1).to_broadcast([P, SB, G]),
                              ALU.subtract).then_inc(rel, 1)
            dve.wait_ge(rel, 1)
            with dve.Fori(0, NI) as it:
                for u in range(U):
                    dve.wait_ge(counted, free(it, u))
                    dve.wait_ge(weighed, free(it, u))
                    dve.tensor_scalar(b.hot[:, u % 2, :], m.iota[0:P, 0:W], m.dst_rel[:, bass.ds(2 * it + u // G, 1), u % G], None,
                                      ALU.is_equal).then_inc(window, 1)
                    dve.wait_ge(path, U * it + u + 1)
                    dve.wait_ge(gathered[u], 16 * it + 16)
                    dve.wait_ge(seg, free(it, u))
                    w, row, pr = m.ps[0:P, u % 2, :], b.rows[:, u, :], b.prod[:, u % 2, :]
                    dve.tensor_tensor(pr[:, 0:256].rearrange("p (a c) -> p a c", a=2), w[:, 0:256].rearrange("p (a c) -> p a c", a=2),
                                      row[:, 0:128].rearrange("p (a c) -> p a c", a=1).to_broadcast([P, 2, 128]), ALU.mult)
                    for a in range(2):
                        ins = dve.tensor_tensor(pr[:, 256 + 384 * a:640 + 384 * a].rearrange("p (a c) -> p a c", a=3),
                                                w[:, 256 + 128 * a:384 + 128 * a].rearrange("p (a c) -> p a c", a=1).to_broadcast([P, 3, 128]),
                                                row[:, 128:512].rearrange("p (a c) -> p a c", a=3), ALU.mult)
                    ins.then_inc(prod, 1)
                    if u % 2:
                        dve.tensor_scalar(b.hot_src[:, 1, 0:N], m.iota[0:P, 0:N], m.src_f[:, bass.ds(2 * it + u // G, 1), u % G], None,
                                          ALU.is_equal).then_inc(odd_senders, 1)
                    if u == G + 1:
                        flush(it, 0)
                flush(it, 1)


def edges(nc, m, a, ctx):
    edge_base_phase(nc, m, ctx, a["src_l"], a["dst_l"], a["ea4_l"])
    b = Tensors()
    b.h3 = sb(nc, ctx, "edge_hidden", [128, 2, 625])
    b.w4r = sb(nc, ctx, "w4_raw", [HID, 4 * MUL])
    b.w4 = sb(nc, ctx, "w4", [128, 4 * MUL])
    b.idx = sb(nc, ctx, "edge_index", [P, 2, G], I32)
    b.sender = sb(nc, ctx, "sender", [P, 2, G])
    b.rows = sb(nc, ctx, "sender_rows", [P, 2 * G, D])
    b.hot_src = sb(nc, ctx, "hot_src", [P, 2, N + 3], BF16)
    b.hot = sb(nc, ctx, "hot_dst", [P, 2, W], BF16)
    b.sy = sb(nc, ctx, "weighed_hot", [P, 2, 4 * W])
    b.prod = sb(nc, ctx, "edge_products", [P, 2, 8 * MUL])
    with phase(nc, "loaded", "done") as (block, loaded, done):
        @block.sync
        def _(sp):
            sp.dma_start(b.w4r[:, :], a["L0_gnn_W_mlp4"]).then_inc(loaded, 16)

        @block.vector
        def _(dve):
            dve.wait_ge(loaded, 16)
            c = SILU_2MOM * HID ** -0.5
            dve.tensor_scalar(b.w4[0:HID, 0:384], b.w4r[:, 0:384], c, None, ALU.mult).then_inc(done, 1)
            dve.tensor_scalar(b.w4[0:HID, 384:512], b.w4r[:, 384:512], c * 3 ** -0.5, None, ALU.mult).then_inc(done, 1)
            dve.memset(b.w4[HID:128, :], 0.0).then_inc(done, 1)
            dve.memset(b.h3[HID:128, :, :], 0.0).then_inc(done, 1)
            dve.memset(b.hot_src[:, :, N:N + 3], 0.0).then_inc(done, 1)
            dve.memset(m.acc[:, :, :], 0.0).then_inc(done, 1)
            dve.memset(m.cnt[:, :, :], 0.0).then_inc(done, 1)
    wide = nc.values_load(m.wide[0:1, 0:1], min_val=0, max_val=1)
    with nc.If(wide == 0):
        edge_sum_phase(nc, m, b, a["h3"], a["xup"])
    with nc.Else():
        with phase(nc, "done") as (block, done):
            @block.vector
            def _(dve):
                dve.memset(m.base_f[:, :], 0.0).then_inc(done, 1)
                dve.memset(m.base_i[:, :], 0).then_inc(done, 1)
        with nc.Fori(0, -(-N // W)) as _w:
            edge_sum_phase(nc, m, b, a["h3"], a["xup"])
            with phase(nc, "moved") as (block, moved):
                @block.vector
                def _(dve):
                    dve.tensor_scalar(b.sy[0:P, 0, 0:SB], m.base_f[:, :], float(W), None, ALU.add).then_inc(moved, 1)
                    dve.wait_ge(moved, 1)
                    dve.tensor_copy(m.base_f[:, :], b.sy[0:P, 0, 0:SB]).then_inc(moved, 1)
                    dve.tensor_copy(m.base_i[:, :], b.sy[0:P, 0, 0:SB]).then_inc(moved, 1)



def l0_mix(nc, m, a):
    R = 4
    with ExitStack() as ctx:
        w_in = sb(nc, ctx, "mix_w_in", [128, KB, D])
        b_in = sb(nc, ctx, "mix_b_in", [128, KB])
        xm = sb(nc, ctx, "mix_mid", [128, KB, N])
        bd = sb(nc, ctx, "mix_heads", [128, 144])
        qk = sb(nc, ctx, "mix_qk", [P, 2, T, 32])
        v = sb(nc, ctx, "mix_v", [P, T, D])
        w_out = sb(nc, ctx, "mix_w_out", [128, KB, D])
        b_out = sb(nc, ctx, "mix_b_out", [P, D])

        with phase(nc, "zeroed", "loaded") as (block, zeroed, loaded):
            @block.vector
            def _(dve):
                dve.memset(bd[:, :], 0.0).then_inc(zeroed, 1)

            @block.sync
            def _(sp):
                sp.wait_ge(zeroed, 1)
                for h in range(2):
                    rows = slice(64 * h, 64 * h + 64)
                    sp.dma_start(bd[rows, R * h:R * h + R], a["L0_mix_W_q"]).then_inc(loaded, 16)
                    sp.dma_start(bd[rows, 8 + R * h:8 + R * h + R], a["L0_mix_W_k"]).then_inc(loaded, 16)
                    sp.dma_start(bd[rows, 16 + 64 * h:80 + 64 * h], a["L0_mix_W_v"]).then_inc(loaded, 16)
                sp.wait_ge(loaded, 96)

        def mid_products(n, bank):
            f, (c0, cn) = n // 3, CH[n % 3]
            return [(bank[:, 0:cn], w_in[:, k, f * 128:(f + 1) * 128], m.xt[:, k, c0:c0 + cn]) for k in range(KB)]

        def mid_take(n, eng, bank, on_act):
            f, (c0, cn) = n // 3, CH[n % 3]
            return copy_scaled(eng, xm[:, f, c0:c0 + cn], bank[:, 0:cn], on_act, bias=b_in[:, f:f + 1])

        groups_phase(nc, m, 12, mid_products, mid_take,
                     loads=[(w_in[:, :, :], wview(a["L0_mix_W_in"])), (b_in[:, :], a["L0_mix_b_in"])])

        def head_products(n, bank):
            i, half = n // 2, n % 2
            return [(bank[0:P, 144 * k:144 * k + 144], xm[:, 2 * half + k, tile(i)], bd[:, :]) for k in range(2)]

        def head_take(n, eng, bank, on_act):
            i, half = n // 2, n % 2
            two = bank[0:P, 0:288].rearrange("p (k c) -> p k c", k=2)
            for j in range(2):
                out = qk[:, j, i, 16 * half:16 * half + 16].rearrange("p (k c) -> p k c", k=2)
                copy_scaled(eng, out, two[:, :, 8 * j:8 * j + 8], on_act)
            out = v[:, i, 256 * half:256 * half + 256].rearrange("p (k c) -> p k c", k=2)
            return copy_scaled(eng, out, two[:, :, 16:144], on_act)

        groups_phase(nc, m, 2 * T, head_products, head_take,
                     loads=[(w_out[:, :, :], wview(a["L0_mix_W_out"])), (b_out[:, :], spread_row(a["L0_mix_b_out"]))])

        qmax = sb(nc, ctx, "mix_qmax", [P, T, HEADS])
        qsum = sb(nc, ctx, "mix_qsum", [P, T, HEADS])
        qinv = sb(nc, ctx, "mix_qinv", [P, T, HEADS])
        kmax = sb(nc, ctx, "mix_kmax", [P, 32])
        kmax_all = sb(nc, ctx, "mix_kmax_all", [P, 32])
        sh = sb(nc, ctx, "mix_shifted", [P, 2, T, 32])
        ex = sb(nc, ctx, "mix_exp", [P, 2, T, 32])
        qs = sb(nc, ctx, "mix_q_soft", [P, T, 32])
        qt = sb(nc, ctx, "mix_qt", [32, N])
        mask = sb(nc, ctx, "mix_mask", [32, HEADS, DH])
        dinv = sb(nc, ctx, "mix_dinv", [32, 1])
        kv = sb(nc, ctx, "mix_kv", [32, D])
        kvt = sb(nc, ctx, "mix_kvt", [128, KB, 32])
        kvw = sb(nc, ctx, "mix_kvw", [32, D])
        with phase(nc, "masked", "v_step", "a_step", "p_step", "t_step") as (block, masked, v_step, a_step, p_step, t_step):
            @block.gpsimd
            def _(pool):
                pool.memset(mask[:, :, :], 1.0).then_inc(masked, 1)
                pool.wait_ge(masked, 1)
                pool.affine_select(out=mask[:, :, :], in_=mask[:, :, :], compare_op=ALU.is_ge, fill=0.0, base=0,
                                   pattern=[[-R, HEADS], [0, DH]], channel_multiplier=1).then_inc(masked, 1)
                pool.wait_ge(masked, 2)
                pool.affine_select(out=mask[:, :, :], in_=mask[:, :, :], compare_op=ALU.is_ge, fill=0.0, base=R - 1,
                                   pattern=[[R, HEADS], [0, DH]], channel_multiplier=-1).then_inc(masked, 1)
                pool.wait_ge(v_step, 1)
                pool.partition_all_reduce(kmax_all[:, :], kmax[:, :], P, RMAX).then_inc(p_step, 1)

            @block.vector
            def _(dve):
                heads = lambda ap: ap.rearrange("p t (h r) -> p t h r", r=R)
                wide = lambda ap: ap.rearrange("p t (h a) -> p t h a", a=1).to_broadcast([P, T, HEADS, R])
                dve.tensor_reduce(kmax[:, :], qk[:, 1, :, :].rearrange("p t c -> p c t"), AX.X, ALU.max).then_inc(v_step, 1)
                dve.tensor_reduce(qmax[:, :, :], heads(qk[:, 0, :, :]), AX.X, ALU.max).then_inc(v_step, 1)
                dve.wait_ge(v_step, 2)
                dve.tensor_tensor(heads(sh[:, 0, :, :]), heads(qk[:, 0, :, :]), wide(qmax[:, :, :]), ALU.subtract).then_inc(v_step, 1)
                dve.wait_ge(p_step, 1)
                dve.tensor_tensor(sh[:, 1, :, :], qk[:, 1, :, :],
                                  kmax_all[:, :].rearrange("p (a c) -> p a c", a=1).to_broadcast([P, T, 32]), ALU.subtract).then_inc(v_step, 1)
                dve.wait_ge(a_step, 1)
                dve.tensor_reduce(qsum[:, :, :], heads(ex[:, 0, :, :]), AX.X, ALU.add).then_inc(v_step, 1)
                dve.wait_ge(v_step, 5)
                dve.reciprocal(qinv[:, :, :], qsum[:, :, :]).then_inc(v_step, 1)
                dve.wait_ge(v_step, 6)
                dve.tensor_tensor(heads(qs[:, :, :]), heads(ex[:, 0, :, :]), wide(qinv[:, :, :]), ALU.mult).then_inc(v_step, 1)
                dve.wait_ge(t_step, 1)
                dve.reciprocal(dinv[:, :], m.ps[0:32, 1, 0:1]).then_inc(v_step, 1)
                dve.wait_ge(v_step, 8)
                dve.wait_ge(masked, 3)
                dve.scalar_tensor_tensor(kv[:, :], m.ps[0:32, 0, :], dinv[:, 0:1], mask[:, :, :].rearrange("p h c -> p (h c)"),
                                         ALU.mult, ALU.mult).then_inc(v_step, 1)
                dve.wait_ge(t_step, 3)
                dve.tensor_copy(kvt[:, :, :], m.ps[:, 5, 0:128].rearrange("p (k c) -> p k c", k=KB)).then_inc(v_step, 1)
                dve.wait_ge(t_step, 4)
                dve.tensor_copy(kvw[:, :], m.ps[0:32, 6, :]).then_inc(v_step, 1)

            @block.scalar
            def _(act):
                act.wait_ge(v_step, 4)
                act.activation(ex[:, :, :, :], sh[:, :, :, :], ACT.Exp).then_inc(a_step, 1)
                act.wait_ge(t_step, 2)
                for c0, cn in CH:
                    ins = act.activation(qt[:, c0:c0 + cn], m.ps[0:32, 2 + c0 // 500, 0:cn], ACT.Copy)
                ins.then_inc(a_step, 1)

            @block.tensor
            def _(pe):
                pe.wait_ge(a_step, 1)
                for i in range(T):
                    pe.matmul(m.ps[0:32, 0, :], ex[:, 1, i, :], v[:, i, :], start=i == 0, stop=i == T - 1)
                for i in range(T):
                    ins = pe.matmul(m.ps[0:32, 1, 0:1], ex[:, 1, i, :], m.ones[0:P, 0:1], start=i == 0, stop=i == T - 1)
                ins.then_inc(t_step, 1)
                pe.wait_ge(v_step, 7)
                for i in range(T):
                    ins = pe.transpose(m.ps[0:32, 2 + i // 4, (i % 4) * P:(i % 4 + 1) * P], qs[:, i, :], m.ident[0:P, 0:P])
                ins.then_inc(t_step, 1)
                pe.wait_ge(v_step, 9)
                for k in range(KB):
                    ins = pe.transpose(m.ps[:, 5, k * 32:(k + 1) * 32], kv[:, k * 128:(k + 1) * 128], m.ident[0:32, 0:32])
                ins.then_inc(t_step, 1)
                pe.wait_ge(v_step, 10)
                for k in range(KB):
                    ins = pe.matmul(m.ps[0:32, 6, :], kvt[:, k, :], w_out[:, k, :], start=k == 0, stop=k == KB - 1)
                ins.then_inc(t_step, 1)

        def out_products(n, bank):
            return [(bank[0:P, :], qt[:, tile(n)], kvw[:, :])]

        def out_take(n, dve, bank):
            return dve.tensor_tensor(m.x[:, n, :], bank[0:P, :], m.x[:, n, :], ALU.add)

        vector_groups_phase(nc, m, T, out_products, out_take)
        add_rows(nc, m, b_out)


def add_rows(nc, m, row):
    with phase(nc, "added") as (block, added):
        @block.vector
        def _(dve):
            for i in range(T):
                dve.tensor_tensor(m.x[:, i, :], m.x[:, i, :], row[:, :], ALU.add).then_inc(added, 1)



def l0_ffn(nc, m, a):
    NE = 8
    KEEP = N // NE
    with ExitStack() as ctx:
        layernorm_phase(nc, m, m.x, lambda i: m.tmp[:, i % 2, :], m.xt)
        gw = sb(nc, ctx, "gate_w", [128, KB, NE])
        g0 = sb(nc, ctx, "gates", [P, T, NE])
        t = sb(nc, ctx, "sink_t", [P, T, NE])
        cg = sb(nc, ctx, "sink_weights", [P, T, NE])
        coef = sb(nc, ctx, "combine", [P, T, NE])

        def gate_products(n, bank):
            return [(bank[0:P, 0:NE], m.xt[:, k, tile(n)], gw[:, k, :]) for k in range(KB)]

        def gate_take(n, dve, bank):
            return dve.tensor_scalar(g0[:, n, :], bank[0:P, 0:NE], 1e-10, None, ALU.max)

        vector_groups_phase(nc, m, T, gate_products, gate_take, loads=[(gw[:, :, :], wview(a["L0_ffn_gate_w"][0]))])
        with phase(nc, "logged") as (block, logged):
            @block.scalar
            def _(act):
                act.activation(t[:, :, :], g0[:, :, :], ACT.Ln).then_inc(logged, 1)

        mt = sb(nc, ctx, "sink_max", [P, NE])
        mall = sb(nc, ctx, "sink_max_all", [P, NE])
        d1 = sb(nc, ctx, "sink_d1", [P, T, NE])
        e1 = sb(nc, ctx, "sink_e1", [P, T, NE])
        s1 = sb(nc, ctx, "sink_s1", [P, NE])
        l1 = sb(nc, ctx, "sink_l1", [P, NE])
        d2 = sb(nc, ctx, "sink_d2", [P, T, NE])
        m2 = sb(nc, ctx, "sink_m2", [P, T])
        d3 = sb(nc, ctx, "sink_d3", [P, T, NE])
        e2 = sb(nc, ctx, "sink_e2", [P, T, NE])
        s2 = sb(nc, ctx, "sink_s2", [P, T])
        l2 = sb(nc, ctx, "sink_l2", [P, T])
        by_expert = lambda ap: ap.rearrange("p (a e) -> p a e", a=1).to_broadcast([P, T, NE])
        by_token = lambda ap: ap.rearrange("p (t a) -> p t a", a=1).to_broadcast([P, T, NE])
        with nc.Fori(0, 8):
            with phase(nc, "v_step", "a_step", "p_step", "t_step") as (block, v_step, a_step, p_step, t_step):
                @block.vector
                def _(dve):
                    dve.tensor_reduce(mt[:, :], t[:, :, :].rearrange("p t e -> p e t"), AX.X, ALU.max).then_inc(v_step, 1)
                    dve.wait_ge(p_step, 1)
                    dve.tensor_tensor(d1[:, :, :], t[:, :, :], by_expert(mall[:, :]), ALU.subtract).then_inc(v_step, 1)
                    dve.wait_ge(a_step, 1)
                    dve.tensor_reduce(s1[:, :], e1[:, :, :].rearrange("p t e -> p e t"), AX.X, ALU.add).then_inc(v_step, 1)
                    dve.wait_ge(a_step, 2)
                    dve.tensor_tensor(d2[:, :, :], d1[:, :, :], by_expert(l1[:, :]), ALU.subtract).then_inc(v_step, 1)
                    dve.wait_ge(v_step, 4)
                    dve.tensor_reduce(m2[:, :], d2[:, :, :], AX.X, ALU.max).then_inc(v_step, 1)
                    dve.wait_ge(v_step, 5)
                    dve.tensor_tensor(d3[:, :, :], d2[:, :, :], by_token(m2[:, :]), ALU.subtract).then_inc(v_step, 1)
                    dve.wait_ge(a_step, 3)
                    dve.tensor_reduce(s2[:, :], e2[:, :, :], AX.X, ALU.add).then_inc(v_step, 1)
                    dve.wait_ge(a_step, 4)
                    dve.tensor_tensor(t[:, :, :], d3[:, :, :], by_token(l2[:, :]), ALU.subtract).then_inc(v_step, 1)

                @block.gpsimd
                def _(pool):
                    pool.wait_ge(v_step, 1)
                    pool.partition_all_reduce(mall[:, :], mt[:, :], P, RMAX).then_inc(p_step, 1)

                @block.tensor
                def _(pe):
                    pe.wait_ge(v_step, 3)
                    pe.matmul(m.ps[0:P, 0, 0:NE], m.ones[0:P, 0:P], s1[:, :], start=True, stop=True).then_inc(t_step, 1)

                @block.scalar
                def _(act):
                    act.wait_ge(v_step, 2)
                    act.activation(e1[:, :, :], d1[:, :, :], ACT.Exp).then_inc(a_step, 1)
                    act.wait_ge(t_step, 1)
                    act.activation(l1[:, :], m.ps[0:P, 0, 0:NE], ACT.Ln).then_inc(a_step, 1)
                    act.wait_ge(v_step, 6)
                    act.activation(e2[:, :, :], d3[:, :, :], ACT.Exp).then_inc(a_step, 1)
                    act.wait_ge(v_step, 7)
                    act.activation(l2[:, :], s2[:, :], ACT.Ln).then_inc(a_step, 1)

        cgt = sb(nc, ctx, "weights_by_expert", [NE, 2, N + 8])
        best = sb(nc, ctx, "best", [NE, 2, 8])
        chosen_t = sb(nc, ctx, "chosen_by_expert", [NE, N])
        chosen = sb(nc, ctx, "chosen", [P, T, NE])
        count = sb(nc, ctx, "chosen_by", [P, T])
        inv = sb(nc, ctx, "share", [P, T])
        half = sb(nc, ctx, "over_half", [P, T, NE])
        ROUNDS = -(-KEEP // 8)
        REST = KEEP - 8 * (ROUNDS - 1)
        TAKEN, PAD = -2.0, -1.0
        with phase(nc, "v_step", "a_step", "t_step", "found", "struck") as (block, v_step, a_step, t_step, found, struck):
            @block.scalar
            def _(act):
                act.activation(cg[:, :, :], t[:, :, :], ACT.Exp).then_inc(a_step, 1)
                act.wait_ge(t_step, 1)
                for c0, cn in CH:
                    ins = act.activation(cgt[:, 0, c0:c0 + cn], m.ps[0:NE, c0 // 500, 0:cn], ACT.Copy)
                ins.then_inc(a_step, 1)

            @block.tensor
            def _(pe):
                pe.wait_ge(a_step, 1)
                for i in range(T):
                    ins = pe.transpose(m.ps[0:NE, i // 4, (i % 4) * P:(i % 4 + 1) * P], cg[:, i, :], m.ident[0:P, 0:P])
                ins.then_inc(t_step, 1)
                pe.wait_ge(v_step, 3)
                for i in range(T):
                    ins = pe.transpose(m.ps[0:P, 4, i * NE:(i + 1) * NE], chosen_t[:, tile(i)], m.ident[0:NE, 0:NE])
                ins.then_inc(t_step, 1)

            @block.vector
            def _(dve):
                dve.memset(cgt[:, :, N:N + 8], PAD).then_inc(v_step, 1)
                dve.memset(best[:, 1, :], PAD).then_inc(v_step, 1)
                dve.wait_ge(v_step, 2)
                dve.wait_ge(a_step, 2)
                for r in range(ROUNDS):
                    last = r == ROUNDS - 1
                    if r:
                        dve.wait_ge(struck, r)
                    dve.max(best[:, 0, :], cgt[:, r % 2, :]).then_inc(found, 1)
                    dve.wait_ge(found, r + 1)
                    if last:
                        dve.tensor_copy(best[:, 1, 0:REST], best[:, 0, 0:REST]).then_inc(found, 1)
                        dve.wait_ge(found, r + 2)
                    dve.match_replace(cgt[:, (r + 1) % 2, :], best[:, int(last), :], cgt[:, r % 2, :], TAKEN).then_inc(struck, 1)
                dve.wait_ge(struck, ROUNDS)
                dve.tensor_scalar(chosen_t[:, :], cgt[:, ROUNDS % 2, 0:N], (TAKEN + PAD) / 2, None, ALU.is_le).then_inc(v_step, 1)
                dve.wait_ge(t_step, 2)
                dve.tensor_copy(chosen[:, :, :], m.ps[0:P, 4, 0:T * NE].rearrange("p (t e) -> p t e", e=NE)).then_inc(v_step, 1)
                dve.tensor_scalar(half[:, :, :], cg[:, :, :], 0.5, None, ALU.is_gt).then_inc(v_step, 1)
                dve.wait_ge(v_step, 5)
                dve.tensor_reduce(count[:, :], chosen[:, :, :], AX.X, ALU.add).then_inc(v_step, 1)
                dve.tensor_tensor(half[:, :, :], half[:, :, :], chosen[:, :, :], ALU.mult).then_inc(v_step, 1)
                dve.wait_ge(v_step, 7)
                dve.tensor_scalar(s2[:, :], count[:, :], 1.0, None, ALU.add).then_inc(v_step, 1)
                dve.wait_ge(v_step, 8)
                dve.reciprocal(inv[:, :], s2[:, :]).then_inc(v_step, 1)
                dve.wait_ge(v_step, 9)
                dve.tensor_tensor(coef[:, :, :], half[:, :, :], by_token(inv[:, :]), ALU.mult).then_inc(v_step, 1)

        HALF = D // 2
        xh = sb(nc, ctx, "expert_x_high", [128, KB, N], F32R)
        xl = sb(nc, ctx, "expert_x_low", [128, KB, N], F32R)
        raw = sb(nc, ctx, "expert_w", [128, 2, KB, HALF])
        wh = sb(nc, ctx, "expert_w_high", [128, 2, KB, HALF], F32R)
        wl = sb(nc, ctx, "expert_w_low", [128, 2, KB, HALF], F32R)
        SLOTS, AHEAD = 5, 2 * T
        with phase(nc, "w_a", "w_b", "w_rounded", "w_ready", "x_rounded", "x_ready", "product", "taken") as (
                block, w_a, w_b, w_rounded, w_ready, x_rounded, x_ready, product, taken):
            arrived = (w_a, w_b)
            experts = a["L0_ffn_experts"].rearrange("e (k p) f -> e p k f", p=128)

            @block.sync
            def _(sp):
                for c in range(2):
                    sp.dma_start(raw[:, c, :, :], experts[0][:, :, c * HALF:(c + 1) * HALF]).then_inc(arrived[c], 16)
                with sp.Fori(0, NE - 1) as it:
                    for c in range(2):
                        sp.wait_ge(w_ready, 2 * it + c + 1)
                        sp.dma_start(raw[:, c, :, :], experts[bass.ds(it + 1, 1)].rearrange("a p k f -> (a p) k f")[:, :, c * HALF:(c + 1) * HALF]
                                     ).then_inc(arrived[c], 16)

            @block.gpsimd
            def _(pool):
                with pool.Fori(0, NE) as it:
                    for c in range(2):
                        pool.wait_ge(w_rounded, 2 * it + c + 1)
                        pool.tensor_tensor(wl[:, c, :, :], raw[:, c, :, :], wh[:, c, :, :].bitcast(F32), ALU.subtract).then_inc(w_ready, 1)

            @block.tensor
            def _(pe):
                pe.sem_inc(product, AHEAD)
                with pe.Fori(0, NE) as it:
                    for c in range(2):
                        pe.wait_ge(w_ready, 2 * it + c + 1)
                        for i in range(T):
                            n = T * c + i
                            pe.wait_ge(x_ready, i // 4 + 1)
                            pe.wait_ge(taken, 2 * T * it + n + 1 - SLOTS + AHEAD)
                            for k in range(KB):
                                for q, (x, w) in enumerate(((xh, wh), (xl, wh), (xh, wl))):
                                    ins = pe.matmul(m.ps[0:P, n % SLOTS, 0:HALF], x[:, k, tile(i)], w[:, c, k, :],
                                                    start=k == 0 and q == 0, stop=k == KB - 1 and q == 2)
                            ins.then_inc(product, 1)

            @block.scalar
            def _(act):
                for c0, cn in CH:
                    act.activation(xh[:, :, c0:c0 + cn], m.xt[:, :, c0:c0 + cn], ACT.Copy).then_inc(x_rounded, 1)
                with act.Fori(0, NE) as it:
                    for c in range(2):
                        act.wait_ge(arrived[c], 16 * it + 16)
                        act.wait_ge(product, 2 * T * it + T * (c - 1) + AHEAD)
                        act.activation(wh[:, c, :, :], raw[:, c, :, :], ACT.Copy).then_inc(w_rounded, 1)

            @block.vector
            def _(dve):
                dve.sem_inc(taken, AHEAD)
                for c, (c0, cn) in enumerate(CH):
                    dve.wait_ge(x_rounded, c + 1)
                    dve.tensor_tensor(xl[:, :, c0:c0 + cn], m.xt[:, :, c0:c0 + cn], xh[:, :, c0:c0 + cn].bitcast(F32), ALU.subtract).then_inc(x_ready, 1)
                with dve.Fori(0, NE) as it:
                    for c in range(2):
                        for i in range(T):
                            n = T * c + i
                            dve.wait_ge(product, 2 * T * it + n + 1 + AHEAD)
                            dve.wait_ge(taken, 2 * T * it + n + 1 - 2 * T + AHEAD)
                            part = m.x[:, i, c * HALF:(c + 1) * HALF]
                            dve.scalar_tensor_tensor(part, m.ps[0:P, n % SLOTS, 0:HALF], coef[:, i, bass.ds(it, 1)], part,
                                                     ALU.mult, ALU.add).then_inc(taken, 1)



def attention(nc, m, tag, qt, kt, v, ot, mask=None, cnt=None):
    own = lambda h: slice(64 * (h % 2), 64 * (h % 2) + 64)
    other = lambda h: own(h + 1)
    C = len(CH)
    UNITS = HEADS * C
    with ExitStack() as ctx:
        per = 2 if mask is None else 3
        part = sb(nc, ctx, tag + "row_max_parts", [P, HEADS * T, per])
        rmax = sb(nc, ctx, tag + "row_max", [P, HEADS * T])
        ks = sb(nc, ctx, tag + "k_split", [128, 2, N], F32R)
        qs = sb(nc, ctx, tag + "q_split", [128, C, 2, 512], F32R)
        z = m.tmp4

        def round_k(act, h, halves, k_rounded):
            for half in halves:
                ins = act.activation(ks[half(h), h % 2, :], kt[own(h), h // 2, :], ACT.Copy)
            if halves[-1] is other:
                ins.then_inc(k_rounded, 1)

        def round_q(act, u, q_rounded):
            h, (c0, cn) = u // C, CH[u % C]
            act.activation(qs[own(h), u % C, 0, 0:cn], qt[own(h), h // 2, c0:c0 + cn], ACT.Copy)
            act.activation(qs[other(h), u % C, 0, 0:cn], qt[own(h), h // 2, c0:c0 + cn], ACT.Copy).then_inc(q_rounded, 1)

        def rest_k(pool, h, k_rounded, k_ready):
            pool.wait_ge(k_rounded, h + 1)
            pool.tensor_tensor(ks[own(h), h % 2, :], kt[own(h), h // 2, :], ks[own(h), h % 2, :].bitcast(F32), ALU.subtract).then_inc(k_ready, 1)

        def rests(pool, q_rounded, k_rounded, q_rest, k_ready, early):
            rest_k(pool, 0, k_rounded, k_ready)
            for u in range(UNITS):
                h, (c0, cn) = u // C, CH[u % C]
                pool.wait_ge(q_rounded, u + 1)
                pool.tensor_tensor(qs[own(h), u % C, 1, 0:cn], qt[own(h), h // 2, c0:c0 + cn], qs[own(h), u % C, 0, 0:cn].bitcast(F32),
                                   ALU.subtract).then_inc(q_rest, 1)
                if u % C == 2 - early and h + 1 < HEADS:
                    rest_k(pool, h + 1, k_rounded, k_ready)

        def double_rest(act, u, q_rest, q_ready):
            h, (c0, cn) = u // C, CH[u % C]
            act.wait_ge(q_rest, u + 1)
            act.activation(qs[other(h), u % C, 1, 0:cn], qs[own(h), u % C, 1, 0:cn].bitcast(F32), ACT.Copy).then_inc(q_ready, 1)

        tiles_to = lambda u: T * (u // C) + (4, 8, 10)[u % C]
        with phase(nc, "scores", "maxed", "row", "q_rounded", "k_rounded", "q_rest", "k_ready", "q_ready") as (
                block, scores, maxed, row, q_rounded, k_rounded, q_rest, k_ready, q_ready):
            @block.tensor
            def _(pe):
                for n in range(HEADS * T):
                    h, i = n // T, n % T
                    u = C * h + i // 4
                    if i % 4 == 0:
                        pe.wait_ge(q_ready, u + 1)
                        pe.wait_ge(k_ready, h + 1)
                    if n >= 2:
                        pe.wait_ge(maxed, per * (n - 1))
                    for j, (c0, cn) in enumerate(CH):
                        for r in range(2):
                            ins = pe.matmul(m.ps[0:P, 4 * (n % 2) + j, 0:cn], qs[:, u % C, r, (i % 4) * P:(i % 4 + 1) * P],
                                            ks[:, h % 2, c0:c0 + cn], start=r == 0, stop=r == 1)
                    ins.then_inc(scores, 1)

            @block.gpsimd
            def _(pool):
                rests(pool, q_rounded, k_rounded, q_rest, k_ready, True)

            @block.scalar
            def _(act):
                round_k(act, 0, (own, other), k_rounded)
                for u in range(UNITS):
                    h = u // C
                    if u >= C:
                        act.wait_ge(scores, tiles_to(u - C))
                    round_q(act, u, q_rounded)
                    if u % C == 1 and h + 1 < HEADS:
                        if h:
                            act.wait_ge(scores, T * h)
                        round_k(act, h + 1, (own, other), k_rounded)
                    double_rest(act, u, q_rest, q_ready)

            @block.vector
            def _(dve):
                for n in range(HEADS * T):
                    dve.wait_ge(scores, n + 1)
                    bank = 4 * (n % 2)
                    if mask is None:
                        dve.tensor_reduce(part[:, n, 0:1], m.ps[0:P, bank:bank + 2, 0:500], AX.XY, ALU.max).then_inc(maxed, 1)
                        dve.tensor_reduce(part[:, n, 1:2], m.ps[0:P, bank + 2, 0:250], AX.X, ALU.max).then_inc(maxed, 1)
                        continue
                    for j, (c0, cn) in enumerate(CH):
                        if n:
                            dve.wait_ge(maxed, 3 * n - 2 + j)
                        dve.tensor_tensor_reduce(z[:, j, 0:cn], m.ps[0:P, bank + j, 0:cn], mask[:, n % T, c0:c0 + cn],
                                                 1.0, -BIG, ALU.add, ALU.max, part[:, n, j:j + 1]).then_inc(maxed, 1)
                dve.wait_ge(maxed, per * HEADS * T)
                dve.tensor_reduce(rmax[:, :], part[:, :, :], AX.X, ALU.max).then_inc(row, 1)

        RING = 4
        mb = sb(nc, ctx, tag + "max_by_column", [P, 2, 512])
        rec = sb(nc, ctx, tag + "denominators", [128, 512])
        LAG = 3
        with phase(nc, "spread", "kept", "scores", "shift", "clip", "expd", "counted", "summed", "inverted",
                   "normed", "q_rounded", "k_rounded", "q_rest", "k_ready", "q_ready") as (
                block, spread, kept, scores, shift, clip, expd, counted, summed, inverted, normed,
                q_rounded, k_rounded, q_rest, k_ready, q_ready):
            weighed = expd if mask is None else counted

            @block.tensor
            def _(pe):
                def maxima(u):
                    h, (c0, cn) = u // C, CH[u % C]
                    if u >= 2:
                        pe.wait_ge(kept, u - 1)
                    for i in range(cn // P):
                        col = h * T + c0 // P + i
                        ins = pe.transpose(m.ps[0:P, 6 + u % 2, i * P:(i + 1) * P], rmax[:, col:col + 1].to_broadcast([P, P]),
                                           m.ident[0:P, 0:P])
                    ins.then_inc(spread, 1)

                def sums(n):
                    u, j = n // T, n % T
                    h, (c0, cn) = u // C, CH[u % C]
                    if j == 0 and u >= 2:
                        pe.wait_ge(normed, u - 1)
                    pe.wait_ge(weighed, n + 1)
                    w0 = 64 * (h % 2)
                    pe.matmul(m.ps[:, 4 + u % 2, 0:cn], v[:, j, h // 2, w0:w0 + 128], z[:, n % RING, 0:cn],
                              start=j == 0, stop=j == T - 1).then_inc(summed, 1)

                maxima(0)
                for n in range(UNITS * T + LAG):
                    if n < UNITS * T:
                        u, j = n // T, n % T
                        h, (c0, cn) = u // C, CH[u % C]
                        if j == 0:
                            pe.wait_ge(q_ready, u + 1)
                            pe.wait_ge(k_ready, h + 1)
                        if n >= 4:
                            pe.wait_ge(shift, n - 3)
                        for r in range(2):
                            ins = pe.matmul(m.ps[0:P, n % 4, 0:cn], ks[:, h % 2, tile(j)], qs[:, u % C, r, 0:cn], start=r == 0, stop=r == 1)
                        ins.then_inc(scores, 1)
                        if j == 5 and u + 1 < UNITS:
                            maxima(u + 1)
                    if n >= LAG:
                        sums(n - LAG)

            @block.gpsimd
            def _(pool):
                rests(pool, q_rounded, k_rounded, q_rest, k_ready, False)

            @block.vector
            def _(dve):
                def norm(u):
                    h, (c0, cn) = u // C, CH[u % C]
                    num, den = own(h), other(h)
                    dve.wait_ge(summed, T * (u + 1))
                    if u:
                        dve.wait_ge(normed, u)
                    dve.reciprocal(rec[num, 0:cn], m.ps[den, 4 + u % 2, 0:cn]).then_inc(inverted, 1)
                    dve.wait_ge(inverted, u + 1)
                    dve.tensor_tensor(ot[num, h // 2, c0:c0 + cn], m.ps[num, 4 + u % 2, 0:cn], rec[num, 0:cn],
                                      ALU.mult).then_inc(normed, 1)

                def count(n):
                    u, j = n // T, n % T
                    c0, cn = CH[u % C]
                    dve.wait_ge(expd, n + 1)
                    dve.tensor_tensor(z[:, n % RING, 0:cn], z[:, n % RING, 0:cn], cnt[:, j, c0:c0 + cn], ALU.mult).then_inc(counted, 1)

                for n in range(UNITS * T):
                    u, j = n // T, n % T
                    c0, cn = CH[u % C]
                    if j == 0:
                        dve.wait_ge(kept, u + 1)
                    if n >= RING:
                        dve.wait_ge(summed, n - RING + 1)
                    dve.wait_ge(scores, n + 1)
                    dve.tensor_tensor(z[:, n % RING, 0:cn], m.ps[0:P, n % 4, 0:cn], mb[:, u % 2, 0:cn], ALU.subtract).then_inc(shift, 1)
                    if mask is not None and n >= 1:
                        count(n - 1)
                    if j == 4 and u >= 1:
                        norm(u - 1)
                if mask is not None:
                    count(UNITS * T - 1)
                norm(UNITS - 1)

            @block.scalar
            def _(act):
                def keep(u):
                    c0, cn = CH[u % C]
                    act.wait_ge(spread, u + 1)
                    if u >= 2:
                        act.wait_ge(shift, T * (u - 1))
                    act.activation(mb[:, u % 2, 0:cn], m.ps[0:P, 6 + u % 2, 0:cn], ACT.Copy).then_inc(kept, 1)

                round_k(act, 0, (own, other), k_rounded)
                round_q(act, 0, q_rounded)
                double_rest(act, 0, q_rest, q_ready)
                keep(0)
                for n in range(UNITS * T):
                    u, j = n // T, n % T
                    cn = CH[u % C][1]
                    slot = z[:, n % RING, 0:cn]
                    act.wait_ge(shift, n + 1)
                    if mask is None:
                        act.activation(slot, slot, ACT.Exp, scale=DH ** -0.5).then_inc(expd, 1)
                    else:
                        act.activation(slot, slot, ACT.Relu, scale=-(DH ** -0.5)).then_inc(clip, 1)
                        act.wait_ge(clip, n + 1)
                        act.activation(slot, slot, ACT.Exp, scale=-1.0).then_inc(expd, 1)
                    if u + 1 < UNITS:
                        if j == 1:
                            if u + 1 >= C:
                                act.wait_ge(scores, T * (u + 2 - C))
                            round_q(act, u + 1, q_rounded)
                        if j == 6:
                            double_rest(act, u + 1, q_rest, q_ready)
                            keep(u + 1)
                    if u % C == 1 and u // C + 1 < HEADS and j in (3, 8):
                        round_k(act, u // C + 1, (own,) if j == 3 else (other,), k_rounded)


def split_gemm_phase(nc, m, tag, sources, width, groups, take, takers="both"):
    J = len(sources)
    flat = [(j, g) for j in range(J) for g in groups[j]]
    upto = [sum(len(groups[i]) for i in range(j + 1)) for j in range(J)]
    taker = lambda n: {"both": n % 2, "act": 0, "dve": 1}[takers]
    turn = lambda n: n // 2 + 1 if takers == "both" else n + 1
    with ExitStack() as ctx:
        xh = sb(nc, ctx, tag + "x_high", [128, KB, N], F32R)
        xl = sb(nc, ctx, tag + "x_low", [128, KB, N], F32R)
        raw = sb(nc, ctx, tag + "w_raw", [128, 2, KB, width])
        wh = sb(nc, ctx, tag + "w_high", [128, 2, KB, width], F32R)
        wl = sb(nc, ctx, tag + "w_low", [128, 2, KB, width], F32R)
        with phase(nc, "w_a", "w_b", "w_rounded", "w_ready", "x_rounded", "x_ready", "product", "taken_by_act", "taken_by_dve") as (
                block, w_a, w_b, w_rounded, w_ready, x_rounded, x_ready, product, taken_act, taken_dve):
            arrived, taken = (w_a, w_b), (taken_act, taken_dve)

            @block.sync
            def _(sp):
                for j in range(J):
                    if j >= 2:
                        sp.wait_ge(w_ready, j - 1)
                    sp.dma_start(raw[:, j % 2, :, :], sources[j]).then_inc(arrived[j % 2], 16)

            @block.gpsimd
            def _(pool):
                for j in range(J):
                    pool.wait_ge(w_rounded, j + 1)
                    pool.tensor_tensor(wl[:, j % 2, :, :], raw[:, j % 2, :, :], wh[:, j % 2, :, :].bitcast(F32),
                                       ALU.subtract).then_inc(w_ready, 1)

            @block.tensor
            def _(pe):
                chunks = 0
                for n, (j, g) in enumerate(flat):
                    if n == 0 or flat[n - 1][0] != j:
                        pe.wait_ge(w_ready, j + 1)
                    c = g[2] if g[0] == "feature" else g[1] // 4
                    if c >= chunks:
                        chunks = c + 1
                        pe.wait_ge(x_ready, chunks)
                    if n >= 8:
                        pe.wait_ge(taken[taker(n - 8)], turn(n - 8))
                    ops = []
                    for k in range(KB):
                        for x, w in ((xh, wh), (xl, wh), (xh, wl)):
                            if g[0] == "feature":
                                c0, cn = CH[c]
                                ops.append((m.ps[:, n % 8, 0:cn], w[:, j % 2, k, g[1] * 128:(g[1] + 1) * 128], x[:, k, c0:c0 + cn]))
                            else:
                                ops.append((m.ps[0:P, n % 8, 0:width], x[:, k, tile(g[1])], w[:, j % 2, k, :]))
                    for o, (out, lhsT, rhs) in enumerate(ops):
                        ins = pe.matmul(out, lhsT, rhs, start=o == 0, stop=o == len(ops) - 1)
                    ins.then_inc(product, 1)

            @block.scalar
            def _(act):
                def round_w(j):
                    act.wait_ge(arrived[j % 2], 16 * (j // 2) + 16)
                    if j >= 2:
                        act.wait_ge(product, upto[j - 2])
                    act.activation(wh[:, j % 2, :, :], raw[:, j % 2, :, :], ACT.Copy).then_inc(w_rounded, 1)

                for c, (c0, cn) in enumerate(CH):
                    act.activation(xh[:, :, c0:c0 + cn], m.xt[:, :, c0:c0 + cn], ACT.Copy).then_inc(x_rounded, 1)
                    if c < min(2, J):
                        round_w(c)
                for n, (j, g) in enumerate(flat):
                    if n and flat[n - 1][0] != j and j + 1 < J:
                        round_w(j + 1)
                    if taker(n) == 0:
                        act.wait_ge(product, n + 1)
                        take(j, g, act, m.ps[:, n % 8, :], True).then_inc(taken_act, 1)

            @block.vector
            def _(dve):
                for c, (c0, cn) in enumerate(CH):
                    dve.wait_ge(x_rounded, c + 1)
                    dve.tensor_tensor(xl[:, :, c0:c0 + cn], m.xt[:, :, c0:c0 + cn], xh[:, :, c0:c0 + cn].bitcast(F32),
                                      ALU.subtract).then_inc(x_ready, 1)
                for n, (j, g) in enumerate(flat):
                    if taker(n) == 1:
                        dve.wait_ge(product, n + 1)
                        take(j, g, dve, m.ps[:, n % 8, :], False).then_inc(taken_dve, 1)


def qkv_for_attention(nc, m, tag, sources, qt, kt, v):
    def take(j, g, eng, bank, on_act):
        if j < 4:
            c0, cn = CH[g[2]]
            return copy_scaled(eng, (qt, kt)[j // 2][:, 2 * (j % 2) + g[1], c0:c0 + cn], bank[:, 0:cn], on_act)
        pairs = bank[0:P, 0:256].rearrange("p (b e c) -> p b e c", b=2, e=2)
        b0 = 2 * (j - 4)
        copy_scaled(eng, v[:, g[1], b0:b0 + 2, 0:64], pairs[:, :, 0, :], on_act)
        return copy_scaled(eng, v[:, g[1], b0:b0 + 2, 128:192], pairs[:, :, 1, :], on_act)

    by_feature = [("feature", f, c) for c in range(len(CH)) for f in range(2)]
    by_token = [("token", i) for i in range(T)]
    split_gemm_phase(nc, m, tag, sources, 256, [by_feature] * 4 + [by_token] * 2, take)


def add_product(nc, m, tag, sources):
    def take(j, g, dve, bank, on_act):
        part = m.x[:, g[1], 256 * j:256 * j + 256]
        return dve.tensor_tensor(part, bank[0:P, 0:256], part, ALU.add)

    split_gemm_phase(nc, m, tag, sources, 256, [[("token", i) for i in range(T)]] * 2, take, takers="dve")


def pieces(w, n):
    f = w.shape[1] // n
    return [wview(w)[:, :, j * f:(j + 1) * f] for j in range(n)]


def qkv_unsplit(nc, m, w, wq, wk, wv, qt, kt, v, loads):
    def products(n, bank):
        if n < 24:
            wx, f = (wq, n // 3) if n < 12 else (wk, n // 3 - 4)
            c0, cn = CH[n % 3]
            return [(bank[:, 0:cn], wx(k)[:, f * 128:(f + 1) * 128], m.xt[:, k, c0:c0 + cn]) for k in range(KB)]
        return [(bank[0:P, :], m.xt[:, k, tile(n - 24)], wv(k)) for k in range(KB)]

    def take(n, eng, bank, on_act):
        if n < 24:
            dst, f = (qt, n // 3) if n < 12 else (kt, n // 3 - 4)
            c0, cn = CH[n % 3]
            return copy_scaled(eng, dst[:, f, c0:c0 + cn], bank[:, 0:cn], on_act)
        i = n - 24
        pairs = bank[0:P, :].rearrange("p (b e c) -> p b e c", b=KB, e=2)
        copy_scaled(eng, v[:, i, :, 0:64], pairs[:, :, 0, :], on_act)
        return copy_scaled(eng, v[:, i, :, 128:192], pairs[:, :, 1, :], on_act)

    groups_phase(nc, m, 24 + T, products, take, loads=loads)


def ones_between(nc, v):
    with phase(nc, "filled") as (block, filled):
        @block.gpsimd
        def _(pool):
            for i in range(T):
                pool.memset(v[:, i, :, 64:128], 1.0).then_inc(filled, 1)


def move(nc, pairs):
    load_phase(nc, pairs)



def l1_gnn(nc, m, a, tok):
    layernorm_phase(nc, m, m.x, lambda i: m.tmp[:, i % 2, :], m.xt)
    with ExitStack() as ctx:
        with ExitStack() as c2:
            xn = sb(nc, c2, "xn_rows", [P, T, D])
            layernorm_phase(nc, m, m.x, lambda i: xn[:, i, :])
            move(nc, [(tok(a["xs"]), m.x[:, :, :]), (tok(a["xn"]), xn[:, :, :])])
        with ExitStack() as c2:
            qt = m.xraw[:, 0:KB * N].rearrange("p (k n) -> p k n", k=KB)
            kt = sb(nc, c2, "kt", [128, KB, N])
            v = sb(nc, c2, "v", [P, T, KB, 192])
            ones_between(nc, v)
            with ExitStack() as c3:
                w = sb(nc, c3, "wqkv", [128, 3, KB, D])
                qkv_unsplit(nc, m, w, lambda k: w[:, 0, k, :], lambda k: w[:, 1, k, :], lambda k: w[:, 2, k, :], qt, kt, v,
                                  [(w[:, j, :, :], wview(x)) for j, x in enumerate((a["L1_gnn_Wq"], a["L1_gnn_Wk"], a["L1_gnn_Wv"]))])
            mask = sb(nc, c2, "mask", [P, T, N], BF16)

            with phase(nc, "turned", "taken") as (block, turned, taken):
                @block.tensor
                def _(pe):
                    for n in range(T * 3):
                        i, (c0, cn) = n // 3, CH[n % 3]
                        if n >= 8:
                            pe.wait_ge(taken, n - 7)
                        for b in range(cn // P):
                            ins = pe.transpose(m.ps[0:P, n % 8, b * P:(b + 1) * P], m.cnt[:, c0 // P + b, tile(i)], m.ident[0:P, 0:P])
                        ins.then_inc(turned, 1)

                @block.vector
                def _(dve):
                    for n in range(T * 3):
                        i, (c0, cn) = n // 3, CH[n % 3]
                        dve.wait_ge(turned, n + 1)
                        dve.tensor_scalar(mask[:, i, c0:c0 + cn], m.ps[0:P, n % 8, 0:cn], 0.0, -1e30, ALU.is_equal, ALU.mult).then_inc(taken, 1)

            attention(nc, m, "gnn_", qt, kt, v, m.xt, mask, m.cnt)

    move(nc, [(m.x[:, :, :], tok(a["xn"]))])
    add_product(nc, m, "gnn_out_", pieces(a["L1_gnn_Wo"], 2))
    with ExitStack() as ctx:
        y = sb(nc, ctx, "gnn_y", [P, T, D])
        rows = sb(nc, ctx, "gnn_rows", [P, 5, D])
        w1 = sb(nc, ctx, "gnn_w1", [128, KB, 256])
        w2 = sb(nc, ctx, "gnn_w2", [128, 2, D])
        b1 = sb(nc, ctx, "gnn_b1", [128, 2])
        hid = sb(nc, ctx, "gnn_hidden", [128, 2, N])
        names = (a["L1_gnn_ln1_g"], a["L1_gnn_ln1_b"], a["L1_gnn_ln2_g"], a["L1_gnn_ln2_b"], a["L1_gnn_b2"])
        move(nc, [(w1[:, :, :], wview(a["L1_gnn_W1"])),
                  (w2[:, :, :], wview(a["L1_gnn_W2"])), (b1[:, :], a["L1_gnn_b1"])]
             + [(rows[:, j, :], spread_row(r)) for j, r in enumerate(names)])
        layernorm_phase(nc, m, m.x, lambda i: y[:, i, :], m.xt, gain_row=rows[:, 0, :], bias_row=rows[:, 1, :])

        def hidden_products(n, bank):
            f, (c0, cn) = n // 3, CH[n % 3]
            return [(bank[:, 0:cn], w1[:, k, f * 128:(f + 1) * 128], m.xt[:, k, c0:c0 + cn]) for k in range(KB)]

        def hidden_take(n, dve, bank):
            f, (c0, cn) = n // 3, CH[n % 3]
            return dve.tensor_scalar(hid[:, f, c0:c0 + cn], bank[:, 0:cn], b1[:, f:f + 1], 0.0, ALU.add, ALU.max)

        vector_groups_phase(nc, m, 6, hidden_products, hidden_take)
        vector_groups_phase(nc, m, T, lambda n, bank: [(bank[0:P, :], hid[:, k, tile(n)], w2[:, k, :]) for k in range(2)],
                            lambda n, dve, bank: dve.tensor_tensor(y[:, n, :], bank[0:P, :], y[:, n, :], ALU.add))
        with phase(nc, "added") as (block, added):
            @block.vector
            def _(dve):
                for i in range(T):
                    dve.tensor_tensor(y[:, i, :], y[:, i, :], rows[:, 4, :], ALU.add).then_inc(added, 1)
        layernorm_phase(nc, m, y, lambda i: m.x[:, i, :], None, gain_row=rows[:, 2, :], bias_row=rows[:, 3, :])
        add_into_saved(nc, m, a, tok, y)


def add_into_saved(nc, m, a, tok, y):
    with phase(nc, "loaded", "added", "stored") as (block, loaded, added, stored):
        @block.sync
        def _(sp):
            sp.dma_start(y[:, :, :], tok(a["xs"])).then_inc(loaded, 16)
            sp.wait_ge(added, T)
            sp.dma_start(tok(a["xs"]), m.x[:, :, :]).then_inc(stored, 16)
            sp.wait_ge(stored, 16)

        @block.vector
        def _(dve):
            dve.wait_ge(loaded, 16)
            for i in range(T):
                dve.tensor_tensor(m.x[:, i, :], m.x[:, i, :], y[:, i, :], ALU.add).then_inc(added, 1)



def l1_mix(nc, m, a, tok):
    F = 256
    H2 = 2 * D
    head = lambda h: slice(64 * (h % 2), 64 * (h % 2) + 64)
    with ExitStack() as ctx:
        cols = sb(nc, ctx, "mixer_cols", [128, 4, KB])
        move(nc, [(m.x[:, :, :], tok(a["xn"]))] + [(cols[:, j, :], c) for j, c in enumerate(
            (a["L1_mix_g1"], a["L1_mix_be1"], a["L1_mix_g2"], a["L1_mix_be2"]))])
        layernorm_phase(nc, m, m.x, lambda i: m.tmp[:, i % 2, :], m.xt, gain_col=cols[:, 0, :], bias_col=cols[:, 1, :])
        attn = sb(nc, ctx, "mixer_attn", [P, T, D])
        with ExitStack() as c2:
            qt = sb(nc, c2, "mixer_q", [128, KB, N])
            kt = sb(nc, c2, "mixer_k", [128, KB, N])
            v = sb(nc, c2, "mixer_v", [P, T, HEADS, 65])
            with ExitStack() as c3:
                bqk = sb(nc, c3, "mixer_bqk", [128, 12])
                bv = sb(nc, c3, "mixer_bv", [P, D])

                def take(j, g, dve, bank, on_act):
                    if j < 4:
                        c0, cn = CH[g[2]]
                        return dve.tensor_scalar((qt, kt)[j // 2][:, 2 * (j % 2) + g[1], c0:c0 + cn], bank[:, 0:cn],
                                                 bqk[:, 2 * j + g[1]:2 * j + g[1] + 1], None, ALU.add)
                    h0, by_head = 4 * (j - 4), lambda ap: ap.rearrange("p (h c) -> p h c", h=4)
                    return dve.tensor_tensor(v[:, g[1], h0:h0 + 4, 0:64], by_head(bank[0:P, 0:256]), by_head(bv[:, 64 * h0:64 * h0 + 256]), ALU.add)

                move(nc, [(bqk[:, :], a["L1_mix_bqk"]), (bv[:, :], a["L1_mix_bqkv"][2 * D:3 * D].rearrange("(a n) -> a n", a=1).to_broadcast([P, D]))])
                split_gemm_phase(nc, m, "mixer_qkv_", pieces(a["L1_mix_Wqkv"], 6), 256,
                                 [[("feature", f, c) for c in range(len(CH)) for f in range(2)]] * 4 + [[("token", i) for i in range(T)]] * 2,
                                 take, takers="dve")
                with phase(nc, "filled") as (block, filled):
                    @block.vector
                    def _(dve):
                        dve.memset(v[:, :, :, 64:65], 1.0).then_inc(filled, 1)
            pm = sb(nc, c2, "mixer_pmat", [128, 2, F])
            kvs = sb(nc, c2, "mixer_kv", [128, HEADS, 2, 65])
            nm = sb(nc, c2, "mixer_neg_max", [P, 4])
            feat = sb(nc, c2, "mixer_features", [P, 3, F])
            feat_t = sb(nc, c2, "mixer_features_t", [128, 2, 2, P])
            inv = sb(nc, c2, "mixer_inverse", [P, 4])
            NU = HEADS * T
            with phase(nc, "zeroed", "loaded", "product", "maxed", "expd", "added", "taken", "shifted") as (
                    block, zeroed, loaded, product, maxed, expd, added, taken, shifted):
                @block.gpsimd
                def _(pool):
                    pool.memset(pm[:, :, :], 0.0).then_inc(zeroed, 1)

                @block.sync
                def _(sp):
                    sp.wait_ge(zeroed, 1)
                    for h in range(2):
                        sp.dma_start(pm[head(h), h, :], a["L1_mix_Pmat"]).then_inc(loaded, 16)

                @block.tensor
                def _(pe):
                    def sums(n):
                        h, i = n // T, n % T
                        if i == 0 and h >= 2:
                            pe.wait_ge(taken, h - 1)
                        pe.wait_ge(expd, n + 1)
                        for f in range(2):
                            ins = pe.matmul(m.ps[:, 4 + h % 2, 65 * f:65 * f + 65], feat[:, n % 3, f * 128:(f + 1) * 128], v[:, i, h, :],
                                            start=i == 0 and f == 0, stop=i == T - 1, skip_group_check=True)
                        ins.then_inc(added, 1)

                    pe.wait_ge(loaded, 32)
                    for n in range(NU + 2):
                        if n < NU:
                            h, i = n // T, n % T
                            if n >= 4:
                                pe.wait_ge(expd, n - 3)
                            pe.matmul(m.ps[0:P, n % 4, 0:F], kt[:, h // 2, tile(i)], pm[:, h % 2, :], start=True, stop=True).then_inc(product, 1)
                        if n >= 2:
                            sums(n - 2)

                @block.vector
                def _(dve):
                    def take(h):
                        dve.wait_ge(added, T * (h + 1))
                        dve.tensor_scalar(kvs[:, h, :, :], m.ps[:, 4 + h % 2, 0:130].rearrange("p (f c) -> p f c", f=2),
                                          F ** -0.5, None, ALU.mult).then_inc(taken, 1)

                    for n in range(NU):
                        dve.wait_ge(product, n + 1)
                        if n >= 4:
                            dve.wait_ge(expd, n - 3)
                        dve.tensor_reduce(nm[:, n % 4:n % 4 + 1], m.ps[0:P, n % 4, 0:F], AX.X, ALU.max, negate=True).then_inc(maxed, 1)
                        if n % T == 4 and n > T:
                            take(n // T - 1)
                    take(HEADS - 1)
                    dve.wait_ge(taken, HEADS)
                    dve.tensor_scalar(kvs[:, :, :, 64:65], kvs[:, :, :, 64:65], 1e-6, None, ALU.add).then_inc(shifted, 1)

                @block.scalar
                def _(act):
                    for n in range(NU):
                        act.wait_ge(maxed, n + 1)
                        if n >= 3:
                            act.wait_ge(added, n - 2)
                        act.activation(feat[:, n % 3, :], m.ps[0:P, n % 4, 0:F], ACT.Exp, bias=nm[:, n % 4:n % 4 + 1]).then_inc(expd, 1)

            with phase(nc, "product", "maxed", "expd", "turned", "kept", "out", "inverted", "done") as (
                    block, product, maxed, expd, turned, kept, out, inverted, done):
                @block.tensor
                def _(pe):
                    for n in range(NU + 4):
                        if n < NU:
                            h, i = n // T, n % T
                            if n >= 4:
                                pe.wait_ge(expd, n - 3)
                            pe.matmul(m.ps[0:P, n % 4, 0:F], qt[:, h // 2, tile(i)], pm[:, h % 2, :], start=True, stop=True).then_inc(product, 1)
                        if 2 <= n < NU + 2:
                            u = n - 2
                            pe.wait_ge(expd, u + 1)
                            if u >= 2:
                                pe.wait_ge(kept, u - 1)
                            for f in range(2):
                                ins = pe.transpose(m.ps[:, 4 + u % 2, f * P:(f + 1) * P], feat[:, u % 3, f * 128:(f + 1) * 128], m.ident[0:P, 0:P])
                            ins.then_inc(turned, 1)
                        if n >= 4:
                            u = n - 4
                            pe.wait_ge(kept, u + 1)
                            if u >= 2:
                                pe.wait_ge(done, u - 1)
                            for f in range(2):
                                ins = pe.matmul(m.ps[0:P, 6 + u % 2, 0:65], feat_t[:, u % 2, f, :], kvs[:, u // T, f, :], start=f == 0, stop=f == 1)
                            ins.then_inc(out, 1)

                @block.vector
                def _(dve):
                    def finish(u):
                        h, i = u // T, u % T
                        dve.wait_ge(out, u + 1)
                        dve.reciprocal(inv[:, u % 4:u % 4 + 1], m.ps[0:P, 6 + u % 2, 64:65]).then_inc(inverted, 1)
                        dve.wait_ge(inverted, u + 1)
                        dve.tensor_scalar(attn[:, i, 64 * h:64 * h + 64], m.ps[0:P, 6 + u % 2, 0:64], inv[:, u % 4:u % 4 + 1], None,
                                          ALU.mult).then_inc(done, 1)

                    for n in range(NU + 4):
                        if n < NU:
                            dve.wait_ge(product, n + 1)
                            if n >= 4:
                                dve.wait_ge(expd, n - 3)
                            dve.tensor_reduce(nm[:, n % 4:n % 4 + 1], m.ps[0:P, n % 4, 0:F], AX.X, ALU.max, negate=True).then_inc(maxed, 1)
                        if n >= 4:
                            finish(n - 4)

                @block.scalar
                def _(act):
                    for n in range(NU + 2):
                        if n < NU:
                            act.wait_ge(maxed, n + 1)
                            if n >= 3:
                                act.wait_ge(turned, n - 2)
                            act.activation(feat[:, n % 3, :], m.ps[0:P, n % 4, 0:F], ACT.Exp, bias=nm[:, n % 4:n % 4 + 1]).then_inc(expd, 1)
                        if n >= 2:
                            u = n - 2
                            act.wait_ge(turned, u + 1)
                            if u >= 2:
                                act.wait_ge(out, u - 1)
                            act.activation(feat_t[:, u % 2, :, :], m.ps[:, 4 + u % 2, 0:2 * P].rearrange("p (f t) -> p f t", f=2),
                                           ACT.Copy).then_inc(kept, 1)

        transpose_rows_phase(nc, m, attn, m.xt)
        add_product(nc, m, "mixer_proj_", pieces(a["L1_mix_Wproj"], 2))
        w2 = sb(nc, ctx, "mixer_w2", [128, H2 // 128, D])
        b1 = sb(nc, ctx, "mixer_b1", [128, H2 // 128])
        rows = sb(nc, ctx, "mixer_rows", [P, 2, D])
        hid = sb(nc, ctx, "mixer_hidden", [128, H2 // 128, N])
        move(nc, [(w2[:, :, :], wview(a["L1_mix_W2"])), (b1[:, :], a["L1_mix_b1"]),
                  (rows[:, 0, :], spread_row(a["L1_mix_bproj"])), (rows[:, 1, :], spread_row(a["L1_mix_b2"]))])
        add_rows(nc, m, rows[:, 0, :])
        layernorm_phase(nc, m, m.x, lambda i: m.tmp[:, i % 2, :], m.xt, gain_col=cols[:, 2, :], bias_col=cols[:, 3, :])

        def hidden_take(j, g, act, bank, on_act):
            f, (c0, cn) = 2 * j + g[1], CH[g[2]]
            return act.activation(hid[:, f, c0:c0 + cn], bank[:, 0:cn], ACT.Gelu, bias=b1[:, f:f + 1])

        split_gemm_phase(nc, m, "mixer_hidden_", pieces(a["L1_mix_W1"], 4), 256,
                         [[("feature", f, c) for c in range(len(CH)) for f in range(2)]] * 4, hidden_take, takers="act")
        vector_groups_phase(nc, m, T, lambda n, bank: [(bank[0:P, :], hid[:, k, tile(n)], w2[:, k, :]) for k in range(H2 // 128)],
                            lambda n, dve, bank: dve.tensor_tensor(m.x[:, n, :], bank[0:P, :], m.x[:, n, :], ALU.add))
        add_rows(nc, m, rows[:, 1, :])
        add_into_saved(nc, m, a, tok, attn)


def transpose_rows_phase(nc, m, src, dst):
    with phase(nc, "turned", "kept") as (block, turned, kept):
        @block.tensor
        def _(pe):
            for i in range(T):
                if i >= 4:
                    pe.wait_ge(kept, i - 3)
                for k in range(KB):
                    ins = pe.transpose(m.ps[:, i % 4, k * P:(k + 1) * P], src[:, i, k * 128:(k + 1) * 128], m.ident[0:P, 0:P])
                ins.then_inc(turned, 1)

        @block.scalar
        def _(act):
            for i in range(T):
                act.wait_ge(turned, i + 1)
                act.activation(dst[:, :, tile(i)], m.ps[:, i % 4, 0:KB * P].rearrange("p (k t) -> p k t", k=KB), ACT.Copy).then_inc(kept, 1)



def l1_ffn(nc, m, a, tok):
    L, NE, H = 4, 8, 256
    with ExitStack() as ctx:
        layernorm_phase(nc, m, m.x, lambda i: m.x[:, i, :])
        cols = sb(nc, ctx, "ln_cols", [128, 4, KB])
        rows = sb(nc, ctx, "row", [P, D])
        with nc.Fori(0, L) as l:
            at = lambda v, pat="a p k -> (a p) k": v[bass.ds(l, 1)].rearrange(pat)
            move(nc, [(cols[:, j, :], at(c)) for j, c in enumerate((a["L1_ffn_ln1_w"], a["L1_ffn_ln1_b"], a["L1_ffn_ln2_w"], a["L1_ffn_ln2_b"]))]
                 + [(rows[:, :], a["L1_ffn_out_b"][bass.ds(l, 1), :].to_broadcast([P, D]))])
            layernorm_phase(nc, m, m.x, lambda i: m.tmp[:, i % 2, :], m.xt, gain_col=cols[:, 0, :], bias_col=cols[:, 1, :])
            with ExitStack() as c2:
                qt = sb(nc, c2, "ffn_qt", [128, KB, N])
                kt = sb(nc, c2, "ffn_kt", [128, KB, N])
                v = sb(nc, c2, "ffn_v", [P, T, KB, 192])
                ones_between(nc, v)
                w = a["L1_ffn_qkv_w"][bass.ds(l, 1)].rearrange("a (k p) f -> p (a k) f", p=128)
                qkv_for_attention(nc, m, "ffn_qkv_", [w[:, :, 256 * j:256 * j + 256] for j in range(6)], qt, kt, v)
                attention(nc, m, "ffn_", qt, kt, v, m.xt)
            with ExitStack() as c2:
                wo = a["L1_ffn_out_w"][bass.ds(l, 1)].rearrange("a (k p) f -> p (a k) f", p=128)
                add_product(nc, m, "ffn_out_", [wo[:, :, 256 * j:256 * j + 256] for j in range(2)])
                add_rows(nc, m, rows)
                layernorm_phase(nc, m, m.x, lambda i: m.tmp[:, i % 2, :], m.xt, gain_col=cols[:, 2, :], bias_col=cols[:, 3, :])
                moe(nc, m, a, l, c2, NE, H)
        row2 = sb(nc, ctx, "final_rows", [P, 2, D])
        xs = sb(nc, ctx, "block_input", [P, T, D])
        layernorm_phase(nc, m, m.x, lambda i: m.xt_rows[:, i, :], None, gain_row=row2[:, 0, :], bias_row=row2[:, 1, :],
                        loads=[(xs[:, :, :], tok(a["xs"])), (row2[:, 0, :], spread_row(a["L1_ffn_fln_w"])), (row2[:, 1, :], spread_row(a["L1_ffn_fln_b"]))])
        with phase(nc, "added", "stored") as (block, added, stored):
            @block.vector
            def _(dve):
                for i in range(T):
                    dve.tensor_tensor(xs[:, i, :], xs[:, i, :], m.xt_rows[:, i, :], ALU.add).then_inc(added, 1)

            @block.sync
            def _(sp):
                out = tok(a["out"])
                for i in range(T):
                    sp.wait_ge(added, i + 1)
                    sp.dma_start(out[:, i, :], xs[:, i, :]).then_inc(stored, 16)
                sp.wait_ge(stored, 16 * T)


def moe(nc, m, a, l, ctx, NE, H):
    wg = sb(nc, ctx, "ffn_w_gate", [128, KB, NE])
    logit = sb(nc, ctx, "logits", [P, T, 2 * NE])
    struck = sb(nc, ctx, "struck", [P, T, 2 * NE])
    best = sb(nc, ctx, "top", [P, T, 8])
    only2 = sb(nc, ctx, "top2", [P, T, 8])
    d = sb(nc, ctx, "logit_shifted", [P, T, NE])
    e = sb(nc, ctx, "logit_exp", [P, T, NE])
    eg = sb(nc, ctx, "chosen_exp", [P, T, NE])
    den = sb(nc, ctx, "gate_sum", [P, T])
    inv = sb(nc, ctx, "gate_inv", [P, T])
    gates = sb(nc, ctx, "moe_gates", [P, T, NE])
    gates_t = sb(nc, ctx, "gates_t", [128, N])
    eb1 = sb(nc, ctx, "eb1", [128, 2, H // 128])
    eb2 = sb(nc, ctx, "eb2", [128, D])
    FB = H // 128
    xh = sb(nc, ctx, "moe_x_high", [128, KB, N], F32R)
    xl = sb(nc, ctx, "moe_x_low", [128, KB, N], F32R)
    w1 = sb(nc, ctx, "ew1", [128, 2, KB, H])
    w1h = sb(nc, ctx, "ew1_high", [128, 2, KB, H], F32R)
    w1l = sb(nc, ctx, "ew1_low", [128, 2, KB, H], F32R)
    w2 = sb(nc, ctx, "ew2", [128, 2, FB, D])
    w2h = sb(nc, ctx, "ew2_high", [128, 2, FB, D], F32R)
    w2l = sb(nc, ctx, "ew2_low", [128, 2, FB, D], F32R)
    hid = sb(nc, ctx, "expert_hidden", [128, 3, 512])
    hh = sb(nc, ctx, "expert_hidden_high", [128, FB, N], F32R)
    hl = sb(nc, ctx, "expert_hidden_low", [128, FB, N], F32R)
    NG = 3 * FB
    SLOTS = 5
    w1_all = a["L1_ffn_ew1"].rearrange("l e (k p) f -> (l e) p k f", p=128)
    eb1_all = a["L1_ffn_eb1"].rearrange("l e p k -> (l e) p k")
    w2_all = a["L1_ffn_ew2"].rearrange("l e (k p) f -> (l e) p k f", p=128)

    def load_pairs(expert, c):
        own = lambda v: v[bass.ds(expert, 1)]
        return [(w1[:, c, :, :], own(w1_all).rearrange("a p k f -> (a p) k f")), (w2[:, c, :, :], own(w2_all).rearrange("a p k f -> (a p) k f")),
                (eb1[:, c, :], own(eb1_all).rearrange("a p k -> (a p) k"))]

    def round_weights(act, c):
        act.activation(w1h[:, c, :, :], w1[:, c, :, :], ACT.Copy)
        return act.activation(w2h[:, c, :, :], w2[:, c, :, :], ACT.Copy)

    def rest_weights(pool, c):
        pool.tensor_tensor(w1l[:, c, :, :], w1[:, c, :, :], w1h[:, c, :, :].bitcast(F32), ALU.subtract)
        return pool.tensor_tensor(w2l[:, c, :, :], w2[:, c, :, :], w2h[:, c, :, :].bitcast(F32), ALU.subtract)

    by_token = lambda ap: ap.rearrange("p (t a) -> p t a", a=1).to_broadcast([P, T, NE])
    with phase(nc, "loaded", "first", "w_rounded", "x_rounded", "rest", "padded", "filled", "product", "taken", "maxed", "two", "strike",
               "v_step", "a_step", "t_step") as (
            block, loaded, first, w_rounded, x_rounded, rest, padded, filled, product, taken, maxed, two, strike, v_step, a_step, t_step):
        @block.gpsimd
        def _(pool):
            pool.memset(gates_t[:, :], 0.0).then_inc(padded, 1)
            pool.memset(eb2[:, :], 0.0).then_inc(padded, 1)
            for c, (c0, cn) in enumerate(CH):
                pool.wait_ge(x_rounded, c + 1)
                pool.tensor_tensor(xl[:, :, c0:c0 + cn], m.xt[:, :, c0:c0 + cn], xh[:, :, c0:c0 + cn].bitcast(F32), ALU.subtract).then_inc(rest, 1)
            pool.wait_ge(w_rounded, 1)
            rest_weights(pool, 0).then_inc(rest, 1)

        @block.sync
        def _(sp):
            sp.dma_start(wg[:, :, :], a["L1_ffn_w_gate"][bass.ds(l, 1)].rearrange("a (k p) f -> p (a k) f", p=128)).then_inc(loaded, 16)
            sp.wait_ge(padded, 2)
            sp.dma_start(eb2[0:NE, :], a["L1_ffn_eb2"][bass.ds(l, 1)].rearrange("a e f -> (a e) f")).then_inc(first, 16)
            for dst, src in load_pairs(l * NE, 0):
                sp.dma_start(dst, src).then_inc(first, 16)

        @block.tensor
        def _(pe):
            pe.wait_ge(loaded, 16)
            for i in range(T):
                if i >= 4:
                    pe.wait_ge(taken, i - 3)
                for k in range(KB):
                    ins = pe.matmul(m.ps[0:P, i % 4, 0:NE], m.xt[:, k, tile(i)], wg[:, k, :], start=k == 0, stop=k == KB - 1)
                ins.then_inc(product, 1)
            pe.wait_ge(v_step, 5)
            for i in range(T):
                ins = pe.transpose(m.ps[0:NE, 4 + i // 4, (i % 4) * P:(i % 4 + 1) * P], gates[:, i, :], m.ident[0:P, 0:P])
            ins.then_inc(t_step, 1)

        @block.vector
        def _(dve):
            dve.memset(logit[:, :, NE:2 * NE], -BIG).then_inc(filled, 1)
            dve.memset(only2[:, :, :], -BIG).then_inc(filled, 1)
            for i in range(T):
                dve.wait_ge(product, i + 1)
                dve.tensor_copy(logit[:, i, 0:NE], m.ps[0:P, i % 4, 0:NE]).then_inc(taken, 1)
            dve.wait_ge(filled, 2)
            for i in range(T):
                dve.wait_ge(taken, i + 1)
                dve.max(best[:, i, :], logit[:, i, :]).then_inc(maxed, 1)
            dve.wait_ge(maxed, T)
            dve.tensor_copy(only2[:, :, 0:2], best[:, :, 0:2]).then_inc(two, 1)
            dve.tensor_tensor(d[:, :, :], logit[:, :, 0:NE], best[:, :, 0:1].to_broadcast([P, T, NE]), ALU.subtract).then_inc(v_step, 1)
            dve.wait_ge(two, 1)
            for i in range(T):
                dve.match_replace(struck[:, i, :], only2[:, i, :], logit[:, i, :], BIG).then_inc(strike, 1)
            dve.wait_ge(strike, T)
            dve.wait_ge(a_step, 1)
            dve.scalar_tensor_tensor(eg[:, :, :], struck[:, :, 0:NE], BIG, e[:, :, :], ALU.is_equal, ALU.mult).then_inc(v_step, 1)
            dve.wait_ge(v_step, 2)
            dve.tensor_reduce(den[:, :], eg[:, :, :], AX.X, ALU.add).then_inc(v_step, 1)
            dve.wait_ge(v_step, 3)
            dve.reciprocal(inv[:, :], den[:, :]).then_inc(v_step, 1)
            dve.wait_ge(v_step, 4)
            dve.tensor_tensor(gates[:, :, :], eg[:, :, :], by_token(inv[:, :]), ALU.mult).then_inc(v_step, 1)

        @block.scalar
        def _(act):
            for c0, cn in CH:
                act.activation(xh[:, :, c0:c0 + cn], m.xt[:, :, c0:c0 + cn], ACT.Copy).then_inc(x_rounded, 1)
            act.wait_ge(first, 64)
            round_weights(act, 0).then_inc(w_rounded, 1)
            act.wait_ge(padded, 2)
            act.wait_ge(v_step, 1)
            act.activation(e[:, :, :], d[:, :, :], ACT.Exp).then_inc(a_step, 1)
            act.wait_ge(t_step, 1)
            for c0, cn in CH:
                ins = act.activation(gates_t[0:NE, c0:c0 + cn], m.ps[0:NE, 4 + c0 // 500, 0:cn], ACT.Copy)
            ins.then_inc(a_step, 1)

    with phase(nc, "w_rounded", "w_ready", "w_next_a", "w_next_b", "h_product", "h_taken", "h_rounded", "h_ready", "y_product", "y_taken") as (
            block, w_rounded, w_ready, w_next_a, w_next_b, h_product, h_taken, h_rounded, h_ready, y_product, y_taken):
        arrived = (w_next_a, w_next_b)
        STEPS = NE // 2

        @block.sync
        def _(sp):
            def load(expert, c):
                for dst, src in load_pairs(expert, c):
                    sp.dma_start(dst, src).then_inc(arrived[c], 16)

            load(l * NE + 1, 1)
            with sp.Fori(0, STEPS - 1) as it:
                for c in range(2):
                    sp.wait_ge(y_product, 2 * T * it + T * (c + 2))
                    load(l * NE + 2 * it + 2 + c, c)

        @block.tensor
        def _(pe):
            def expert(it, c):
                for g in range(NG):
                    f, (c0, cn) = g % FB, CH[g // FB]
                    pe.wait_ge(h_taken, 2 * NG * it + NG * c + g + 1)
                    for k in range(KB):
                        for q, (x, w) in enumerate(((xh, w1h), (xl, w1h), (xh, w1l))):
                            ins = pe.matmul(m.ps[:, g % 3, 0:cn], w[:, c, k, f * 128:(f + 1) * 128], x[:, k, c0:c0 + cn],
                                            start=k == 0 and q == 0, stop=k == KB - 1 and q == 2)
                    ins.then_inc(h_product, 1)
                for i in range(T):
                    n = T * c + i
                    pe.wait_ge(h_ready, 2 * NG * it + NG * c + FB * (i // 4 + 1) + 3)
                    pe.wait_ge(y_taken, 2 * T * it + n + 1 - SLOTS + T)
                    for k in range(FB):
                        for q, (x, w) in enumerate(((hh, w2h), (hl, w2h), (hh, w2l))):
                            ins = pe.matmul(m.ps[0:P, 3 + n % SLOTS, :], x[:, k, tile(i)], w[:, c, k, :],
                                            start=k == 0 and q == 0, stop=k == FB - 1 and q == 2)
                    ins.then_inc(y_product, 1)

            for i in range(T):
                if i >= SLOTS:
                    pe.wait_ge(y_taken, i - SLOTS + 1)
                pe.matmul(m.ps[0:P, 3 + i % SLOTS, :], gates_t[:, tile(i)], eb2[:, :], start=True, stop=True).then_inc(y_product, 1)
            with pe.Fori(0, STEPS) as it:
                for c in range(2):
                    pe.wait_ge(w_ready, 2 * it + c + 1)
                    expert(it, c)

        @block.gpsimd
        def _(pool):
            def expert(it, c):
                for g in range(NG):
                    f, (c0, cn) = g % FB, CH[g // FB]
                    pool.wait_ge(h_rounded, 2 * NG * it + NG * c + g + 1)
                    pool.tensor_tensor(hl[:, f, c0:c0 + cn], hid[:, g % 3, 0:cn], hh[:, f, c0:c0 + cn].bitcast(F32),
                                       ALU.subtract).then_inc(h_ready, 1)

            def next_weights(it, c):
                pool.wait_ge(w_rounded, 2 * it + c + 1)
                rest_weights(pool, 1 - c).then_inc(w_ready, 1)

            pool.sem_inc(h_ready, 3)
            pool.sem_inc(w_ready, 1)
            with pool.Fori(0, STEPS - 1) as it:
                for c in range(2):
                    expert(it, c)
                    next_weights(it, c)
            expert(STEPS - 1, 0)
            next_weights(STEPS - 1, 0)
            expert(STEPS - 1, 1)

        @block.scalar
        def _(act):
            def expert(it, c):
                for g in range(NG):
                    f, (c0, cn) = g % FB, CH[g // FB]
                    act.wait_ge(h_product, 2 * NG * it + NG * c + g + 1)
                    act.wait_ge(h_ready, 2 * NG * it + NG * c + g + 1)
                    act.activation(hid[:, g % 3, 0:cn], m.ps[:, g % 3, 0:cn], ACT.Gelu, bias=eb1[:, c, f:f + 1]).then_inc(h_taken, 1)
                    act.wait_ge(h_taken, 2 * NG * it + NG * c + g + 4)
                    act.activation(hh[:, f, c0:c0 + cn], hid[:, g % 3, 0:cn], ACT.Copy).then_inc(h_rounded, 1)

            act.sem_inc(h_taken, 3)
            with act.Fori(0, STEPS - 1) as it:
                for c in range(2):
                    expert(it, c)
                    act.wait_ge(arrived[1 - c], 48 * it + 48)
                    round_weights(act, 1 - c).then_inc(w_rounded, 1)
            expert(STEPS - 1, 0)
            act.wait_ge(arrived[1], 48 * STEPS)
            round_weights(act, 1).then_inc(w_rounded, 1)
            expert(STEPS - 1, 1)

        @block.vector
        def _(dve):
            for i in range(T):
                dve.wait_ge(y_product, i + 1)
                dve.tensor_tensor(m.x[:, i, :], m.ps[0:P, 3 + i % SLOTS, :], m.x[:, i, :], ALU.add).then_inc(y_taken, 1)
            with dve.Fori(0, STEPS) as it:
                for c in range(2):
                    for i in range(T):
                        n = T * c + i
                        dve.wait_ge(y_product, 2 * T * it + n + 1 + T)
                        dve.wait_ge(y_taken, 2 * T * it + n + 1)
                        dve.scalar_tensor_tensor(m.x[:, i, :], m.ps[0:P, 3 + n % SLOTS, :], gates[:, i, bass.ds(2 * it + c, 1)], m.x[:, i, :],
                                                 ALU.mult, ALU.add).then_inc(y_taken, 1)



def program(nc, a, stop=None):
    ctx = ExitStack()
    with ctx:
        m = Tensors()
        m.ps = ctx.enter_context(nc.psum_tensor("ps", [128, 8, 512], F32))
        m.gathered = [ctx.enter_context(nc.semaphore(f"gathered{u}")) for u in range(2 * G)]
        m.ident = sb(nc, ctx, "ident", [128, 128])
        m.eps = sb(nc, ctx, "eps", [128, 1])
        m.ones = sb(nc, ctx, "ones", [128, 128])
        m.xraw = sb(nc, ctx, "x", [128, T * D])
        m.x = m.xraw[0:P, :].rearrange("p (t d) -> p t d", t=T)
        xt_raw = sb(nc, ctx, "xt", [128, T * D])
        m.xt = xt_raw[:, 0:KB * N].rearrange("p (k n) -> p k n", k=KB)
        m.xt_rows = xt_raw[0:P, :].rearrange("p (t d) -> p t d", t=T)
        m.bn = sb(nc, ctx, "bn", [P, T, 6])
        m.mv = sb(nc, ctx, "mv", [P, T, 2])
        m.sd = sb(nc, ctx, "sd", [P, T])
        m.rstd = sb(nc, ctx, "rstd", [P, T])
        m.tmp4 = sb(nc, ctx, "tmp", [P, 4, D])
        m.tmp = m.tmp4[:, 0:2, :]
        m.tmp2 = m.tmp4[:, 2:4, :]
        tok = lambda v: v.rearrange("(t p) d -> p t d", p=P)
        ring = lambda i: m.tmp[:, i % 2, :]

        with phase(nc, "made", "loaded") as (block, made, loaded):
            @block.gpsimd
            def _(pool):
                pool.memset(m.ident[:, :], 0.0).then_inc(made, 1)
                pool.memset(m.eps[:, :], EPS).then_inc(made, 1)
                pool.memset(m.ones[:, :], 1.0)
                pool.wait_ge(made, 2)
                pool.affine_select(out=m.ident[:, :], in_=m.ident[:, :], compare_op=ALU.not_equal, fill=1.0,
                                   base=0, pattern=[[-1, 128]], channel_multiplier=1).then_inc(made, 1)

            @block.sync
            def _(sp):
                sp.dma_start(m.x[:, :, :], tok(a["x"])).then_inc(loaded, 16)
                sp.wait_ge(loaded, 16)

        cctx = ctx.enter_context(ExitStack())
        m.cnt = sb(nc, cctx, "cnt", [P, T, NPAD])
        l0_gnn(nc, m, a, tok, ring)
        if stop == "gnn0":
            return
        l0_mix(nc, m, a)
        if stop == "mix0":
            return
        l0_ffn(nc, m, a)
        if stop == "ffn0":
            return
        l1_gnn(nc, m, a, tok)
        cctx.close()
        if stop == "gnn1":
            return
        l1_mix(nc, m, a, tok)
        if stop == "mix1":
            return
        l1_ffn(nc, m, a, tok)


def l0_gnn(nc, m, a, tok, ring):
    with ExitStack() as ctx:
        m.acc = sb(nc, ctx, "acc", [128, 8, NPAD])
        with ExitStack() as c2:
            up = sb(nc, c2, "w_up", [128, 2, MUL])
            res = sb(nc, c2, "up_rows", [P, 2, D])
            by_channel = lambda ap, k: ap[:, 0:128] if k == 0 else ap[:, 128 + k - 1:512:3]
            layernorm_phase(nc, m, m.x, ring, m.xt, cols=by_channel)

            def operands(n, bank):
                return [(bank[0:P, k * 128:(k + 1) * 128], m.xt[:, k, tile(n)], up[:, min(k, 1), :]) for k in range(KB)]

            with phase(nc, "loaded", "product", "taken", "st_a", "st_b") as (block, loaded, product, taken, st_a, st_b):
                stored = (st_a, st_b)

                @block.sync
                def _(sp):
                    sp.dma_start(up[:, 0, :], a["L0_gnn_W_up0"]).then_inc(loaded, 16)
                    sp.dma_start(up[:, 1, :], a["L0_gnn_W_up1"]).then_inc(loaded, 16)
                    for i in range(T):
                        sp.wait_ge(taken, i + 1)
                        sp.dma_start(a["xup"][tile(i), :], res[:, i % 2, :]).then_inc(stored[i % 2], 16)
                    for s in stored:
                        sp.wait_ge(s, 16 * T // 2)

                @block.tensor
                def _(pe):
                    pe.wait_ge(loaded, 32)
                    for i in range(T):
                        if i >= 8:
                            pe.wait_ge(taken, i - 7)
                        for out, lhsT, rhs in operands(i, m.ps[:, i % 8, :]):
                            ins = pe.matmul(out, lhsT, rhs, start=True, stop=True)
                        ins.then_inc(product, 1)

                @block.scalar
                def _(act):
                    for i in range(T):
                        act.wait_ge(product, i + 1)
                        if i >= 2:
                            act.wait_ge(stored[i % 2], 16 * (i // 2))
                        act.activation(res[:, i % 2, :], m.ps[0:P, i % 8, :], ACT.Copy, scale=MUL ** -0.5).then_inc(taken, 1)

        edge_mlp_phase(nc, m, a["ef_t"], a["L0_gnn_W_mlp1"], a["L0_gnn_W_mlp2"], a["L0_gnn_W_mlp3"], a["h3"])
        with ExitStack() as c2:
            m.iota = sb(nc, c2, "iota", [P, N])
            with phase(nc, "made") as (block, made):
                @block.gpsimd
                def _(pool):
                    pool.iota(m.iota[:, :], pattern=[[1, N]], base=0, channel_multiplier=0,
                              allow_small_or_imprecise_dtypes=True).then_inc(made, 1)
            edges(nc, m, a, c2)
        with ExitStack() as c2:
            wo = sb(nc, c2, "w_out", [128, 2, 2, MUL])

            def operands(n, bank):
                t = tile(n)
                blocks = [(4, 3, 0)] + [(k, 5 + k, 1) for k in range(3)]
                out = []
                for k in range(4):
                    first, second = (3, 4) if k == 0 else (k - 1, 4 + k)
                    for j, blk in enumerate((first, second)):
                        out.append((k, j, m.acc[:, blk, t], wo[:, min(k, 1), j, :]))
                return out

            with phase(nc, "loaded", "product", "taken") as (block, loaded, product, taken):
                @block.sync
                def _(sp):
                    for k, w in enumerate((a["L0_gnn_W_out0"], a["L0_gnn_W_out1"])):
                        sp.dma_start(wo[:, k, :, :], wview(w)).then_inc(loaded, 16)

                @block.tensor
                def _(pe):
                    pe.wait_ge(loaded, 32)
                    for i in range(T):
                        if i >= 8:
                            pe.wait_ge(taken, i - 7)
                        for k, j, lhsT, rhs in operands(i, None):
                            ins = pe.matmul(m.ps[0:P, i % 8, k * 128:(k + 1) * 128], lhsT, rhs, start=j == 0, stop=j == 1)
                        ins.then_inc(product, 1)

                @block.vector
                def _(dve):
                    scale = (2 * MUL) ** -0.5 / 10.0
                    for i in range(T):
                        dve.wait_ge(product, i + 1)
                        dve.scalar_tensor_tensor(m.x[:, i, 0:128], m.ps[0:P, i % 8, 0:128], scale, m.x[:, i, 0:128], ALU.mult, ALU.add)
                        vec = m.x[:, i, 128:512].rearrange("p (v k) -> p k v", k=3)
                        dve.scalar_tensor_tensor(vec, m.ps[0:P, i % 8, 128:512].rearrange("p (k v) -> p k v", k=3),
                                                 scale, vec, ALU.mult, ALU.add).then_inc(taken, 1)



COLUMNS = ("L0_mix_b_in", "L1_gnn_b1", "L1_mix_b1", "L1_mix_g1", "L1_mix_be1", "L1_mix_g2", "L1_mix_be2",
           "L1_ffn_ln1_w", "L1_ffn_ln1_b", "L1_ffn_ln2_w", "L1_ffn_ln2_b", "L1_ffn_eb1")


def layouts(inputs):
    import numpy as np
    out = {}
    for k, v in inputs.items():
        out[k] = np.asarray(v)
    by_super = lambda v: np.ascontiguousarray(np.asarray(v).reshape(SB, P, G, -1).transpose(1, 0, 2, 3))
    out["src_l"] = by_super(out.pop("src"))[..., 0].copy()
    out["dst_l"] = by_super(out.pop("dst"))[..., 0].copy()
    out["ea4_l"] = by_super(out.pop("edge_attr_4"))
    ef = out.pop("edge_attr_8").reshape(SB, P, G, 8)
    out["ef_t"] = np.ascontiguousarray(ef.transpose(3, 0, 2, 1).reshape(8, E))
    w = out["L0_mix_W_in"]
    out["L0_mix_W_in"] = np.concatenate([w[:MUL]] + [w[MUL + k::3] for k in range(3)])
    out["L1_mix_bqk"] = np.ascontiguousarray(out["L1_mix_bqkv"].reshape(12, 128).T)
    for k, v in list(out.items()):
        if k in COLUMNS:
            out[k] = np.ascontiguousarray(np.moveaxis(v.reshape(v.shape[:-1] + (-1, 128)), -1, -2))
    return out


def build(nc, arrays, stop=None):
    from concourse import mybir as _mybir
    a = {name: nc.dram_tensor(f"in_{name}", v.shape, _mybir.dt.from_np(v.dtype), kind="ExternalInput").ap()
         for name, v in arrays.items()}
    a["out"] = nc.dram_tensor("out", (N, D), F32, kind="ExternalOutput").ap()
    a["xs"] = nc.dram_tensor("xs", (N, D), F32).ap()
    a["xn"] = nc.dram_tensor("xn", (N, D), F32).ap()
    a["xup"] = nc.dram_tensor("xup", (N, D), F32).ap()
    a["h3"] = nc.dram_tensor("h3", (HID, E), F32).ap()
    program(nc, a, stop)


def kernel(**inputs):
    import concourse.bacc as _bacc
    from concourse.bass_utils import run_bass_kernel_spmd as _run
    nc = _bacc.Bacc("TRN2", target_bir_lowering=False, num_devices=1)
    arrays = layouts(inputs)
    build(nc, arrays)
    r = _run(nc, [{f"in_{k}": v for k, v in arrays.items()}], core_ids=[0])
    return r.results[0]["out"]
```

```python
from contextlib import ExitStack, contextmanager

import concourse.bass as bass
from concourse import mybir

F32 = mybir.dt.float32
F32R = mybir.dt.float32r
BF16 = mybir.dt.bfloat16
I32 = mybir.dt.int32
U32 = mybir.dt.uint32
ALU = mybir.AluOpType
ACT = mybir.ActivationFunctionType
AX = mybir.AxisListType
RMAX = bass.bass_isa.ReduceOp.max

N, D = 1250, 512
P, T = 125, 10
KB = D // 128
E = 21250
G = 5
SB = E // (P * G)
W = 64
NPAD = N + W
MUL = 128
HID = 64
HEADS, DH = 8, 64
SILU_2MOM = 1.679177
CH = [(0, 500), (500, 500), (1000, 250)]
EPS = 1e-5
BIG = 3.0e38


class Tensors:
    pass


@contextmanager
def phase(nc, *names, held=()):
    with ExitStack() as ctx:
        sems = [ctx.enter_context(nc.semaphore(n)) for n in names]
        with nc.Block() as block:
            yield (block, *sems)
        for s in sems:
            nc.sync.sem_clear(s)
        if held:
            nc.gpsimd.dma_reset(range(held[0].num, held[-1].num + 1))
            for s in held:
                nc.gpsimd.sem_clear(s)
        nc.all_engine_barrier()


def sb(nc, ctx, name, shape, dt=F32):
    return ctx.enter_context(nc.sbuf_tensor(name, shape, dt))


def tile(i):
    return slice(i * P, (i + 1) * P)



def load_phase(nc, pairs):
    with phase(nc, "loaded") as (block, loaded):
        @block.sync
        def _(sp):
            for dst, src in pairs:
                sp.dma_start(dst, src).then_inc(loaded, 16)
            sp.wait_ge(loaded, 16 * len(pairs))


def layernorm_phase(nc, m, src, normed, transposed=None, cols=None, gain_col=None, bias_col=None,
                    gain_row=None, bias_row=None, loads=()):
    cols = cols or (lambda ap, k: ap[:, k * 128:(k + 1) * 128])
    with phase(nc, "loaded", "stats", "moments", "spread", "inverse", "centred", "scaled", "ready",
               "turned", "kept", "last_kept") as (block, loaded, stats, moments, spread, inverse, centred, scaled,
                                                  ready, turned, kept, last_kept):
        @block.sync
        def _(sp):
            for dst, s in loads:
                sp.dma_start(dst, s).then_inc(loaded, 16)
            if loads:
                sp.wait_ge(loaded, 16 * len(loads))

        HALF = T // 2

        @block.vector
        def _(dve):
            def raw(i):
                dve.bn_stats(m.bn[:, i, :], src[:, i, :]).then_inc(stats, 1)

            def moment(i):
                dve.wait_ge(stats, i + 1)
                dve.bn_aggr(m.mv[:, i, :], m.bn[:, i, :]).then_inc(moments, 1)

            def invert(half):
                part = slice(half * HALF, half * HALF + HALF)
                dve.wait_ge(spread, half + 1)
                dve.reciprocal(m.rstd[:, part], m.sd[:, part]).then_inc(inverse, 1)
                dve.wait_ge(inverse, half + 1)

            def norm(i):
                if transposed is not None and i >= 2:
                    dve.wait_ge(turned, i - 1)
                out = normed(i) if gain_row is None else m.tmp[:, i % 2, :]
                if gain_row is not None and i >= 2:
                    dve.wait_ge(scaled, i - 1)
                ins = dve.tensor_scalar(out, src[:, i, :], m.mv[:, i, 0:1], m.rstd[:, i:i + 1],
                                        ALU.subtract, ALU.mult)
                if gain_row is None:
                    ins.then_inc(ready, 1)
                    return
                ins.then_inc(centred, 1)
                dve.wait_ge(centred, i + 1)
                if i == 0:
                    dve.wait_ge(loaded, 16 * len(loads))
                dve.tensor_tensor(m.tmp2[:, i % 2, :], m.tmp[:, i % 2, :], gain_row, ALU.mult).then_inc(scaled, 1)
                dve.wait_ge(scaled, i + 1)
                dve.tensor_tensor(normed(i), m.tmp2[:, i % 2, :], bias_row, ALU.add).then_inc(ready, 1)

            def keep_last(i):
                if transposed is None or gain_col is None or i < 0:
                    return
                if i == 0:
                    dve.wait_ge(loaded, 16 * len(loads))
                dve.wait_ge(turned, i + 1)
                dve.tensor_scalar(transposed[:, KB - 1, tile(i)], m.ps[:, 4 + i % 4, 0:P],
                                  gain_col[:, KB - 1:KB], bias_col[:, KB - 1:KB], ALU.mult, ALU.add).then_inc(last_kept, 1)

            for i in range(HALF):
                raw(i)
            for i in range(HALF):
                moment(i)
            raw(HALF)
            raw(HALF + 1)
            invert(0)
            for i in range(HALF):
                norm(i)
                keep_last(i - 1)
                if HALF + 2 + i < T:
                    raw(HALF + 2 + i)
                elif HALF + 2 + i == T:
                    for k in range(HALF, T):
                        moment(k)
            invert(1)
            for i in range(HALF, T):
                norm(i)
                keep_last(i - 1)
            keep_last(T - 1)

        @block.tensor
        def _(pe):
            if transposed is None:
                return
            for i in range(T):
                pe.wait_ge(ready, i + 1)
                if i >= 4:
                    pe.wait_ge(kept, i - 3)
                    if gain_col is not None:
                        pe.wait_ge(last_kept, i - 3)
                for k in range(KB):
                    out = m.ps[:, i % 4, k * P:(k + 1) * P] if gain_col is None or k < KB - 1 else m.ps[:, 4 + i % 4, 0:P]
                    ins = pe.transpose(out, cols(normed(i), k), m.ident[0:P, 0:P])
                ins.then_inc(turned, 1)

        @block.scalar
        def _(act):
            def spreads(half):
                part = slice(half * HALF, half * HALF + HALF)
                act.wait_ge(moments, HALF * (half + 1))
                act.activation(m.sd[:, part], m.mv[:, part, 1], ACT.Sqrt, bias=m.eps[0:P, 0:1]).then_inc(spread, 1)

            spreads(0)
            if transposed is None:
                spreads(1)
                return
            if gain_col is not None:
                act.wait_ge(loaded, 16 * len(loads))
            for i in range(T):
                if i == 2:
                    spreads(1)
                act.wait_ge(turned, i + 1)
                view = m.ps[:, i % 4, 0:KB * P].rearrange("p (k t) -> p k t", k=KB)
                if gain_col is None:
                    act.activation(transposed[:, :, tile(i)], view, ACT.Copy).then_inc(kept, 1)
                else:
                    for k in range(KB - 1):
                        ins = act.activation(transposed[:, k, tile(i)], view[:, k, :], ACT.Identity,
                                             bias=bias_col[:, k:k + 1], scale=gain_col[:, k:k + 1])
                    ins.then_inc(kept, 1)


def groups_phase(nc, m, n_groups, operands, evac, loads=(), slots=8, stores=None):
    with phase(nc, "loaded", "product", "taken_by_act", "taken_by_dve", "stored") as (
            block, loaded, product, taken_act, taken_dve, stored):
        taken = (taken_act, taken_dve)

        @block.sync
        def _(sp):
            for dst, src in loads:
                sp.dma_start(dst, src).then_inc(loaded, 16)
            if stores is not None:
                count = 0
                for n in range(n_groups):
                    for dst, src in stores(n):
                        sp.wait_ge(taken[n % 2], n // 2 + 1)
                        if n % 2:
                            sp.wait_ge(taken[0], n // 2 + 1)
                        sp.dma_start(dst, src).then_inc(stored, 16)
                        count += 16
                sp.wait_ge(stored, count)

        @block.tensor
        def _(pe):
            if loads:
                pe.wait_ge(loaded, 16 * len(loads))
            for n in range(n_groups):
                if n >= slots:
                    pe.wait_ge(taken[n % 2], (n - slots) // 2 + 1)
                ops = operands(n, m.ps[:, n % slots, :])
                for k, (out, lhsT, rhs) in enumerate(ops):
                    ins = pe.matmul(out, lhsT, rhs, start=k == 0, stop=k == len(ops) - 1, skip_group_check=True)
                ins.then_inc(product, 1)

        @block.scalar
        def _(act):
            if loads:
                act.wait_ge(loaded, 16 * len(loads))
            for n in range(0, n_groups, 2):
                act.wait_ge(product, n + 1)
                evac(n, act, m.ps[:, n % slots, :], True).then_inc(taken[0], 1)

        @block.vector
        def _(dve):
            if loads:
                dve.wait_ge(loaded, 16 * len(loads))
            for n in range(1, n_groups, 2):
                dve.wait_ge(product, n + 1)
                evac(n, dve, m.ps[:, n % slots, :], False).then_inc(taken[1], 1)


def copy_scaled(eng, out, in_, on_act, scale=1.0, bias=None):
    if on_act:
        if bias is None:
            return eng.activation(out, in_, ACT.Copy, scale=scale)
        return eng.activation(out, in_, ACT.Identity, bias=bias, scale=scale)
    if bias is None:
        return eng.tensor_scalar(out, in_, scale, None, ALU.mult)
    return eng.tensor_scalar(out, in_, scale, bias, ALU.mult, ALU.add)


def wview(w):
    return w.rearrange("(k p) f -> p k f", p=128)


def vector_groups_phase(nc, m, n_groups, operands, evac, loads=(), slots=8):
    with phase(nc, "loaded", "product", "taken") as (block, loaded, product, taken):
        @block.sync
        def _(sp):
            for dst, src in loads:
                sp.dma_start(dst, src).then_inc(loaded, 16)

        @block.tensor
        def _(pe):
            if loads:
                pe.wait_ge(loaded, 16 * len(loads))
            for n in range(n_groups):
                if n >= slots:
                    pe.wait_ge(taken, n - slots + 1)
                ops = operands(n, m.ps[:, n % slots, :])
                for k, (out, lhsT, rhs) in enumerate(ops):
                    ins = pe.matmul(out, lhsT, rhs, start=k == 0, stop=k == len(ops) - 1, skip_group_check=True)
                ins.then_inc(product, 1)

        @block.vector
        def _(dve):
            for n in range(n_groups):
                dve.wait_ge(product, n + 1)
                evac(n, dve, m.ps[:, n % slots, :]).then_inc(taken, 1)


def spread_row(v, parts=P):
    return v.rearrange("(a n) -> a n", a=1).to_broadcast([parts, v.shape[0]])



def edge_mlp_phase(nc, m, ef_t, w1, w2, w3, h3):
    CE, FLIGHT = 425, 5
    TURNS = E // (CE * FLIGHT)
    with ExitStack() as ctx:
        w1s = sb(nc, ctx, "mlp_w1", [128, 128])
        w2s = sb(nc, ctx, "mlp_w2", [128, 128])
        w3s = sb(nc, ctx, "mlp_w3", [128, 128])
        ef = sb(nc, ctx, "mlp_in", [128, FLIGHT, CE])
        ha = sb(nc, ctx, "mlp_h", [128, FLIGHT, 2, CE])
        ho = sb(nc, ctx, "mlp_out", [HID, FLIGHT, CE])
        names = [f"{what}_{c}" for what in ("in", "mm", "act", "out") for c in range(FLIGHT)]
        with phase(nc, "zeroed", "weights", *names) as (block, zeroed, weights, *by_chunk):
            arrived, mm, acted, stored = (by_chunk[FLIGHT * k:FLIGHT * (k + 1)] for k in range(4))

            @block.sync
            def _(sp):
                sp.wait_ge(zeroed, 5)
                for w, dram in ((w1s, w1), (w2s, w2), (w3s, w3)):
                    sp.dma_start(w[0:dram.shape[0], 0:HID], dram).then_inc(weights, 16)
                for c in range(FLIGHT):
                    sp.dma_start(ef[0:8, c, :], ef_t[:, c * CE:(c + 1) * CE]).then_inc(arrived[c], 16)
                with sp.Fori(0, TURNS - 1) as it:
                    for c in range(FLIGHT):
                        sp.wait_ge(mm[c], 3 * it + 1)
                        sp.dma_start(ef[0:8, c, :], ef_t[:, bass.ds((FLIGHT * it + FLIGHT + c) * CE, CE)]).then_inc(arrived[c], 16)

            @block.tensor
            def _(pe):
                pe.wait_ge(weights, 48)
                pe.wait_ge(zeroed, 5)
                with pe.Fori(0, TURNS) as it:
                    for layer, w in enumerate((w1s, w2s, w3s)):
                        for c in range(FLIGHT):
                            if layer == 0:
                                pe.wait_ge(arrived[c], 16 * it + 16)
                                rhs = ef[:, c, :]
                            else:
                                rhs = ha[:, c, layer - 1, :]
                            pe.wait_ge(acted[c], 3 * it + layer + 1)
                            pe.matmul(m.ps[:, c, 0:CE], w[:, :], rhs, start=True, stop=True).then_inc(mm[c], 1)

            @block.vector
            def _(dve):
                for unfilled in (w1s[:, :], w2s[:, :], w3s[:, :], ef[:, :, :], ha[HID:128, :, :, :]):
                    dve.memset(unfilled, 0.0).then_inc(zeroed, 1)
                dve.memset(m.acc[:, :, :], 0.0)
                dve.memset(m.cnt[:, :, :], 0.0)

            @block.gpsimd
            def _(pool):
                pool.iota(m.iota[:, :], pattern=[[1, N]], base=0, channel_multiplier=0, allow_small_or_imprecise_dtypes=True)

            @block.scalar
            def _(act):
                scales = (8 ** -0.5, SILU_2MOM * HID ** -0.5, SILU_2MOM * HID ** -0.5)
                for c in range(FLIGHT):
                    act.sem_inc(acted[c], 1)
                    act.sem_inc(stored[c], 16)
                with act.Fori(0, TURNS) as it:
                    for layer in range(3):
                        for c in range(FLIGHT):
                            act.wait_ge(mm[c], 3 * it + layer + 1)
                            if layer == 2:
                                act.wait_ge(stored[c], 16 * it + 16)
                            out = ho[:, c, :] if layer == 2 else ha[0:HID, c, layer, :]
                            act.activation(out, m.ps[0:HID, c, 0:CE], ACT.Silu, scale=scales[layer]).then_inc(acted[c], 1)
                    for c in range(FLIGHT):
                        act.wait_ge(acted[c], 3 * it + 4)
                        act.dma_start(h3[:, bass.ds((FLIGHT * it + c) * CE, CE)], ho[:, c, :]).then_inc(stored[c], 16)
                for c in range(FLIGHT):
                    act.wait_ge(stored[c], 16 * TURNS + 16)


def edge_base_phase(nc, m, ctx, src_l, dst_l, ea4_l):
    t = sb
    m.src_i = t(nc, ctx, "src_i", [P, SB + 1, G], I32)
    m.dst_i = t(nc, ctx, "dst_i", [P, SB, G], I32)
    m.src_f = t(nc, ctx, "src_f", [P, SB, G])
    m.dst_f = t(nc, ctx, "dst_f", [P, SB, G])
    m.dst_rel = t(nc, ctx, "dst_rel", [P, SB, G])
    m.ea4 = t(nc, ctx, "ea4", [P, SB, G, 4])
    m.base_f = t(nc, ctx, "base_f", [P, SB])
    m.base_i = t(nc, ctx, "base_i", [P, SB], I32)
    lo = t(nc, ctx, "lo", [P, SB])
    hi = t(nc, ctx, "hi", [P, SB])
    lo_all = t(nc, ctx, "lo_all", [P, SB])
    hi_all = t(nc, ctx, "hi_all", [P, SB])
    span = t(nc, ctx, "span", [P, SB])
    widest = t(nc, ctx, "widest", [P, 1])
    m.wide = t(nc, ctx, "wide", [P, 1], I32)
    with phase(nc, "loaded", "chain", "reduced") as (block, loaded, chain, reduced):
        @block.sync
        def _(sp):
            sp.dma_start(m.src_i[:, 0:SB, :], src_l).then_inc(loaded, 16)
            sp.dma_start(m.dst_i[:, :, :], dst_l).then_inc(loaded, 16)
            sp.dma_start(m.ea4[:, :, :, :], ea4_l).then_inc(loaded, 16)

        @block.gpsimd
        def _(pool):
            pool.wait_ge(chain, 5)
            pool.partition_all_reduce(lo_all[:, :], lo[:, :], P, RMAX).then_inc(reduced, 1)
            pool.partition_all_reduce(hi_all[:, :], hi[:, :], P, RMAX).then_inc(reduced, 1)

        @block.vector
        def _(dve):
            dve.memset(m.src_i[:, SB, :], 0)
            dve.wait_ge(loaded, 48)
            dve.tensor_copy(m.src_f[:, :, :], m.src_i[:, 0:SB, :]).then_inc(chain, 1)
            dve.tensor_copy(m.dst_f[:, :, :], m.dst_i[:, :, :]).then_inc(chain, 1)
            dve.wait_ge(chain, 2)
            dve.tensor_reduce(span[:, :], m.dst_f[:, :, :], AX.X, ALU.min).then_inc(chain, 1)
            dve.tensor_reduce(hi[:, :], m.dst_f[:, :, :], AX.X, ALU.max).then_inc(chain, 1)
            dve.wait_ge(chain, 4)
            dve.tensor_scalar(lo[:, :], span[:, :], -1.0, None, ALU.mult).then_inc(chain, 1)
            dve.wait_ge(reduced, 2)
            dve.tensor_scalar(m.base_f[:, :], lo_all[:, :], -1.0, None, ALU.mult).then_inc(chain, 1)
            dve.tensor_tensor(span[:, :], hi_all[:, :], lo_all[:, :], ALU.add).then_inc(chain, 1)
            dve.wait_ge(chain, 7)
            dve.tensor_copy(m.base_i[:, :], m.base_f[:, :]).then_inc(chain, 1)
            dve.tensor_reduce(widest[:, :], span[:, :], AX.X, ALU.max).then_inc(chain, 1)
            dve.wait_ge(chain, 9)
            dve.tensor_scalar(m.wide[:, :], widest[:, :], float(W), None, ALU.is_ge).then_inc(chain, 1)


def edge_sum_phase(nc, m, b, h3, xup):
    NI, U, AHEAD = SB // 2, 2 * G, 2
    done = lambda it, u: U * it + u + 1 + AHEAD
    free = lambda it, u: U * it + u - 1 + AHEAD
    gathered = m.gathered
    with phase(nc, "rel", "turn", "h_a", "h_b", "index", "even_senders", "odd_senders", "path", "window", "weighed", "prod",
               "seg", "counted", "flushed", held=gathered) as (
            block, rel, turn, h_a, h_b, index, even_senders, odd_senders, path, window, weighed, prod, seg, counted, flushed):
        h_in = (h_a, h_b)

        @block.sync
        def _(sp):
            for c in range(2):
                sp.dma_start(b.h3[0:HID, c, :], h3[:, c * 625:(c + 1) * 625]).then_inc(h_in[c], 16)
            with sp.Fori(0, NI - 1) as it:
                for c in range(2):
                    sp.wait_ge(path, U * it + G * (c + 1))
                    sp.dma_start(b.h3[0:HID, c, :], h3[:, bass.ds((2 * it + 2 + c) * 625, 625)]).then_inc(h_in[c], 16)

        @block.gpsimd
        def _(pool):
            def gather(u):
                pool.indirect_dma_start(b.rows[:, u, :], None, xup,
                                        bass.IndirectOffsetOnAxis(ap=b.idx[:, u // G, u % G:u % G + 1].bitcast(U32), axis=0)
                                        ).then_inc(gathered[u], 16)

            def senders(it, u):
                pool.wait_ge(counted, free(it, u))
                pool.sem_inc(turn, 1)
                pool.tensor_scalar(b.hot_src[:, 0, 0:N], m.iota[0:P, 0:N], b.sender[:, u // G, u % G:u % G + 1], None,
                                   ALU.is_equal).then_inc(even_senders, 1)

            flat = "p a g -> p (a g)"
            pool.sem_inc(even_senders, AHEAD)
            pool.tensor_copy(b.idx[:, 0, :], m.src_i[:, 0:1, :].rearrange(flat)).then_inc(index, 1)
            pool.wait_ge(index, 1)
            for g in range(G):
                gather(g)
            with pool.Fori(0, NI) as it:
                for c in (0, 1):
                    pool.wait_ge(even_senders, G * it + 3 * c + AHEAD)
                    pool.tensor_copy(b.sender[:, c, :], m.src_f[:, bass.ds(2 * it + c, 1), :].rearrange(flat)).then_inc(index, 1)
                    pool.wait_ge(prod, done(it, G * c - 1))
                    other, ahead = (1, 1) if c == 0 else (0, 2)
                    pool.tensor_copy(b.idx[:, other, :], m.src_i[:, bass.ds(2 * it + ahead, 1), :].rearrange(flat)).then_inc(index, 1)
                    pool.wait_ge(index, 4 * it + 2 * c + 3)
                    pool.sem_inc(turn, 1)
                    for g in range(G):
                        if (G * c + g) % 2 == 0:
                            senders(it, G * c + g)
                        gather(G * other + g)
            for g in range(U):
                pool.wait_ge(gathered[g], 16 * (NI + (1 if g < G else 0)))

        @block.tensor
        def _(pe):
            def segment(it, u):
                c, first, last = u // G, u % G == 0, u % G == G - 1
                ps = m.ps[:, 2 + c, :]
                pr, sy = b.prod[:, u % 2, :], b.sy[:, u % 2, :]

                def add(out, messages, windows, start=False):
                    return pe.matmul(out, messages, windows, start=start, stop=last, skip_group_check=True)
                if first:
                    pe.wait_ge(flushed, 2 * it + c - 1 + AHEAD)
                pe.wait_ge(weighed, done(it, u))
                pe.wait_ge(prod, done(it, u))
                add(ps[:, 0:3 * W], pr[:, 128:256], sy[:, 0:3 * W], start=first)
                add(ps[:, 3 * W:4 * W], pr[:, 0:128], sy[:, 3 * W:4 * W])
                for k in range(3):
                    add(ps[:, 4 * W:5 * W], pr[:, 640 + 128 * k:768 + 128 * k], sy[:, k * W:(k + 1) * W])
                for k in range(3):
                    ins = add(ps[:, (5 + k) * W:(6 + k) * W], pr[:, 256 + 128 * k:384 + 128 * k], sy[:, 3 * W:4 * W])
                ins.then_inc(seg, 1)
                if u % 2 == 0:
                    pe.wait_ge(even_senders, G * it + u // 2 + 1 + AHEAD)
                else:
                    pe.wait_ge(odd_senders, G * it + u // 2 + 1)
                for j in range(T):
                    ins = pe.matmul(m.ps[:, 4 + 2 * c + j // 5, (j % 5) * W:(j % 5 + 1) * W], b.hot_src[:, u % 2, j * P:j * P + 128],
                                    b.hot[:, u % 2, :], start=first and j % 5 == 0, stop=last, skip_group_check=True)
                ins.then_inc(counted, 1)

            pe.sem_inc(seg, AHEAD)
            pe.sem_inc(counted, AHEAD)
            with pe.Fori(0, NI) as it:
                for u in range(U):
                    if u % G == 0:
                        pe.wait_ge(h_in[u // G], 16 * it + 16)
                    pe.wait_ge(prod, free(it, u))
                    pe.matmul(m.ps[0:P, u % 2, :], b.h3[:, u // G, (u % G) * P:(u % G + 1) * P], b.w4[:, :], start=True,
                              stop=True).then_inc(path, 1)
                    if u >= 1:
                        segment(it, u - 1)
                segment(it, U - 1)

        @block.scalar
        def _(act):
            act.sem_inc(weighed, AHEAD)
            with act.Fori(0, NI) as it:
                for u in range(U):
                    act.wait_ge(window, U * it + u + 1)
                    act.wait_ge(seg, free(it, u))
                    for k, y in enumerate((1, 2, 3, 0)):
                        ins = act.activation(b.sy[:, u % 2, k * W:(k + 1) * W], b.hot[:, u % 2, :], ACT.Copy,
                                             scale=m.ea4[:, bass.ds(2 * it + u // G, 1), u % G, y])
                    ins.then_inc(weighed, 1)

        @block.vector
        def _(dve):
            def flush(it, c):
                base = dve.value_load(m.base_i[0:1, bass.ds(2 * it + c, 1)], min_val=0, max_val=N)
                acc = m.acc[:, :, bass.ds(base, W)]
                cnt = m.cnt[:, :, bass.ds(base, W)]
                dve.wait_ge(counted, done(it, G * c + G - 1))
                dve.wait_ge(flushed, 2 * it + c + AHEAD)
                dve.tensor_tensor(acc, m.ps[:, 2 + c, :].rearrange("p (a w) -> p a w", w=W), acc, ALU.add)
                for a in range(2):
                    view = m.ps[0:P, 4 + 2 * c + a, 0:5 * W].rearrange("p (a w) -> p a w", w=W)
                    part = cnt[:, 5 * a:5 * a + 5, :]
                    ins = dve.tensor_tensor(part, view, part, ALU.add)
                ins.then_inc(flushed, 1)

            dve.sem_inc(prod, AHEAD)
            dve.sem_inc(flushed, AHEAD)
            dve.tensor_tensor(m.dst_rel[:, :, :], m.dst_f[:, :, :],
                              m.base_f[:, :].rearrange("p (s a) -> p s a", a=1).to_broadcast([P, SB, G]),
                              ALU.subtract).then_inc(rel, 1)
            dve.wait_ge(rel, 1)
            def turn_of(it, first=False):
                for u in range(U):
                    dve.wait_ge(counted, free(it, u))
                    dve.wait_ge(weighed, free(it, u))
                    dve.tensor_scalar(b.hot[:, u % 2, :], m.iota[0:P, 0:W], m.dst_rel[:, bass.ds(2 * it + u // G, 1), u % G], None,
                                      ALU.is_equal).then_inc(window, 1)
                    dve.wait_ge(path, U * it + u + 1)
                    dve.wait_ge(gathered[u], 16 * it + 16)
                    dve.wait_ge(seg, free(it, u))
                    w, row, pr = m.ps[0:P, u % 2, :], b.rows[:, u, :], b.prod[:, u % 2, :]
                    dve.tensor_tensor(pr[:, 0:256].rearrange("p (a c) -> p a c", a=2), w[:, 0:256].rearrange("p (a c) -> p a c", a=2),
                                      row[:, 0:128].rearrange("p (a c) -> p a c", a=1).to_broadcast([P, 2, 128]), ALU.mult)
                    for a in range(2):
                        ins = dve.tensor_tensor(pr[:, 256 + 384 * a:640 + 384 * a].rearrange("p (a c) -> p a c", a=3),
                                                w[:, 256 + 128 * a:384 + 128 * a].rearrange("p (a c) -> p a c", a=1).to_broadcast([P, 3, 128]),
                                                row[:, 128:512].rearrange("p (a c) -> p a c", a=3), ALU.mult)
                    ins.then_inc(prod, 1)
                    if u % 2:
                        dve.tensor_scalar(b.hot_src[:, 1, 0:N], m.iota[0:P, 0:N], m.src_f[:, bass.ds(2 * it + u // G, 1), u % G], None,
                                          ALU.is_equal).then_inc(odd_senders, 1)
                    if u == 2 and not first:
                        flush(it - 1, 1)
                    if u == G + 2:
                        flush(it, 0)

            turn_of(0, first=True)
            with dve.Fori(0, NI - 1) as it:
                turn_of(it + 1)
            flush(NI - 1, 1)


def edges(nc, m, a, ctx):
    edge_base_phase(nc, m, ctx, a["src_l"], a["dst_l"], a["ea4_l"])
    b = Tensors()
    b.h3 = sb(nc, ctx, "edge_hidden", [128, 2, 625])
    b.w4r = sb(nc, ctx, "w4_raw", [HID, 4 * MUL])
    b.w4 = sb(nc, ctx, "w4", [128, 4 * MUL])
    b.idx = sb(nc, ctx, "edge_index", [P, 2, G], I32)
    b.sender = sb(nc, ctx, "sender", [P, 2, G])
    b.rows = sb(nc, ctx, "sender_rows", [P, 2 * G, D])
    b.hot_src = sb(nc, ctx, "hot_src", [P, 2, N + 3], BF16)
    b.hot = sb(nc, ctx, "hot_dst", [P, 2, W], BF16)
    b.sy = sb(nc, ctx, "weighed_hot", [P, 2, 4 * W])
    b.prod = sb(nc, ctx, "edge_products", [P, 2, 8 * MUL])
    with phase(nc, "loaded", "done") as (block, loaded, done):
        @block.sync
        def _(sp):
            sp.dma_start(b.w4r[:, :], a["L0_gnn_W_mlp4"]).then_inc(loaded, 16)

        @block.vector
        def _(dve):
            dve.wait_ge(loaded, 16)
            c = SILU_2MOM * HID ** -0.5
            dve.tensor_scalar(b.w4[0:HID, 0:384], b.w4r[:, 0:384], c, None, ALU.mult).then_inc(done, 1)
            dve.tensor_scalar(b.w4[0:HID, 384:512], b.w4r[:, 384:512], c * 3 ** -0.5, None, ALU.mult).then_inc(done, 1)
            dve.memset(b.w4[HID:128, :], 0.0).then_inc(done, 1)
            dve.memset(b.h3[HID:128, :, :], 0.0).then_inc(done, 1)
            dve.memset(b.hot_src[:, :, N:N + 3], 0.0).then_inc(done, 1)
    wide = nc.values_load(m.wide[0:1, 0:1], min_val=0, max_val=1)
    with nc.If(wide == 0):
        edge_sum_phase(nc, m, b, a["h3"], a["xup"])
    with nc.Else():
        with phase(nc, "done") as (block, done):
            @block.vector
            def _(dve):
                dve.memset(m.base_f[:, :], 0.0).then_inc(done, 1)
                dve.memset(m.base_i[:, :], 0).then_inc(done, 1)
        with nc.Fori(0, -(-N // W)) as _w:
            edge_sum_phase(nc, m, b, a["h3"], a["xup"])
            with phase(nc, "moved") as (block, moved):
                @block.vector
                def _(dve):
                    dve.tensor_scalar(b.sy[0:P, 0, 0:SB], m.base_f[:, :], float(W), None, ALU.add).then_inc(moved, 1)
                    dve.wait_ge(moved, 1)
                    dve.tensor_copy(m.base_f[:, :], b.sy[0:P, 0, 0:SB]).then_inc(moved, 1)
                    dve.tensor_copy(m.base_i[:, :], b.sy[0:P, 0, 0:SB]).then_inc(moved, 1)



def l0_mix(nc, m, a):
    R = 4
    with ExitStack() as ctx:
        w_in = sb(nc, ctx, "mix_w_in", [128, KB, D])
        b_in = sb(nc, ctx, "mix_b_in", [128, KB])
        xm = sb(nc, ctx, "mix_mid", [128, KB, N])
        bd = sb(nc, ctx, "mix_heads", [128, 144])
        qk = sb(nc, ctx, "mix_qk", [P, 2, T, 32])
        v = sb(nc, ctx, "mix_v", [P, T, D])
        w_out = sb(nc, ctx, "mix_w_out", [128, KB, D])
        b_out = sb(nc, ctx, "mix_b_out", [P, D])

        with phase(nc, "zeroed", "loaded") as (block, zeroed, loaded):
            @block.vector
            def _(dve):
                dve.memset(bd[:, :], 0.0).then_inc(zeroed, 1)

            @block.sync
            def _(sp):
                sp.wait_ge(zeroed, 1)
                for h in range(2):
                    rows = slice(64 * h, 64 * h + 64)
                    sp.dma_start(bd[rows, R * h:R * h + R], a["L0_mix_W_q"]).then_inc(loaded, 16)
                    sp.dma_start(bd[rows, 8 + R * h:8 + R * h + R], a["L0_mix_W_k"]).then_inc(loaded, 16)
                    sp.dma_start(bd[rows, 16 + 64 * h:80 + 64 * h], a["L0_mix_W_v"]).then_inc(loaded, 16)
                sp.wait_ge(loaded, 96)

        def mid_products(n, bank):
            f, (c0, cn) = n // 3, CH[n % 3]
            return [(bank[:, 0:cn], w_in[:, k, f * 128:(f + 1) * 128], m.xt[:, k, c0:c0 + cn]) for k in range(KB)]

        def mid_take(n, eng, bank, on_act):
            f, (c0, cn) = n // 3, CH[n % 3]
            return copy_scaled(eng, xm[:, f, c0:c0 + cn], bank[:, 0:cn], on_act, bias=b_in[:, f:f + 1])

        groups_phase(nc, m, 12, mid_products, mid_take,
                     loads=[(w_in[:, :, :], wview(a["L0_mix_W_in"])), (b_in[:, :], a["L0_mix_b_in"])])

        def head_products(n, bank):
            i, half = n // 2, n % 2
            return [(bank[0:P, 144 * k:144 * k + 144], xm[:, 2 * half + k, tile(i)], bd[:, :]) for k in range(2)]

        def head_take(n, eng, bank, on_act):
            i, half = n // 2, n % 2
            two = bank[0:P, 0:288].rearrange("p (k c) -> p k c", k=2)
            for j in range(2):
                out = qk[:, j, i, 16 * half:16 * half + 16].rearrange("p (k c) -> p k c", k=2)
                copy_scaled(eng, out, two[:, :, 8 * j:8 * j + 8], on_act)
            out = v[:, i, 256 * half:256 * half + 256].rearrange("p (k c) -> p k c", k=2)
            return copy_scaled(eng, out, two[:, :, 16:144], on_act)

        groups_phase(nc, m, 2 * T, head_products, head_take,
                     loads=[(w_out[:, :, :], wview(a["L0_mix_W_out"])), (b_out[:, :], spread_row(a["L0_mix_b_out"]))])

        qmax = sb(nc, ctx, "mix_qmax", [P, T, HEADS])
        qsum = sb(nc, ctx, "mix_qsum", [P, T, HEADS])
        qinv = sb(nc, ctx, "mix_qinv", [P, T, HEADS])
        kmax = sb(nc, ctx, "mix_kmax", [P, 32])
        kmax_all = sb(nc, ctx, "mix_kmax_all", [P, 32])
        sh = sb(nc, ctx, "mix_shifted", [P, 2, T, 32])
        ex = sb(nc, ctx, "mix_exp", [P, 2, T, 32])
        qs = sb(nc, ctx, "mix_q_soft", [P, T, 32])
        qt = sb(nc, ctx, "mix_qt", [32, N])
        mask = sb(nc, ctx, "mix_mask", [32, HEADS, DH])
        dinv = sb(nc, ctx, "mix_dinv", [32, 1])
        kv = sb(nc, ctx, "mix_kv", [32, D])
        kvt = sb(nc, ctx, "mix_kvt", [128, KB, 32])
        kvw = sb(nc, ctx, "mix_kvw", [32, D])
        with phase(nc, "masked", "v_step", "a_step", "p_step", "t_step") as (block, masked, v_step, a_step, p_step, t_step):
            @block.gpsimd
            def _(pool):
                pool.memset(mask[:, :, :], 1.0).then_inc(masked, 1)
                pool.wait_ge(masked, 1)
                pool.affine_select(out=mask[:, :, :], in_=mask[:, :, :], compare_op=ALU.is_ge, fill=0.0, base=0,
                                   pattern=[[-R, HEADS], [0, DH]], channel_multiplier=1).then_inc(masked, 1)
                pool.wait_ge(masked, 2)
                pool.affine_select(out=mask[:, :, :], in_=mask[:, :, :], compare_op=ALU.is_ge, fill=0.0, base=R - 1,
                                   pattern=[[R, HEADS], [0, DH]], channel_multiplier=-1).then_inc(masked, 1)
                pool.wait_ge(v_step, 1)
                pool.partition_all_reduce(kmax_all[:, :], kmax[:, :], P, RMAX).then_inc(p_step, 1)

            @block.vector
            def _(dve):
                heads = lambda ap: ap.rearrange("p t (h r) -> p t h r", r=R)
                wide = lambda ap: ap.rearrange("p t (h a) -> p t h a", a=1).to_broadcast([P, T, HEADS, R])
                dve.tensor_reduce(kmax[:, :], qk[:, 1, :, :].rearrange("p t c -> p c t"), AX.X, ALU.max).then_inc(v_step, 1)
                dve.tensor_reduce(qmax[:, :, :], heads(qk[:, 0, :, :]), AX.X, ALU.max).then_inc(v_step, 1)
                dve.wait_ge(v_step, 2)
                dve.tensor_tensor(heads(sh[:, 0, :, :]), heads(qk[:, 0, :, :]), wide(qmax[:, :, :]), ALU.subtract).then_inc(v_step, 1)
                dve.wait_ge(p_step, 1)
                dve.tensor_tensor(sh[:, 1, :, :], qk[:, 1, :, :],
                                  kmax_all[:, :].rearrange("p (a c) -> p a c", a=1).to_broadcast([P, T, 32]), ALU.subtract).then_inc(v_step, 1)
                dve.wait_ge(a_step, 1)
                dve.tensor_reduce(qsum[:, :, :], heads(ex[:, 0, :, :]), AX.X, ALU.add).then_inc(v_step, 1)
                dve.wait_ge(v_step, 5)
                dve.reciprocal(qinv[:, :, :], qsum[:, :, :]).then_inc(v_step, 1)
                dve.wait_ge(v_step, 6)
                dve.tensor_tensor(heads(qs[:, :, :]), heads(ex[:, 0, :, :]), wide(qinv[:, :, :]), ALU.mult).then_inc(v_step, 1)
                dve.wait_ge(t_step, 1)
                dve.reciprocal(dinv[:, :], m.ps[0:32, 1, 0:1]).then_inc(v_step, 1)
                dve.wait_ge(v_step, 8)
                dve.wait_ge(masked, 3)
                dve.scalar_tensor_tensor(kv[:, :], m.ps[0:32, 0, :], dinv[:, 0:1], mask[:, :, :].rearrange("p h c -> p (h c)"),
                                         ALU.mult, ALU.mult).then_inc(v_step, 1)
                dve.wait_ge(t_step, 3)
                dve.tensor_copy(kvt[:, :, :], m.ps[:, 5, 0:128].rearrange("p (k c) -> p k c", k=KB)).then_inc(v_step, 1)
                dve.wait_ge(t_step, 4)
                dve.tensor_copy(kvw[:, :], m.ps[0:32, 6, :]).then_inc(v_step, 1)

            @block.scalar
            def _(act):
                act.wait_ge(v_step, 4)
                act.activation(ex[:, :, :, :], sh[:, :, :, :], ACT.Exp).then_inc(a_step, 1)
                act.wait_ge(t_step, 2)
                for c0, cn in CH:
                    ins = act.activation(qt[:, c0:c0 + cn], m.ps[0:32, 2 + c0 // 500, 0:cn], ACT.Copy)
                ins.then_inc(a_step, 1)

            @block.tensor
            def _(pe):
                pe.wait_ge(a_step, 1)
                for i in range(T):
                    pe.matmul(m.ps[0:32, 0, :], ex[:, 1, i, :], v[:, i, :], start=i == 0, stop=i == T - 1)
                for i in range(T):
                    ins = pe.matmul(m.ps[0:32, 1, 0:1], ex[:, 1, i, :], m.ones[0:P, 0:1], start=i == 0, stop=i == T - 1)
                ins.then_inc(t_step, 1)
                pe.wait_ge(v_step, 7)
                for i in range(T):
                    ins = pe.transpose(m.ps[0:32, 2 + i // 4, (i % 4) * P:(i % 4 + 1) * P], qs[:, i, :], m.ident[0:P, 0:P])
                ins.then_inc(t_step, 1)
                pe.wait_ge(v_step, 9)
                for k in range(KB):
                    ins = pe.transpose(m.ps[:, 5, k * 32:(k + 1) * 32], kv[:, k * 128:(k + 1) * 128], m.ident[0:32, 0:32])
                ins.then_inc(t_step, 1)
                pe.wait_ge(v_step, 10)
                for k in range(KB):
                    ins = pe.matmul(m.ps[0:32, 6, :], kvt[:, k, :], w_out[:, k, :], start=k == 0, stop=k == KB - 1)
                ins.then_inc(t_step, 1)

        def out_products(n, bank):
            return [(bank[0:P, :], qt[:, tile(n)], kvw[:, :])]

        def out_take(n, dve, bank):
            return dve.tensor_tensor(m.x[:, n, :], bank[0:P, :], m.x[:, n, :], ALU.add)

        vector_groups_phase(nc, m, T, out_products, out_take)
        add_rows(nc, m, b_out)


def add_rows(nc, m, row):
    with phase(nc, "added") as (block, added):
        @block.vector
        def _(dve):
            for i in range(T):
                dve.tensor_tensor(m.x[:, i, :], m.x[:, i, :], row[:, :], ALU.add).then_inc(added, 1)



def l0_ffn(nc, m, a):
    NE = 8
    KEEP = N // NE
    with ExitStack() as ctx:
        layernorm_phase(nc, m, m.x, lambda i: m.tmp[:, i % 2, :], m.xt)
        gw = sb(nc, ctx, "gate_w", [128, KB, NE])
        g0 = sb(nc, ctx, "gates", [P, T, NE])
        t = sb(nc, ctx, "sink_t", [P, T, NE])
        cg = sb(nc, ctx, "sink_weights", [P, T, NE])
        coef = sb(nc, ctx, "combine", [P, T, NE])

        def gate_products(n, bank):
            return [(bank[0:P, 0:NE], m.xt[:, k, tile(n)], gw[:, k, :]) for k in range(KB)]

        def gate_take(n, dve, bank):
            return dve.tensor_scalar(g0[:, n, :], bank[0:P, 0:NE], 1e-10, None, ALU.max)

        vector_groups_phase(nc, m, T, gate_products, gate_take, loads=[(gw[:, :, :], wview(a["L0_ffn_gate_w"][0]))])
        with phase(nc, "logged") as (block, logged):
            @block.scalar
            def _(act):
                act.activation(t[:, :, :], g0[:, :, :], ACT.Ln).then_inc(logged, 1)

        mt = sb(nc, ctx, "sink_max", [P, NE])
        mall = sb(nc, ctx, "sink_max_all", [P, NE])
        d1 = sb(nc, ctx, "sink_d1", [P, T, NE])
        e1 = sb(nc, ctx, "sink_e1", [P, T, NE])
        s1 = sb(nc, ctx, "sink_s1", [P, NE])
        l1 = sb(nc, ctx, "sink_l1", [P, NE])
        d2 = sb(nc, ctx, "sink_d2", [P, T, NE])
        m2 = sb(nc, ctx, "sink_m2", [P, T])
        d3 = sb(nc, ctx, "sink_d3", [P, T, NE])
        e2 = sb(nc, ctx, "sink_e2", [P, T, NE])
        s2 = sb(nc, ctx, "sink_s2", [P, T])
        l2 = sb(nc, ctx, "sink_l2", [P, T])
        by_expert = lambda ap: ap.rearrange("p (a e) -> p a e", a=1).to_broadcast([P, T, NE])
        by_token = lambda ap: ap.rearrange("p (t a) -> p t a", a=1).to_broadcast([P, T, NE])
        with nc.Fori(0, 8):
            with phase(nc, "v_step", "a_step", "p_step", "t_step") as (block, v_step, a_step, p_step, t_step):
                @block.vector
                def _(dve):
                    dve.tensor_reduce(mt[:, :], t[:, :, :].rearrange("p t e -> p e t"), AX.X, ALU.max).then_inc(v_step, 1)
                    dve.wait_ge(p_step, 1)
                    dve.tensor_tensor(d1[:, :, :], t[:, :, :], by_expert(mall[:, :]), ALU.subtract).then_inc(v_step, 1)
                    dve.wait_ge(a_step, 1)
                    dve.tensor_reduce(s1[:, :], e1[:, :, :].rearrange("p t e -> p e t"), AX.X, ALU.add).then_inc(v_step, 1)
                    dve.wait_ge(a_step, 2)
                    dve.tensor_tensor(d2[:, :, :], d1[:, :, :], by_expert(l1[:, :]), ALU.subtract).then_inc(v_step, 1)
                    dve.wait_ge(v_step, 4)
                    dve.tensor_reduce(m2[:, :], d2[:, :, :], AX.X, ALU.max).then_inc(v_step, 1)
                    dve.wait_ge(v_step, 5)
                    dve.tensor_tensor(d3[:, :, :], d2[:, :, :], by_token(m2[:, :]), ALU.subtract).then_inc(v_step, 1)
                    dve.wait_ge(a_step, 3)
                    dve.tensor_reduce(s2[:, :], e2[:, :, :], AX.X, ALU.add).then_inc(v_step, 1)
                    dve.wait_ge(a_step, 4)
                    dve.tensor_tensor(t[:, :, :], d3[:, :, :], by_token(l2[:, :]), ALU.subtract).then_inc(v_step, 1)

                @block.gpsimd
                def _(pool):
                    pool.wait_ge(v_step, 1)
                    pool.partition_all_reduce(mall[:, :], mt[:, :], P, RMAX).then_inc(p_step, 1)

                @block.tensor
                def _(pe):
                    pe.wait_ge(v_step, 3)
                    pe.matmul(m.ps[0:P, 0, 0:NE], m.ones[0:P, 0:P], s1[:, :], start=True, stop=True).then_inc(t_step, 1)

                @block.scalar
                def _(act):
                    act.wait_ge(v_step, 2)
                    act.activation(e1[:, :, :], d1[:, :, :], ACT.Exp).then_inc(a_step, 1)
                    act.wait_ge(t_step, 1)
                    act.activation(l1[:, :], m.ps[0:P, 0, 0:NE], ACT.Ln).then_inc(a_step, 1)
                    act.wait_ge(v_step, 6)
                    act.activation(e2[:, :, :], d3[:, :, :], ACT.Exp).then_inc(a_step, 1)
                    act.wait_ge(v_step, 7)
                    act.activation(l2[:, :], s2[:, :], ACT.Ln).then_inc(a_step, 1)

        cgt = sb(nc, ctx, "weights_by_expert", [NE, 2, N + 8])
        best = sb(nc, ctx, "best", [NE, 2, 8])
        chosen_t = sb(nc, ctx, "chosen_by_expert", [NE, N])
        chosen = sb(nc, ctx, "chosen", [P, T, NE])
        count = sb(nc, ctx, "chosen_by", [P, T])
        inv = sb(nc, ctx, "share", [P, T])
        half = sb(nc, ctx, "over_half", [P, T, NE])
        ROUNDS = -(-KEEP // 8)
        REST = KEEP - 8 * (ROUNDS - 1)
        TAKEN, PAD = -2.0, -1.0
        with phase(nc, "v_step", "a_step", "t_step", "found", "struck") as (block, v_step, a_step, t_step, found, struck):
            @block.scalar
            def _(act):
                act.activation(cg[:, :, :], t[:, :, :], ACT.Exp).then_inc(a_step, 1)
                act.wait_ge(t_step, 1)
                for c0, cn in CH:
                    ins = act.activation(cgt[:, 0, c0:c0 + cn], m.ps[0:NE, c0 // 500, 0:cn], ACT.Copy)
                ins.then_inc(a_step, 1)

            @block.tensor
            def _(pe):
                pe.wait_ge(a_step, 1)
                for i in range(T):
                    ins = pe.transpose(m.ps[0:NE, i // 4, (i % 4) * P:(i % 4 + 1) * P], cg[:, i, :], m.ident[0:P, 0:P])
                ins.then_inc(t_step, 1)
                pe.wait_ge(v_step, 3)
                for i in range(T):
                    ins = pe.transpose(m.ps[0:P, 4, i * NE:(i + 1) * NE], chosen_t[:, tile(i)], m.ident[0:NE, 0:NE])
                ins.then_inc(t_step, 1)

            @block.vector
            def _(dve):
                dve.memset(cgt[:, :, N:N + 8], PAD).then_inc(v_step, 1)
                dve.memset(best[:, 1, :], PAD).then_inc(v_step, 1)
                dve.wait_ge(v_step, 2)
                dve.wait_ge(a_step, 2)
                for r in range(ROUNDS):
                    last = r == ROUNDS - 1
                    if r:
                        dve.wait_ge(struck, r)
                    dve.max(best[:, 0, :], cgt[:, r % 2, :]).then_inc(found, 1)
                    dve.wait_ge(found, r + 1)
                    if last:
                        dve.tensor_copy(best[:, 1, 0:REST], best[:, 0, 0:REST]).then_inc(found, 1)
                        dve.wait_ge(found, r + 2)
                    dve.match_replace(cgt[:, (r + 1) % 2, :], best[:, int(last), :], cgt[:, r % 2, :], TAKEN).then_inc(struck, 1)
                dve.wait_ge(struck, ROUNDS)
                dve.tensor_scalar(chosen_t[:, :], cgt[:, ROUNDS % 2, 0:N], (TAKEN + PAD) / 2, None, ALU.is_le).then_inc(v_step, 1)
                dve.wait_ge(t_step, 2)
                dve.tensor_copy(chosen[:, :, :], m.ps[0:P, 4, 0:T * NE].rearrange("p (t e) -> p t e", e=NE)).then_inc(v_step, 1)
                dve.tensor_scalar(half[:, :, :], cg[:, :, :], 0.5, None, ALU.is_gt).then_inc(v_step, 1)
                dve.wait_ge(v_step, 5)
                dve.tensor_reduce(count[:, :], chosen[:, :, :], AX.X, ALU.add).then_inc(v_step, 1)
                dve.tensor_tensor(half[:, :, :], half[:, :, :], chosen[:, :, :], ALU.mult).then_inc(v_step, 1)
                dve.wait_ge(v_step, 7)
                dve.tensor_scalar(s2[:, :], count[:, :], 1.0, None, ALU.add).then_inc(v_step, 1)
                dve.wait_ge(v_step, 8)
                dve.reciprocal(inv[:, :], s2[:, :]).then_inc(v_step, 1)
                dve.wait_ge(v_step, 9)
                dve.tensor_tensor(coef[:, :, :], half[:, :, :], by_token(inv[:, :]), ALU.mult).then_inc(v_step, 1)

        HALF = D // 2
        xh = sb(nc, ctx, "expert_x_high", [128, KB, N], F32R)
        xl = sb(nc, ctx, "expert_x_low", [128, KB, N], F32R)
        raw = sb(nc, ctx, "expert_w", [128, 2, KB, HALF])
        wh = sb(nc, ctx, "expert_w_high", [128, 2, KB, HALF], F32R)
        wl = sb(nc, ctx, "expert_w_low", [128, 2, KB, HALF], F32R)
        SLOTS, AHEAD = 5, 2 * T
        with phase(nc, "w_a", "w_b", "w_rounded", "w_ready", "x_rounded", "x_ready", "product", "taken") as (
                block, w_a, w_b, w_rounded, w_ready, x_rounded, x_ready, product, taken):
            arrived = (w_a, w_b)
            experts = a["L0_ffn_experts"].rearrange("e (k p) f -> e p k f", p=128)

            @block.sync
            def _(sp):
                for c in range(2):
                    sp.dma_start(raw[:, c, :, :], experts[0][:, :, c * HALF:(c + 1) * HALF]).then_inc(arrived[c], 16)
                with sp.Fori(0, NE - 1) as it:
                    for c in range(2):
                        sp.wait_ge(w_ready, 2 * it + c + 1)
                        sp.dma_start(raw[:, c, :, :], experts[bass.ds(it + 1, 1)].rearrange("a p k f -> (a p) k f")[:, :, c * HALF:(c + 1) * HALF]
                                     ).then_inc(arrived[c], 16)

            @block.gpsimd
            def _(pool):
                with pool.Fori(0, NE) as it:
                    for c in range(2):
                        pool.wait_ge(w_rounded, 2 * it + c + 1)
                        pool.tensor_tensor(wl[:, c, :, :], raw[:, c, :, :], wh[:, c, :, :].bitcast(F32), ALU.subtract).then_inc(w_ready, 1)

            @block.tensor
            def _(pe):
                pe.sem_inc(product, AHEAD)
                with pe.Fori(0, NE) as it:
                    for c in range(2):
                        pe.wait_ge(w_ready, 2 * it + c + 1)
                        for i in range(T):
                            n = T * c + i
                            pe.wait_ge(x_ready, i // 4 + 1)
                            pe.wait_ge(taken, 2 * T * it + n + 1 - SLOTS + AHEAD)
                            for k in range(KB):
                                for q, (x, w) in enumerate(((xh, wh), (xl, wh), (xh, wl))):
                                    ins = pe.matmul(m.ps[0:P, n % SLOTS, 0:HALF], x[:, k, tile(i)], w[:, c, k, :],
                                                    start=k == 0 and q == 0, stop=k == KB - 1 and q == 2)
                            ins.then_inc(product, 1)

            @block.scalar
            def _(act):
                for c0, cn in CH:
                    act.activation(xh[:, :, c0:c0 + cn], m.xt[:, :, c0:c0 + cn], ACT.Copy).then_inc(x_rounded, 1)
                with act.Fori(0, NE) as it:
                    for c in range(2):
                        act.wait_ge(arrived[c], 16 * it + 16)
                        act.wait_ge(product, 2 * T * it + T * (c - 1) + AHEAD)
                        act.activation(wh[:, c, :, :], raw[:, c, :, :], ACT.Copy).then_inc(w_rounded, 1)

            @block.vector
            def _(dve):
                dve.sem_inc(taken, AHEAD)
                for c, (c0, cn) in enumerate(CH):
                    dve.wait_ge(x_rounded, c + 1)
                    dve.tensor_tensor(xl[:, :, c0:c0 + cn], m.xt[:, :, c0:c0 + cn], xh[:, :, c0:c0 + cn].bitcast(F32), ALU.subtract).then_inc(x_ready, 1)
                with dve.Fori(0, NE) as it:
                    for c in range(2):
                        for i in range(T):
                            n = T * c + i
                            dve.wait_ge(product, 2 * T * it + n + 1 + AHEAD)
                            dve.wait_ge(taken, 2 * T * it + n + 1 - 2 * T + AHEAD)
                            part = m.x[:, i, c * HALF:(c + 1) * HALF]
                            dve.scalar_tensor_tensor(part, m.ps[0:P, n % SLOTS, 0:HALF], coef[:, i, bass.ds(it, 1)], part,
                                                     ALU.mult, ALU.add).then_inc(taken, 1)



def attention(nc, m, tag, qt, kt, v, ot, slots, mask=None, cnt=None):
    own = lambda h: slice(64 * (h % 2), 64 * (h % 2) + 64)
    other = lambda h: own(h + 1)
    C = len(CH)
    UNITS, STEPS, PIECES = HEADS * C, C * T, T * C
    FIRST, LAST = (0 if slots == 3 else 8), 26
    COLS = slots - 1
    ahead = slots - 1
    make = {2: (0, 0, 1, 1, 6), 3: (2, 6, 10, 14, 24)}[slots]

    def pieces_at(n):
        h, s = n // STEPS, n % STEPS
        if h + 1 >= HEADS or not FIRST <= s < LAST:
            return range(0)
        upto = lambda s: PIECES * (s - FIRST) // (LAST - FIRST)
        return range(PIECES * (h + 1) + upto(s), PIECES * (h + 1) + upto(s + 1))

    with ExitStack() as ctx:
        part = sb(nc, ctx, tag + "row_max_parts", [P, HEADS * T, C])
        rmax = sb(nc, ctx, tag + "row_max", [P, HEADS * T])
        ks = sb(nc, ctx, tag + "k_split", [128, slots, N], F32R)
        qs = sb(nc, ctx, tag + "q_split", [128, slots, 2, N], F32R)
        mb = sb(nc, ctx, tag + "max_by_column", [P, COLS, 512])
        z = m.tmp4
        RING, SCORES = 4, 3
        LAG = 3
        SUMS, SPREAD, PIECE = 3, 5, 6
        with phase(nc, "k_rounded", "k_ready", "first_q", "q_rounded", "q_rest", "q_ready", "piece", "maxed", "row", "spread", "kept",
                   "scores", "shift", "clip", "expd", "counted", "summed", "inverted", "normed") as (
                block, k_rounded, k_ready, first_q, q_rounded, q_rest, q_ready, piece, maxed, row, spread, kept,
                scores, shift, clip, expd, counted, summed, inverted, normed):
            weighed = expd if mask is None else counted
            spread_step = lambda u: 8 if (u + 1) % C == 0 else 5
            keep_step = lambda u: T - 1 if COLS == 1 else spread_step(u) + 1

            @block.tensor
            def _(pe):
                def try_piece(p):
                    h, i, (c0, cn) = p // PIECES, p % PIECES // C, CH[p % C]
                    if p % PIECES == 0:
                        if h == 0:
                            pe.wait_ge(first_q, 3)
                        else:
                            pe.wait_ge(q_ready, h)
                        pe.wait_ge(k_ready, h + 1)
                    if p >= 2:
                        pe.wait_ge(maxed, p - 1)
                    for r in range(2):
                        ins = pe.matmul(m.ps[0:P, PIECE + p % 2, 0:cn], qs[:, h % slots, r, tile(i)], ks[:, h % slots, c0:c0 + cn],
                                        start=r == 0, stop=r == 1)
                    ins.then_inc(piece, 1)

                def maxima(u):
                    h, (c0, cn) = u // C, CH[u % C]
                    pe.wait_ge(row, h + 1)
                    if u:
                        pe.wait_ge(kept, u)
                    for i in range(cn // P):
                        col = h * T + c0 // P + i
                        ins = pe.transpose(m.ps[0:P, SPREAD, i * P:(i + 1) * P], rmax[:, col:col + 1].to_broadcast([P, P]),
                                           m.ident[0:P, 0:P])
                    ins.then_inc(spread, 1)

                def sums(n):
                    u, j = n // T, n % T
                    h, (c0, cn) = u // C, CH[u % C]
                    if j == 0 and u >= 2:
                        pe.wait_ge(normed, u - 1)
                    pe.wait_ge(weighed, n + 1)
                    w0 = 64 * (h % 2)
                    pe.matmul(m.ps[:, SUMS + u % 2, 0:cn], v[:, j, h // 2, w0:w0 + 128], z[:, n % RING, 0:cn],
                              start=j == 0, stop=j == T - 1).then_inc(summed, 1)

                for p in range(PIECES):
                    try_piece(p)
                maxima(0)
                for n in range(UNITS * T + LAG):
                    if n < UNITS * T:
                        u, j = n // T, n % T
                        h, (c0, cn) = u // C, CH[u % C]
                        if n >= SCORES:
                            pe.wait_ge(shift, n - SCORES + 1)
                        for r in range(2):
                            ins = pe.matmul(m.ps[0:P, n % SCORES, 0:cn], ks[:, h % slots, tile(j)], qs[:, h % slots, r, c0:c0 + cn],
                                            start=r == 0, stop=r == 1)
                        ins.then_inc(scores, 1)
                        for p in pieces_at(n):
                            try_piece(p)
                        if j == spread_step(u) and u + 1 < UNITS:
                            maxima(u + 1)
                    if n >= LAG:
                        sums(n - LAG)

            @block.gpsimd
            def _(pool):
                for h in range(HEADS):
                    s = h % slots
                    pool.wait_ge(k_rounded, h + 1)
                    pool.tensor_tensor(ks[own(h), s, :], kt[own(h), h // 2, :], ks[own(h), s, :].bitcast(F32), ALU.subtract).then_inc(k_ready, 1)
                    if h == 0:
                        continue
                    pool.wait_ge(q_rounded, h)
                    pool.tensor_tensor(qs[own(h), s, 1, :], qt[own(h), h // 2, :], qs[own(h), s, 0, :].bitcast(F32), ALU.subtract).then_inc(q_rest, 1)

            @block.vector
            def _(dve):
                def reduce_piece(p):
                    i, (c0, cn) = p % PIECES // C, CH[p % C]
                    dve.wait_ge(piece, p + 1)
                    scored, best = m.ps[0:P, PIECE + p % 2, 0:cn], part[:, p // C, p % C:p % C + 1]
                    if mask is None:
                        dve.tensor_reduce(best, scored, AX.X, ALU.max).then_inc(maxed, 1)
                    else:
                        dve.tensor_tensor_reduce(scored, scored, mask[:, i, c0:c0 + cn], 1.0, -BIG, ALU.add, ALU.max, best).then_inc(maxed, 1)

                def reduce_rows(h):
                    dve.wait_ge(maxed, PIECES * (h + 1))
                    dve.tensor_reduce(rmax[:, h * T:(h + 1) * T], part[:, h * T:(h + 1) * T, :], AX.X, ALU.max).then_inc(row, 1)

                def norm(u):
                    h, (c0, cn) = u // C, CH[u % C]
                    num, den = own(h), other(h)
                    out = ot[num, h // 2, c0:c0 + cn]
                    dve.wait_ge(summed, T * (u + 1))
                    dve.reciprocal(out, m.ps[den, SUMS + u % 2, 0:cn]).then_inc(inverted, 1)
                    dve.wait_ge(inverted, u + 1)
                    dve.tensor_tensor(out, m.ps[num, SUMS + u % 2, 0:cn], out, ALU.mult).then_inc(normed, 1)

                def count(n):
                    u, j = n // T, n % T
                    c0, cn = CH[u % C]
                    dve.wait_ge(expd, n + 1)
                    dve.tensor_tensor(z[:, n % RING, 0:cn], z[:, n % RING, 0:cn], cnt[:, j, c0:c0 + cn], ALU.mult).then_inc(counted, 1)

                q0 = qt[own(0), 0, :]
                dve.tensor_copy(qs[own(0), 0, 0, :], q0).then_inc(first_q, 1)
                dve.tensor_copy(qs[other(0), 0, 0, :], q0)
                dve.wait_ge(first_q, 1)
                dve.tensor_tensor(qs[own(0), 0, 1, :], q0, qs[own(0), 0, 0, :].bitcast(F32), ALU.subtract).then_inc(first_q, 1)
                dve.wait_ge(first_q, 2)
                dve.tensor_copy(qs[other(0), 0, 1, :], qs[own(0), 0, 1, :].bitcast(F32)).then_inc(first_q, 1)
                for p in range(PIECES):
                    reduce_piece(p)
                reduce_rows(0)
                for n in range(UNITS * T):
                    u, j = n // T, n % T
                    c0, cn = CH[u % C]
                    if j == 0:
                        dve.wait_ge(kept, u + 1)
                    if n >= RING:
                        dve.wait_ge(summed, n - RING + 1)
                    dve.wait_ge(scores, n + 1)
                    dve.tensor_tensor(z[:, n % RING, 0:cn], m.ps[0:P, n % SCORES, 0:cn], mb[:, u % COLS, 0:cn], ALU.subtract).then_inc(shift, 1)
                    if mask is not None and n >= 1:
                        count(n - 1)
                    for p in pieces_at(n):
                        reduce_piece(p)
                    if n % STEPS == LAST and u // C + 1 < HEADS:
                        reduce_rows(u // C + 1)
                    if j == 4 and u >= 1:
                        norm(u - 1)
                if mask is not None:
                    count(UNITS * T - 1)
                norm(UNITS - 1)

            @block.scalar
            def _(act):
                def part_of(h, k):
                    s = h % slots
                    if k < 2:
                        half = (own, other)[k](h)
                        ins = act.activation(ks[half, s, :], kt[own(h), h // 2, :], ACT.Copy)
                        if k == 1:
                            ins.then_inc(k_rounded, 1)
                    elif k < 4:
                        half = (own, other)[k - 2](h)
                        ins = act.activation(qs[half, s, 0, :], qt[own(h), h // 2, :], ACT.Copy)
                        if k == 3:
                            ins.then_inc(q_rounded, 1)
                    else:
                        act.wait_ge(q_rest, h)
                        act.activation(qs[other(h), s, 1, :], qs[own(h), s, 1, :].bitcast(F32), ACT.Copy).then_inc(q_ready, 1)

                def keep(u):
                    c0, cn = CH[u % C]
                    act.wait_ge(spread, u + 1)
                    if u >= COLS:
                        act.wait_ge(shift, T * (u + 1 - COLS))
                    act.activation(mb[:, u % COLS, 0:cn], m.ps[0:P, SPREAD, 0:cn], ACT.Copy).then_inc(kept, 1)

                for h in range(ahead):
                    for k in range(5 if h else 2):
                        part_of(h, k)
                keep(0)
                for n in range(UNITS * T):
                    u, j = n // T, n % T
                    cn = CH[u % C][1]
                    slot = z[:, n % RING, 0:cn]
                    act.wait_ge(shift, n + 1)
                    if mask is None:
                        act.activation(slot, slot, ACT.Exp, scale=DH ** -0.5).then_inc(expd, 1)
                    else:
                        act.activation(slot, slot, ACT.Relu, scale=-(DH ** -0.5)).then_inc(clip, 1)
                        act.wait_ge(clip, n + 1)
                        act.activation(slot, slot, ACT.Exp, scale=-1.0).then_inc(expd, 1)
                    if u + 1 < UNITS and j == keep_step(u):
                        keep(u + 1)
                    for k, at in enumerate(make):
                        if at == n % STEPS and u // C + ahead < HEADS:
                            part_of(u // C + ahead, k)


def split_gemm_phase(nc, m, tag, sources, width, groups, take, takers="both", aside=None, loads=()):
    J = len(sources)
    flat = [(j, g) for j in range(J) for g in groups[j]]
    upto = [sum(len(groups[i]) for i in range(j + 1)) for j in range(J)]
    taker = lambda n: {"both": n % 2, "act": 0, "dve": 1}[takers]
    turn = lambda n: n // 2 + 1 if takers == "both" else n + 1
    with ExitStack() as ctx:
        xh = sb(nc, ctx, tag + "x_high", [128, KB, N], F32R)
        xl = sb(nc, ctx, tag + "x_low", [128, KB, N], F32R)
        raw = sb(nc, ctx, tag + "w_raw", [128, 2, KB, width])
        wh = sb(nc, ctx, tag + "w_high", [128, 2, KB, width], F32R)
        wl = sb(nc, ctx, tag + "w_low", [128, 2, KB, width], F32R)
        with phase(nc, "w_a", "w_b", "w_rounded", "w_ready", "x_rounded", "x_ready", "product", "taken_by_act", "taken_by_dve",
                   "loaded") as (
                block, w_a, w_b, w_rounded, w_ready, x_rounded, x_ready, product, taken_act, taken_dve, loaded):
            arrived, taken = (w_a, w_b), (taken_act, taken_dve)

            @block.sync
            def _(sp):
                for j in range(J):
                    if j >= 2:
                        sp.wait_ge(w_ready, j - 1)
                    sp.dma_start(raw[:, j % 2, :, :], sources[j]).then_inc(arrived[j % 2], 16)
                for dst, source in loads:
                    sp.dma_start(dst, source).then_inc(loaded, 16)
                if loads:
                    sp.wait_ge(loaded, 16 * len(loads))

            @block.gpsimd
            def _(pool):
                for j in range(J):
                    pool.wait_ge(w_rounded, j + 1)
                    pool.tensor_tensor(wl[:, j % 2, :, :], raw[:, j % 2, :, :], wh[:, j % 2, :, :].bitcast(F32),
                                       ALU.subtract).then_inc(w_ready, 1)
                    if j == 1 and aside is not None:
                        aside(pool)

            @block.tensor
            def _(pe):
                chunks = 0
                for n, (j, g) in enumerate(flat):
                    if n == 0 or flat[n - 1][0] != j:
                        pe.wait_ge(w_ready, j + 1)
                    c = g[2] if g[0] == "feature" else g[1] // 4
                    if c >= chunks:
                        chunks = c + 1
                        pe.wait_ge(x_ready, chunks)
                    if n >= 8:
                        pe.wait_ge(taken[taker(n - 8)], turn(n - 8))
                    ops = []
                    for k in range(KB):
                        for x, w in ((xh, wh), (xl, wh), (xh, wl)):
                            if g[0] == "feature":
                                c0, cn = CH[c]
                                ops.append((m.ps[:, n % 8, 0:cn], w[:, j % 2, k, g[1] * 128:(g[1] + 1) * 128], x[:, k, c0:c0 + cn]))
                            else:
                                ops.append((m.ps[0:P, n % 8, 0:width], x[:, k, tile(g[1])], w[:, j % 2, k, :]))
                    for o, (out, lhsT, rhs) in enumerate(ops):
                        ins = pe.matmul(out, lhsT, rhs, start=o == 0, stop=o == len(ops) - 1)
                    ins.then_inc(product, 1)

            @block.scalar
            def _(act):
                def round_w(j):
                    act.wait_ge(arrived[j % 2], 16 * (j // 2) + 16)
                    if j >= 2:
                        act.wait_ge(product, upto[j - 2])
                    act.activation(wh[:, j % 2, :, :], raw[:, j % 2, :, :], ACT.Copy).then_inc(w_rounded, 1)

                for c, (c0, cn) in enumerate(CH):
                    act.activation(xh[:, :, c0:c0 + cn], m.xt[:, :, c0:c0 + cn], ACT.Copy).then_inc(x_rounded, 1)
                    if c < min(2, J):
                        round_w(c)
                for n, (j, g) in enumerate(flat):
                    if n and flat[n - 1][0] != j and j + 1 < J:
                        round_w(j + 1)
                    if taker(n) == 0:
                        act.wait_ge(product, n + 1)
                        take(j, g, act, m.ps[:, n % 8, :], True).then_inc(taken_act, 1)

            @block.vector
            def _(dve):
                for c, (c0, cn) in enumerate(CH):
                    dve.wait_ge(x_rounded, c + 1)
                    dve.tensor_tensor(xl[:, :, c0:c0 + cn], m.xt[:, :, c0:c0 + cn], xh[:, :, c0:c0 + cn].bitcast(F32),
                                      ALU.subtract).then_inc(x_ready, 1)
                for n, (j, g) in enumerate(flat):
                    if taker(n) == 1:
                        dve.wait_ge(product, n + 1)
                        take(j, g, dve, m.ps[:, n % 8, :], False).then_inc(taken_dve, 1)


def qkv_for_attention(nc, m, tag, sources, qt, kt, v, x_row):
    def take(j, g, eng, bank, on_act):
        if j < 4:
            c0, cn = CH[g[2]]
            return copy_scaled(eng, (qt, kt)[j // 2][:, 2 * (j % 2) + g[1], c0:c0 + cn], bank[:, 0:cn], on_act)
        pairs = bank[0:P, 0:256].rearrange("p (b e c) -> p b e c", b=2, e=2)
        b0 = 2 * (j - 4)
        copy_scaled(eng, v[:, g[1], b0:b0 + 2, 0:64], pairs[:, :, 0, :], on_act)
        return copy_scaled(eng, v[:, g[1], b0:b0 + 2, 128:192], pairs[:, :, 1, :], on_act)

    def aside(pool):
        for i in range(T):
            pool.memset(v[:, i, :, 64:128], 1.0)
        add_row(pool, m.x, x_row)

    by_feature = [("feature", f, c) for c in range(len(CH)) for f in range(2)]
    by_token = [("token", i) for i in range(T)]
    split_gemm_phase(nc, m, tag, sources, 256, [by_feature] * 4 + [by_token] * 2, take, aside=aside)


def add_product(nc, m, tag, sources, loads=()):
    def take(j, g, dve, bank, on_act):
        part = m.x[:, g[1], 256 * j:256 * j + 256]
        return dve.tensor_tensor(part, bank[0:P, 0:256], part, ALU.add)

    split_gemm_phase(nc, m, tag, sources, 256, [[("token", i) for i in range(T)]] * 2, take, takers="dve", loads=loads)


def add_row(pool, x, row):
    for i in range(T):
        pool.tensor_tensor(x[:, i, :], x[:, i, :], row, ALU.add)


def pieces(w, n):
    f = w.shape[1] // n
    return [wview(w)[:, :, j * f:(j + 1) * f] for j in range(n)]


def qkv_unsplit(nc, m, w, wq, wk, wv, qt, kt, v, loads):
    def products(n, bank):
        if n < 24:
            wx, f = (wq, n // 3) if n < 12 else (wk, n // 3 - 4)
            c0, cn = CH[n % 3]
            return [(bank[:, 0:cn], wx(k)[:, f * 128:(f + 1) * 128], m.xt[:, k, c0:c0 + cn]) for k in range(KB)]
        return [(bank[0:P, :], m.xt[:, k, tile(n - 24)], wv(k)) for k in range(KB)]

    def take(n, eng, bank, on_act):
        if n < 24:
            dst, f = (qt, n // 3) if n < 12 else (kt, n // 3 - 4)
            c0, cn = CH[n % 3]
            return copy_scaled(eng, dst[:, f, c0:c0 + cn], bank[:, 0:cn], on_act)
        i = n - 24
        pairs = bank[0:P, :].rearrange("p (b e c) -> p b e c", b=KB, e=2)
        copy_scaled(eng, v[:, i, :, 0:64], pairs[:, :, 0, :], on_act)
        return copy_scaled(eng, v[:, i, :, 128:192], pairs[:, :, 1, :], on_act)

    groups_phase(nc, m, 24 + T, products, take, loads=loads)


def ones_between(nc, v):
    with phase(nc, "filled") as (block, filled):
        @block.gpsimd
        def _(pool):
            for i in range(T):
                pool.memset(v[:, i, :, 64:128], 1.0).then_inc(filled, 1)


def move(nc, pairs):
    load_phase(nc, pairs)



def l1_gnn(nc, m, a, tok):
    with ExitStack() as ctx:
        with ExitStack() as c2:
            xn = sb(nc, c2, "xn_rows", [P, T, D])
            layernorm_phase(nc, m, m.x, lambda i: xn[:, i, :], m.xt, loads=[(tok(a["xs"]), m.x[:, :, :])])
            move(nc, [(tok(a["xn"]), xn[:, :, :])])
        with ExitStack() as c2:
            qt = m.xraw[:, 0:KB * N].rearrange("p (k n) -> p k n", k=KB)
            kt = sb(nc, c2, "kt", [128, KB, N])
            v = sb(nc, c2, "v", [P, T, KB, 192])
            ones_between(nc, v)
            with ExitStack() as c3:
                w = sb(nc, c3, "wqkv", [128, 3, KB, D])
                qkv_unsplit(nc, m, w, lambda k: w[:, 0, k, :], lambda k: w[:, 1, k, :], lambda k: w[:, 2, k, :], qt, kt, v,
                                  [(w[:, j, :, :], wview(x)) for j, x in enumerate((a["L1_gnn_Wq"], a["L1_gnn_Wk"], a["L1_gnn_Wv"]))])
            mask = sb(nc, c2, "mask", [P, T, N], BF16)

            with phase(nc, "turned", "taken") as (block, turned, taken):
                @block.tensor
                def _(pe):
                    for n in range(T * 3):
                        i, (c0, cn) = n // 3, CH[n % 3]
                        if n >= 8:
                            pe.wait_ge(taken, n - 7)
                        for b in range(cn // P):
                            ins = pe.transpose(m.ps[0:P, n % 8, b * P:(b + 1) * P], m.cnt[:, c0 // P + b, tile(i)], m.ident[0:P, 0:P])
                        ins.then_inc(turned, 1)

                @block.vector
                def _(dve):
                    for n in range(T * 3):
                        i, (c0, cn) = n // 3, CH[n % 3]
                        dve.wait_ge(turned, n + 1)
                        dve.tensor_scalar(mask[:, i, c0:c0 + cn], m.ps[0:P, n % 8, 0:cn], 0.0, -1e30, ALU.is_equal, ALU.mult).then_inc(taken, 1)

            attention(nc, m, "gnn_", qt, kt, v, m.xt, 2, mask, m.cnt)

    move(nc, [(m.x[:, :, :], tok(a["xn"]))])
    with ExitStack() as ctx:
        rows = sb(nc, ctx, "gnn_rows", [P, 5, D])
        w1 = sb(nc, ctx, "gnn_w1", [128, KB, 256])
        w2 = sb(nc, ctx, "gnn_w2", [128, 2, D])
        b1 = sb(nc, ctx, "gnn_b1", [128, 2])
        names = (a["L1_gnn_ln1_g"], a["L1_gnn_ln1_b"], a["L1_gnn_ln2_g"], a["L1_gnn_ln2_b"], a["L1_gnn_b2"])
        add_product(nc, m, "gnn_out_", pieces(a["L1_gnn_Wo"], 2),
                    loads=[(w1[:, :, :], wview(a["L1_gnn_W1"])), (w2[:, :, :], wview(a["L1_gnn_W2"])), (b1[:, :], a["L1_gnn_b1"])]
                    + [(rows[:, j, :], spread_row(r)) for j, r in enumerate(names)])
        y = sb(nc, ctx, "gnn_y", [P, T, D])
        hid = sb(nc, ctx, "gnn_hidden", [128, 2, N])
        layernorm_phase(nc, m, m.x, lambda i: y[:, i, :], m.xt, gain_row=rows[:, 0, :], bias_row=rows[:, 1, :])

        def hidden_products(n, bank):
            f, (c0, cn) = n // 3, CH[n % 3]
            return [(bank[:, 0:cn], w1[:, k, f * 128:(f + 1) * 128], m.xt[:, k, c0:c0 + cn]) for k in range(KB)]

        def hidden_take(n, dve, bank):
            f, (c0, cn) = n // 3, CH[n % 3]
            return dve.tensor_scalar(hid[:, f, c0:c0 + cn], bank[:, 0:cn], b1[:, f:f + 1], 0.0, ALU.add, ALU.max)

        vector_groups_phase(nc, m, 6, hidden_products, hidden_take)
        vector_groups_phase(nc, m, T, lambda n, bank: [(bank[0:P, :], hid[:, k, tile(n)], w2[:, k, :]) for k in range(2)],
                            lambda n, dve, bank: dve.tensor_tensor(y[:, n, :], bank[0:P, :], y[:, n, :], ALU.add))
        with phase(nc, "added") as (block, added):
            @block.vector
            def _(dve):
                for i in range(T):
                    dve.tensor_tensor(y[:, i, :], y[:, i, :], rows[:, 4, :], ALU.add).then_inc(added, 1)
        saved = sb(nc, ctx, "gnn_saved", [P, T, D])
        layernorm_phase(nc, m, y, lambda i: m.x[:, i, :], None, gain_row=rows[:, 2, :], bias_row=rows[:, 3, :],
                        loads=[(saved[:, :, :], tok(a["xs"]))])
        add_to_saved(nc, m, a, tok, saved)


def add_to_saved(nc, m, a, tok, saved):
    with phase(nc, "added", "stored") as (block, added, stored):
        @block.sync
        def _(sp):
            half = T // 2
            for k in range(2):
                sp.wait_ge(added, half * (k + 1))
                sp.dma_start(tok(a["xs"])[:, half * k:half * (k + 1), :], m.x[:, half * k:half * (k + 1), :]).then_inc(stored, 16)
            sp.wait_ge(stored, 32)

        @block.vector
        def _(dve):
            for i in range(T):
                dve.tensor_tensor(m.x[:, i, :], m.x[:, i, :], saved[:, i, :], ALU.add).then_inc(added, 1)



def l1_mix(nc, m, a, tok):
    F = 256
    H2 = 2 * D
    head = lambda h: slice(64 * (h % 2), 64 * (h % 2) + 64)
    with ExitStack() as ctx:
        cols = sb(nc, ctx, "mixer_cols", [128, 4, KB])
        move(nc, [(m.x[:, :, :], tok(a["xn"]))] + [(cols[:, j, :], c) for j, c in enumerate(
            (a["L1_mix_g1"], a["L1_mix_be1"], a["L1_mix_g2"], a["L1_mix_be2"]))])
        layernorm_phase(nc, m, m.x, lambda i: m.tmp[:, i % 2, :], m.xt, gain_col=cols[:, 0, :], bias_col=cols[:, 1, :])
        attn = sb(nc, ctx, "mixer_attn", [P, T, D])
        with ExitStack() as c2:
            qt = sb(nc, c2, "mixer_q", [128, KB, N])
            kt = sb(nc, c2, "mixer_k", [128, KB, N])
            v = sb(nc, c2, "mixer_v", [P, T, HEADS, 65])
            with ExitStack() as c3:
                bqk = sb(nc, c3, "mixer_bqk", [128, 12])
                bv = sb(nc, c3, "mixer_bv", [P, D])
                bproj = sb(nc, c3, "mixer_bproj", [P, D])

                def take(j, g, dve, bank, on_act):
                    if j < 4:
                        c0, cn = CH[g[2]]
                        return dve.tensor_scalar((qt, kt)[j // 2][:, 2 * (j % 2) + g[1], c0:c0 + cn], bank[:, 0:cn],
                                                 bqk[:, 2 * j + g[1]:2 * j + g[1] + 1], None, ALU.add)
                    h0, by_head = 4 * (j - 4), lambda ap: ap.rearrange("p (h c) -> p h c", h=4)
                    return dve.tensor_tensor(v[:, g[1], h0:h0 + 4, 0:64], by_head(bank[0:P, 0:256]), by_head(bv[:, 64 * h0:64 * h0 + 256]), ALU.add)

                move(nc, [(bqk[:, :], a["L1_mix_bqk"]), (bproj[:, :], spread_row(a["L1_mix_bproj"])), (bv[:, :], a["L1_mix_bqkv"][2 * D:3 * D].rearrange("(a n) -> a n", a=1).to_broadcast([P, D]))])
                split_gemm_phase(nc, m, "mixer_qkv_", pieces(a["L1_mix_Wqkv"], 6), 256,
                                 [[("feature", f, c) for c in range(len(CH)) for f in range(2)]] * 4 + [[("token", i) for i in range(T)]] * 2,
                                 take, takers="dve", aside=lambda pool: add_row(pool, m.x, bproj[:, :]))
                with phase(nc, "filled") as (block, filled):
                    @block.vector
                    def _(dve):
                        dve.memset(v[:, :, :, 64:65], 1.0).then_inc(filled, 1)
            pm = sb(nc, c2, "mixer_pmat", [128, 2, F])
            kvs = sb(nc, c2, "mixer_kv", [128, HEADS, 2, 65])
            nm = sb(nc, c2, "mixer_neg_max", [P, 4])
            feat = sb(nc, c2, "mixer_features", [P, 3, F])
            feat_t = sb(nc, c2, "mixer_features_t", [128, 2, 2, P])
            inv = sb(nc, c2, "mixer_inverse", [P, 4])
            NU = HEADS * T
            with phase(nc, "zeroed", "loaded", "product", "maxed", "expd", "added", "taken", "shifted") as (
                    block, zeroed, loaded, product, maxed, expd, added, taken, shifted):
                @block.gpsimd
                def _(pool):
                    pool.memset(pm[:, :, :], 0.0).then_inc(zeroed, 1)

                @block.sync
                def _(sp):
                    sp.wait_ge(zeroed, 1)
                    for h in range(2):
                        sp.dma_start(pm[head(h), h, :], a["L1_mix_Pmat"]).then_inc(loaded, 16)

                @block.tensor
                def _(pe):
                    def sums(n):
                        h, i = n // T, n % T
                        if i == 0 and h >= 2:
                            pe.wait_ge(taken, h - 1)
                        pe.wait_ge(expd, n + 1)
                        for f in range(2):
                            ins = pe.matmul(m.ps[:, 4 + h % 2, 65 * f:65 * f + 65], feat[:, n % 3, f * 128:(f + 1) * 128], v[:, i, h, :],
                                            start=i == 0 and f == 0, stop=i == T - 1, skip_group_check=True)
                        ins.then_inc(added, 1)

                    pe.wait_ge(loaded, 32)
                    for n in range(NU + 2):
                        if n < NU:
                            h, i = n // T, n % T
                            if n >= 4:
                                pe.wait_ge(expd, n - 3)
                            pe.matmul(m.ps[0:P, n % 4, 0:F], kt[:, h // 2, tile(i)], pm[:, h % 2, :], start=True, stop=True).then_inc(product, 1)
                        if n >= 2:
                            sums(n - 2)

                @block.vector
                def _(dve):
                    def take(h):
                        dve.wait_ge(added, T * (h + 1))
                        dve.tensor_scalar(kvs[:, h, :, :], m.ps[:, 4 + h % 2, 0:130].rearrange("p (f c) -> p f c", f=2),
                                          F ** -0.5, None, ALU.mult).then_inc(taken, 1)

                    for n in range(NU):
                        dve.wait_ge(product, n + 1)
                        if n >= 4:
                            dve.wait_ge(expd, n - 3)
                        dve.tensor_reduce(nm[:, n % 4:n % 4 + 1], m.ps[0:P, n % 4, 0:F], AX.X, ALU.max, negate=True).then_inc(maxed, 1)
                        if n % T == 4 and n > T:
                            take(n // T - 1)
                    take(HEADS - 1)
                    dve.wait_ge(taken, HEADS)
                    dve.tensor_scalar(kvs[:, :, :, 64:65], kvs[:, :, :, 64:65], 1e-6, None, ALU.add).then_inc(shifted, 1)

                @block.scalar
                def _(act):
                    for n in range(NU):
                        act.wait_ge(maxed, n + 1)
                        if n >= 3:
                            act.wait_ge(added, n - 2)
                        act.activation(feat[:, n % 3, :], m.ps[0:P, n % 4, 0:F], ACT.Exp, bias=nm[:, n % 4:n % 4 + 1]).then_inc(expd, 1)

            with phase(nc, "product", "maxed", "expd", "turned", "kept", "out", "inverted", "done") as (
                    block, product, maxed, expd, turned, kept, out, inverted, done):
                @block.tensor
                def _(pe):
                    for n in range(NU + 4):
                        if n < NU:
                            h, i = n // T, n % T
                            if n >= 4:
                                pe.wait_ge(expd, n - 3)
                            pe.matmul(m.ps[0:P, n % 4, 0:F], qt[:, h // 2, tile(i)], pm[:, h % 2, :], start=True, stop=True).then_inc(product, 1)
                        if 2 <= n < NU + 2:
                            u = n - 2
                            pe.wait_ge(expd, u + 1)
                            if u >= 2:
                                pe.wait_ge(kept, u - 1)
                            for f in range(2):
                                ins = pe.transpose(m.ps[:, 4 + u % 2, f * P:(f + 1) * P], feat[:, u % 3, f * 128:(f + 1) * 128], m.ident[0:P, 0:P])
                            ins.then_inc(turned, 1)
                        if n >= 4:
                            u = n - 4
                            pe.wait_ge(kept, u + 1)
                            if u >= 2:
                                pe.wait_ge(done, u - 1)
                            for f in range(2):
                                ins = pe.matmul(m.ps[0:P, 6 + u % 2, 0:65], feat_t[:, u % 2, f, :], kvs[:, u // T, f, :], start=f == 0, stop=f == 1)
                            ins.then_inc(out, 1)

                @block.vector
                def _(dve):
                    def finish(u):
                        h, i = u // T, u % T
                        dve.wait_ge(out, u + 1)
                        dve.reciprocal(inv[:, u % 4:u % 4 + 1], m.ps[0:P, 6 + u % 2, 64:65]).then_inc(inverted, 1)
                        dve.wait_ge(inverted, u + 1)
                        dve.tensor_scalar(attn[:, i, 64 * h:64 * h + 64], m.ps[0:P, 6 + u % 2, 0:64], inv[:, u % 4:u % 4 + 1], None,
                                          ALU.mult).then_inc(done, 1)

                    for n in range(NU + 4):
                        if n < NU:
                            dve.wait_ge(product, n + 1)
                            if n >= 4:
                                dve.wait_ge(expd, n - 3)
                            dve.tensor_reduce(nm[:, n % 4:n % 4 + 1], m.ps[0:P, n % 4, 0:F], AX.X, ALU.max, negate=True).then_inc(maxed, 1)
                        if n >= 4:
                            finish(n - 4)

                @block.scalar
                def _(act):
                    for n in range(NU + 2):
                        if n < NU:
                            act.wait_ge(maxed, n + 1)
                            if n >= 3:
                                act.wait_ge(turned, n - 2)
                            act.activation(feat[:, n % 3, :], m.ps[0:P, n % 4, 0:F], ACT.Exp, bias=nm[:, n % 4:n % 4 + 1]).then_inc(expd, 1)
                        if n >= 2:
                            u = n - 2
                            act.wait_ge(turned, u + 1)
                            if u >= 2:
                                act.wait_ge(out, u - 1)
                            act.activation(feat_t[:, u % 2, :, :], m.ps[:, 4 + u % 2, 0:2 * P].rearrange("p (f t) -> p f t", f=2),
                                           ACT.Copy).then_inc(kept, 1)

        transpose_rows_phase(nc, m, attn, m.xt)
        add_product(nc, m, "mixer_proj_", pieces(a["L1_mix_Wproj"], 2))
        w2 = sb(nc, ctx, "mixer_w2", [128, H2 // 128, D])
        b1 = sb(nc, ctx, "mixer_b1", [128, H2 // 128])
        b2 = sb(nc, ctx, "mixer_b2", [P, D])
        hid = sb(nc, ctx, "mixer_hidden", [128, H2 // 128, N])
        move(nc, [(b1[:, :], a["L1_mix_b1"]), (b2[:, :], spread_row(a["L1_mix_b2"]))])
        layernorm_phase(nc, m, m.x, lambda i: m.tmp[:, i % 2, :], m.xt, gain_col=cols[:, 2, :], bias_col=cols[:, 3, :])

        def hidden_take(j, g, act, bank, on_act):
            f, (c0, cn) = 2 * j + g[1], CH[g[2]]
            return act.activation(hid[:, f, c0:c0 + cn], bank[:, 0:cn], ACT.Gelu, bias=b1[:, f:f + 1])

        split_gemm_phase(nc, m, "mixer_hidden_", pieces(a["L1_mix_W1"], 4), 256,
                         [[("feature", f, c) for c in range(len(CH)) for f in range(2)]] * 4, hidden_take, takers="act",
                         aside=lambda pool: add_row(pool, m.x, b2[:, :]),
                         loads=[(w2[:, :, :], wview(a["L1_mix_W2"])), (attn[:, :, :], tok(a["xs"]))])
        vector_groups_phase(nc, m, T, lambda n, bank: [(bank[0:P, :], hid[:, k, tile(n)], w2[:, k, :]) for k in range(H2 // 128)],
                            lambda n, dve, bank: dve.tensor_tensor(m.x[:, n, :], bank[0:P, :], m.x[:, n, :], ALU.add))
        add_to_saved(nc, m, a, tok, attn)


def transpose_rows_phase(nc, m, src, dst):
    with phase(nc, "turned", "kept") as (block, turned, kept):
        @block.tensor
        def _(pe):
            for i in range(T):
                if i >= 4:
                    pe.wait_ge(kept, i - 3)
                for k in range(KB):
                    ins = pe.transpose(m.ps[:, i % 4, k * P:(k + 1) * P], src[:, i, k * 128:(k + 1) * 128], m.ident[0:P, 0:P])
                ins.then_inc(turned, 1)

        @block.scalar
        def _(act):
            for i in range(T):
                act.wait_ge(turned, i + 1)
                act.activation(dst[:, :, tile(i)], m.ps[:, i % 4, 0:KB * P].rearrange("p (k t) -> p k t", k=KB), ACT.Copy).then_inc(kept, 1)



def l1_ffn(nc, m, a, tok):
    L, NE, H = 4, 8, 256
    with ExitStack() as ctx:
        layernorm_phase(nc, m, m.x, lambda i: m.x[:, i, :])
        cols = sb(nc, ctx, "ln_cols", [128, 4, KB])
        rows = sb(nc, ctx, "row", [P, D])
        with nc.Fori(0, L) as l:
            at = lambda v: v[bass.ds(l, 1)].rearrange("a p k -> (a p) k")
            params = [(cols[:, j, :], at(c)) for j, c in enumerate((a["L1_ffn_ln1_w"], a["L1_ffn_ln1_b"], a["L1_ffn_ln2_w"], a["L1_ffn_ln2_b"]))]
            params.append((rows[:, :], a["L1_ffn_out_b"][bass.ds(l, 1), :].to_broadcast([P, D])))
            layernorm_phase(nc, m, m.x, lambda i: m.tmp[:, i % 2, :], m.xt, gain_col=cols[:, 0, :], bias_col=cols[:, 1, :], loads=params)
            with ExitStack() as c2:
                qt = sb(nc, c2, "ffn_qt", [128, KB, N])
                kt = sb(nc, c2, "ffn_kt", [128, KB, N])
                v = sb(nc, c2, "ffn_v", [P, T, KB, 192])
                w = a["L1_ffn_qkv_w"][bass.ds(l, 1)].rearrange("a (k p) f -> p (a k) f", p=128)
                qkv_for_attention(nc, m, "ffn_qkv_", [w[:, :, 256 * j:256 * j + 256] for j in range(6)], qt, kt, v, rows[:, :])
                attention(nc, m, "ffn_", qt, kt, v, m.xt, 3)
            with ExitStack() as c2:
                wo = a["L1_ffn_out_w"][bass.ds(l, 1)].rearrange("a (k p) f -> p (a k) f", p=128)
                add_product(nc, m, "ffn_out_", [wo[:, :, 256 * j:256 * j + 256] for j in range(2)])
                layernorm_phase(nc, m, m.x, lambda i: m.tmp[:, i % 2, :], m.xt, gain_col=cols[:, 2, :], bias_col=cols[:, 3, :])
                moe(nc, m, a, l, c2, NE, H)
        row2 = sb(nc, ctx, "final_rows", [P, 2, D])
        xs = sb(nc, ctx, "block_input", [P, T, D])
        layernorm_phase(nc, m, m.x, lambda i: m.xt_rows[:, i, :], None, gain_row=row2[:, 0, :], bias_row=row2[:, 1, :],
                        loads=[(xs[:, :, :], tok(a["xs"])), (row2[:, 0, :], spread_row(a["L1_ffn_fln_w"])), (row2[:, 1, :], spread_row(a["L1_ffn_fln_b"]))])
        with phase(nc, "added", "stored") as (block, added, stored):
            @block.vector
            def _(dve):
                for i in range(T):
                    dve.tensor_tensor(xs[:, i, :], xs[:, i, :], m.xt_rows[:, i, :], ALU.add).then_inc(added, 1)

            @block.sync
            def _(sp):
                out = tok(a["out"])
                for i in range(T):
                    sp.wait_ge(added, i + 1)
                    sp.dma_start(out[:, i, :], xs[:, i, :]).then_inc(stored, 16)
                sp.wait_ge(stored, 16 * T)


def moe(nc, m, a, l, ctx, NE, H):
    wg = sb(nc, ctx, "ffn_w_gate", [128, KB, NE])
    logit = sb(nc, ctx, "logits", [P, T, 2 * NE])
    struck = sb(nc, ctx, "struck", [P, T, 2 * NE])
    best = sb(nc, ctx, "top", [P, T, 8])
    only2 = sb(nc, ctx, "top2", [P, T, 8])
    d = sb(nc, ctx, "logit_shifted", [P, T, NE])
    e = sb(nc, ctx, "logit_exp", [P, T, NE])
    eg = sb(nc, ctx, "chosen_exp", [P, T, NE])
    den = sb(nc, ctx, "gate_sum", [P, T])
    inv = sb(nc, ctx, "gate_inv", [P, T])
    gates = sb(nc, ctx, "moe_gates", [P, T, NE])
    gates_t = sb(nc, ctx, "gates_t", [128, N])
    eb1 = sb(nc, ctx, "eb1", [128, 2, H // 128])
    eb2 = sb(nc, ctx, "eb2", [128, D])
    FB = H // 128
    xh = sb(nc, ctx, "moe_x_high", [128, KB, N], F32R)
    xl = sb(nc, ctx, "moe_x_low", [128, KB, N], F32R)
    w1 = sb(nc, ctx, "ew1", [128, 2, KB, H])
    w1h = sb(nc, ctx, "ew1_high", [128, 2, KB, H], F32R)
    w1l = sb(nc, ctx, "ew1_low", [128, 2, KB, H], F32R)
    w2 = sb(nc, ctx, "ew2", [128, 2, FB, D])
    w2h = sb(nc, ctx, "ew2_high", [128, 2, FB, D], F32R)
    w2l = sb(nc, ctx, "ew2_low", [128, 2, FB, D], F32R)
    hid = sb(nc, ctx, "expert_hidden", [128, 3, 512])
    hh = sb(nc, ctx, "expert_hidden_high", [128, FB, N], F32R)
    hl = sb(nc, ctx, "expert_hidden_low", [128, FB, N], F32R)
    NG = 3 * FB
    SLOTS = 5
    w1_all = a["L1_ffn_ew1"].rearrange("l e (k p) f -> (l e) p k f", p=128)
    eb1_all = a["L1_ffn_eb1"].rearrange("l e p k -> (l e) p k")
    w2_all = a["L1_ffn_ew2"].rearrange("l e (k p) f -> (l e) p k f", p=128)

    def load_pairs(expert, c):
        own = lambda v: v[bass.ds(expert, 1)]
        return [(w1[:, c, :, :], own(w1_all).rearrange("a p k f -> (a p) k f")), (w2[:, c, :, :], own(w2_all).rearrange("a p k f -> (a p) k f")),
                (eb1[:, c, :], own(eb1_all).rearrange("a p k -> (a p) k"))]

    def round_weights(act, c):
        act.activation(w1h[:, c, :, :], w1[:, c, :, :], ACT.Copy)
        return act.activation(w2h[:, c, :, :], w2[:, c, :, :], ACT.Copy)

    def rest_weights(pool, c):
        pool.tensor_tensor(w1l[:, c, :, :], w1[:, c, :, :], w1h[:, c, :, :].bitcast(F32), ALU.subtract)
        return pool.tensor_tensor(w2l[:, c, :, :], w2[:, c, :, :], w2h[:, c, :, :].bitcast(F32), ALU.subtract)

    by_token = lambda ap: ap.rearrange("p (t a) -> p t a", a=1).to_broadcast([P, T, NE])
    with phase(nc, "loaded", "first", "w_rounded", "x_rounded", "rest", "padded", "filled", "product", "taken", "maxed", "two", "strike",
               "v_step", "a_step", "t_step") as (
            block, loaded, first, w_rounded, x_rounded, rest, padded, filled, product, taken, maxed, two, strike, v_step, a_step, t_step):
        def x_rest(eng, c):
            c0, cn = CH[c]
            eng.wait_ge(x_rounded, c + 1)
            eng.tensor_tensor(xl[:, :, c0:c0 + cn], m.xt[:, :, c0:c0 + cn], xh[:, :, c0:c0 + cn].bitcast(F32), ALU.subtract).then_inc(rest, 1)

        @block.gpsimd
        def _(pool):
            pool.memset(gates_t[:, :], 0.0).then_inc(padded, 1)
            pool.memset(eb2[:, :], 0.0).then_inc(padded, 1)
            x_rest(pool, 2)
            pool.wait_ge(w_rounded, 1)
            rest_weights(pool, 0).then_inc(rest, 1)

        @block.sync
        def _(sp):
            sp.dma_start(wg[:, :, :], a["L1_ffn_w_gate"][bass.ds(l, 1)].rearrange("a (k p) f -> p (a k) f", p=128)).then_inc(loaded, 16)
            sp.wait_ge(padded, 2)
            sp.dma_start(eb2[0:NE, :], a["L1_ffn_eb2"][bass.ds(l, 1)].rearrange("a e f -> (a e) f")).then_inc(first, 16)
            for dst, src in load_pairs(l * NE, 0):
                sp.dma_start(dst, src).then_inc(first, 16)

        @block.tensor
        def _(pe):
            pe.wait_ge(loaded, 16)
            for i in range(T):
                if i >= 4:
                    pe.wait_ge(taken, i - 3)
                for k in range(KB):
                    ins = pe.matmul(m.ps[0:P, i % 4, 0:NE], m.xt[:, k, tile(i)], wg[:, k, :], start=k == 0, stop=k == KB - 1)
                ins.then_inc(product, 1)
            pe.wait_ge(v_step, 5)
            for i in range(T):
                ins = pe.transpose(m.ps[0:NE, 4 + i // 4, (i % 4) * P:(i % 4 + 1) * P], gates[:, i, :], m.ident[0:P, 0:P])
            ins.then_inc(t_step, 1)

        @block.vector
        def _(dve):
            dve.memset(logit[:, :, NE:2 * NE], -BIG).then_inc(filled, 1)
            dve.memset(only2[:, :, :], -BIG).then_inc(filled, 1)
            x_rest(dve, 0)
            x_rest(dve, 1)
            for i in range(T):
                dve.wait_ge(product, i + 1)
                dve.tensor_copy(logit[:, i, 0:NE], m.ps[0:P, i % 4, 0:NE]).then_inc(taken, 1)
            dve.wait_ge(filled, 2)
            for i in range(T):
                dve.wait_ge(taken, i + 1)
                dve.max(best[:, i, :], logit[:, i, :]).then_inc(maxed, 1)
            dve.wait_ge(maxed, T)
            dve.tensor_copy(only2[:, :, 0:2], best[:, :, 0:2]).then_inc(two, 1)
            dve.tensor_tensor(d[:, :, :], logit[:, :, 0:NE], best[:, :, 0:1].to_broadcast([P, T, NE]), ALU.subtract).then_inc(v_step, 1)
            dve.wait_ge(two, 1)
            for i in range(T):
                dve.match_replace(struck[:, i, :], only2[:, i, :], logit[:, i, :], BIG).then_inc(strike, 1)
            dve.wait_ge(strike, T)
            dve.wait_ge(a_step, 1)
            dve.scalar_tensor_tensor(eg[:, :, :], struck[:, :, 0:NE], BIG, e[:, :, :], ALU.is_equal, ALU.mult).then_inc(v_step, 1)
            dve.wait_ge(v_step, 2)
            dve.tensor_reduce(den[:, :], eg[:, :, :], AX.X, ALU.add).then_inc(v_step, 1)
            dve.wait_ge(v_step, 3)
            dve.reciprocal(inv[:, :], den[:, :]).then_inc(v_step, 1)
            dve.wait_ge(v_step, 4)
            dve.tensor_tensor(gates[:, :, :], eg[:, :, :], by_token(inv[:, :]), ALU.mult).then_inc(v_step, 1)

        @block.scalar
        def _(act):
            for c0, cn in CH:
                act.activation(xh[:, :, c0:c0 + cn], m.xt[:, :, c0:c0 + cn], ACT.Copy).then_inc(x_rounded, 1)
            act.wait_ge(first, 64)
            round_weights(act, 0).then_inc(w_rounded, 1)
            act.wait_ge(padded, 2)
            act.wait_ge(v_step, 1)
            act.activation(e[:, :, :], d[:, :, :], ACT.Exp).then_inc(a_step, 1)
            act.wait_ge(t_step, 1)
            for c0, cn in CH:
                ins = act.activation(gates_t[0:NE, c0:c0 + cn], m.ps[0:NE, 4 + c0 // 500, 0:cn], ACT.Copy)
            ins.then_inc(a_step, 1)

    with phase(nc, "w_rounded", "w_ready", "w_next_a", "w_next_b", "h_product", "h_taken", "h_rounded", "h_ready", "y_product", "y_taken") as (
            block, w_rounded, w_ready, w_next_a, w_next_b, h_product, h_taken, h_rounded, h_ready, y_product, y_taken):
        arrived = (w_next_a, w_next_b)
        STEPS = NE // 2

        @block.sync
        def _(sp):
            def load(expert, c):
                for dst, src in load_pairs(expert, c):
                    sp.dma_start(dst, src).then_inc(arrived[c], 16)

            load(l * NE + 1, 1)
            with sp.Fori(0, STEPS - 1) as it:
                for c in range(2):
                    sp.wait_ge(y_product, 2 * T * it + T * (c + 2))
                    load(l * NE + 2 * it + 2 + c, c)

        @block.tensor
        def _(pe):
            def expert(it, c):
                for g in range(NG):
                    f, (c0, cn) = g % FB, CH[g // FB]
                    pe.wait_ge(h_taken, 2 * NG * it + NG * c + g + 1)
                    for k in range(KB):
                        for q, (x, w) in enumerate(((xh, w1h), (xl, w1h), (xh, w1l))):
                            ins = pe.matmul(m.ps[:, g % 3, 0:cn], w[:, c, k, f * 128:(f + 1) * 128], x[:, k, c0:c0 + cn],
                                            start=k == 0 and q == 0, stop=k == KB - 1 and q == 2)
                    ins.then_inc(h_product, 1)
                for i in range(T):
                    n = T * c + i
                    pe.wait_ge(h_ready, 2 * NG * it + NG * c + FB * (i // 4 + 1) + 3)
                    pe.wait_ge(y_taken, 2 * T * it + n + 1 - SLOTS + T)
                    for k in range(FB):
                        for q, (x, w) in enumerate(((hh, w2h), (hl, w2h), (hh, w2l))):
                            ins = pe.matmul(m.ps[0:P, 3 + n % SLOTS, :], x[:, k, tile(i)], w[:, c, k, :],
                                            start=k == 0 and q == 0, stop=k == FB - 1 and q == 2)
                    ins.then_inc(y_product, 1)

            for i in range(T):
                if i >= SLOTS:
                    pe.wait_ge(y_taken, i - SLOTS + 1)
                pe.matmul(m.ps[0:P, 3 + i % SLOTS, :], gates_t[:, tile(i)], eb2[:, :], start=True, stop=True).then_inc(y_product, 1)
            with pe.Fori(0, STEPS) as it:
                for c in range(2):
                    pe.wait_ge(w_ready, 2 * it + c + 1)
                    expert(it, c)

        @block.gpsimd
        def _(pool):
            def expert(it, c):
                for g in range(NG):
                    f, (c0, cn) = g % FB, CH[g // FB]
                    pool.wait_ge(h_rounded, 2 * NG * it + NG * c + g + 1)
                    pool.tensor_tensor(hl[:, f, c0:c0 + cn], hid[:, g % 3, 0:cn], hh[:, f, c0:c0 + cn].bitcast(F32),
                                       ALU.subtract).then_inc(h_ready, 1)

            def next_weights(it, c):
                pool.wait_ge(w_rounded, 2 * it + c + 1)
                rest_weights(pool, 1 - c).then_inc(w_ready, 1)

            pool.sem_inc(h_ready, 3)
            pool.sem_inc(w_ready, 1)
            with pool.Fori(0, STEPS - 1) as it:
                for c in range(2):
                    expert(it, c)
                    next_weights(it, c)
            expert(STEPS - 1, 0)
            next_weights(STEPS - 1, 0)
            expert(STEPS - 1, 1)

        @block.scalar
        def _(act):
            def expert(it, c):
                for g in range(NG):
                    f, (c0, cn) = g % FB, CH[g // FB]
                    act.wait_ge(h_product, 2 * NG * it + NG * c + g + 1)
                    act.wait_ge(h_ready, 2 * NG * it + NG * c + g + 1)
                    act.activation(hid[:, g % 3, 0:cn], m.ps[:, g % 3, 0:cn], ACT.Gelu, bias=eb1[:, c, f:f + 1]).then_inc(h_taken, 1)
                    act.wait_ge(h_taken, 2 * NG * it + NG * c + g + 4)
                    act.activation(hh[:, f, c0:c0 + cn], hid[:, g % 3, 0:cn], ACT.Copy).then_inc(h_rounded, 1)

            act.sem_inc(h_taken, 3)
            with act.Fori(0, STEPS - 1) as it:
                for c in range(2):
                    expert(it, c)
                    act.wait_ge(arrived[1 - c], 48 * it + 48)
                    round_weights(act, 1 - c).then_inc(w_rounded, 1)
            expert(STEPS - 1, 0)
            act.wait_ge(arrived[1], 48 * STEPS)
            round_weights(act, 1).then_inc(w_rounded, 1)
            expert(STEPS - 1, 1)

        @block.vector
        def _(dve):
            for i in range(T):
                dve.wait_ge(y_product, i + 1)
                dve.tensor_tensor(m.x[:, i, :], m.ps[0:P, 3 + i % SLOTS, :], m.x[:, i, :], ALU.add).then_inc(y_taken, 1)
            with dve.Fori(0, STEPS) as it:
                for c in range(2):
                    for i in range(T):
                        n = T * c + i
                        dve.wait_ge(y_product, 2 * T * it + n + 1 + T)
                        dve.wait_ge(y_taken, 2 * T * it + n + 1)
                        dve.scalar_tensor_tensor(m.x[:, i, :], m.ps[0:P, 3 + n % SLOTS, :], gates[:, i, bass.ds(2 * it + c, 1)], m.x[:, i, :],
                                                 ALU.mult, ALU.add).then_inc(y_taken, 1)



def program(nc, a, stop=None):
    ctx = ExitStack()
    with ctx:
        m = Tensors()
        m.ps = ctx.enter_context(nc.psum_tensor("ps", [128, 8, 512], F32))
        m.gathered = [ctx.enter_context(nc.semaphore(f"gathered{u}")) for u in range(2 * G)]
        m.ident = sb(nc, ctx, "ident", [128, 128])
        m.eps = sb(nc, ctx, "eps", [128, 1])
        m.ones = sb(nc, ctx, "ones", [128, 128])
        m.xraw = sb(nc, ctx, "x", [128, T * D])
        m.x = m.xraw[0:P, :].rearrange("p (t d) -> p t d", t=T)
        xt_raw = sb(nc, ctx, "xt", [128, T * D])
        m.xt = xt_raw[:, 0:KB * N].rearrange("p (k n) -> p k n", k=KB)
        m.xt_rows = xt_raw[0:P, :].rearrange("p (t d) -> p t d", t=T)
        m.bn = sb(nc, ctx, "bn", [P, T, 6])
        m.mv = sb(nc, ctx, "mv", [P, T, 2])
        m.sd = sb(nc, ctx, "sd", [P, T])
        m.rstd = sb(nc, ctx, "rstd", [P, T])
        m.tmp4 = sb(nc, ctx, "tmp", [P, 4, D])
        m.tmp = m.tmp4[:, 0:2, :]
        m.tmp2 = m.tmp4[:, 2:4, :]
        tok = lambda v: v.rearrange("(t p) d -> p t d", p=P)
        ring = lambda i: m.tmp[:, i % 2, :]

        with phase(nc, "made", "loaded") as (block, made, loaded):
            @block.gpsimd
            def _(pool):
                pool.memset(m.ident[:, :], 0.0).then_inc(made, 1)
                pool.memset(m.eps[:, :], EPS).then_inc(made, 1)
                pool.memset(m.ones[:, :], 1.0)
                pool.wait_ge(made, 2)
                pool.affine_select(out=m.ident[:, :], in_=m.ident[:, :], compare_op=ALU.not_equal, fill=1.0,
                                   base=0, pattern=[[-1, 128]], channel_multiplier=1).then_inc(made, 1)

            @block.sync
            def _(sp):
                sp.dma_start(m.x[:, :, :], tok(a["x"])).then_inc(loaded, 16)
                sp.wait_ge(loaded, 16)

        cctx = ctx.enter_context(ExitStack())
        m.cnt = sb(nc, cctx, "cnt", [P, T, NPAD])
        l0_gnn(nc, m, a, tok, ring)
        if stop == "gnn0":
            return
        l0_mix(nc, m, a)
        if stop == "mix0":
            return
        l0_ffn(nc, m, a)
        if stop == "ffn0":
            return
        l1_gnn(nc, m, a, tok)
        cctx.close()
        if stop == "gnn1":
            return
        l1_mix(nc, m, a, tok)
        if stop == "mix1":
            return
        l1_ffn(nc, m, a, tok)


def l0_gnn(nc, m, a, tok, ring):
    with ExitStack() as ctx:
        m.acc = sb(nc, ctx, "acc", [128, 8, NPAD])
        with ExitStack() as c2:
            up = sb(nc, c2, "w_up", [128, 2, MUL])
            res = sb(nc, c2, "up_rows", [P, 2, D])
            by_channel = lambda ap, k: ap[:, 0:128] if k == 0 else ap[:, 128 + k - 1:512:3]
            layernorm_phase(nc, m, m.x, ring, m.xt, cols=by_channel)

            def operands(n, bank):
                return [(bank[0:P, k * 128:(k + 1) * 128], m.xt[:, k, tile(n)], up[:, min(k, 1), :]) for k in range(KB)]

            with phase(nc, "loaded", "product", "taken", "st_a", "st_b") as (block, loaded, product, taken, st_a, st_b):
                stored = (st_a, st_b)

                @block.sync
                def _(sp):
                    sp.dma_start(up[:, 0, :], a["L0_gnn_W_up0"]).then_inc(loaded, 16)
                    sp.dma_start(up[:, 1, :], a["L0_gnn_W_up1"]).then_inc(loaded, 16)
                    for i in range(T):
                        sp.wait_ge(taken, i + 1)
                        sp.dma_start(a["xup"][tile(i), :], res[:, i % 2, :]).then_inc(stored[i % 2], 16)
                    for s in stored:
                        sp.wait_ge(s, 16 * T // 2)

                @block.tensor
                def _(pe):
                    pe.wait_ge(loaded, 32)
                    for i in range(T):
                        if i >= 8:
                            pe.wait_ge(taken, i - 7)
                        for out, lhsT, rhs in operands(i, m.ps[:, i % 8, :]):
                            ins = pe.matmul(out, lhsT, rhs, start=True, stop=True)
                        ins.then_inc(product, 1)

                @block.scalar
                def _(act):
                    for i in range(T):
                        act.wait_ge(product, i + 1)
                        if i >= 2:
                            act.wait_ge(stored[i % 2], 16 * (i // 2))
                        act.activation(res[:, i % 2, :], m.ps[0:P, i % 8, :], ACT.Copy, scale=MUL ** -0.5).then_inc(taken, 1)

        with ExitStack() as c2:
            m.iota = sb(nc, c2, "iota", [P, N])
            edge_mlp_phase(nc, m, a["ef_t"], a["L0_gnn_W_mlp1"], a["L0_gnn_W_mlp2"], a["L0_gnn_W_mlp3"], a["h3"])
            edges(nc, m, a, c2)
        with ExitStack() as c2:
            wo = sb(nc, c2, "w_out", [128, 2, 2, MUL])

            def operands(n, bank):
                t = tile(n)
                out = []
                for k in range(4):
                    first, second = (3, 4) if k == 0 else (k - 1, 4 + k)
                    for j, blk in enumerate((first, second)):
                        out.append((k, j, m.acc[:, blk, t], wo[:, min(k, 1), j, :]))
                return out

            with phase(nc, "loaded", "product", "taken") as (block, loaded, product, taken):
                @block.sync
                def _(sp):
                    for k, w in enumerate((a["L0_gnn_W_out0"], a["L0_gnn_W_out1"])):
                        sp.dma_start(wo[:, k, :, :], wview(w)).then_inc(loaded, 16)

                @block.tensor
                def _(pe):
                    pe.wait_ge(loaded, 32)
                    for i in range(T):
                        if i >= 8:
                            pe.wait_ge(taken, i - 7)
                        for k, j, lhsT, rhs in operands(i, None):
                            ins = pe.matmul(m.ps[0:P, i % 8, k * 128:(k + 1) * 128], lhsT, rhs, start=j == 0, stop=j == 1)
                        ins.then_inc(product, 1)

                @block.vector
                def _(dve):
                    scale = (2 * MUL) ** -0.5 / 10.0
                    for i in range(T):
                        dve.wait_ge(product, i + 1)
                        dve.scalar_tensor_tensor(m.x[:, i, 0:128], m.ps[0:P, i % 8, 0:128], scale, m.x[:, i, 0:128], ALU.mult, ALU.add)
                        vec = m.x[:, i, 128:512].rearrange("p (v k) -> p k v", k=3)
                        dve.scalar_tensor_tensor(vec, m.ps[0:P, i % 8, 128:512].rearrange("p (k v) -> p k v", k=3),
                                                 scale, vec, ALU.mult, ALU.add).then_inc(taken, 1)



COLUMNS = ("L0_mix_b_in", "L1_gnn_b1", "L1_mix_b1", "L1_mix_g1", "L1_mix_be1", "L1_mix_g2", "L1_mix_be2",
           "L1_ffn_ln1_w", "L1_ffn_ln1_b", "L1_ffn_ln2_w", "L1_ffn_ln2_b", "L1_ffn_eb1")


def layouts(inputs):
    import numpy as np
    out = {}
    for k, v in inputs.items():
        out[k] = np.asarray(v)
    by_super = lambda v: np.ascontiguousarray(np.asarray(v).reshape(SB, P, G, -1).transpose(1, 0, 2, 3))
    out["src_l"] = by_super(out.pop("src"))[..., 0].copy()
    out["dst_l"] = by_super(out.pop("dst"))[..., 0].copy()
    out["ea4_l"] = by_super(out.pop("edge_attr_4"))
    ef = out.pop("edge_attr_8").reshape(SB, P, G, 8)
    out["ef_t"] = np.ascontiguousarray(ef.transpose(3, 0, 2, 1).reshape(8, E))
    w = out["L0_mix_W_in"]
    out["L0_mix_W_in"] = np.concatenate([w[:MUL]] + [w[MUL + k::3] for k in range(3)])
    out["L1_mix_bqk"] = np.ascontiguousarray(out["L1_mix_bqkv"].reshape(12, 128).T)
    for k, v in list(out.items()):
        if k in COLUMNS:
            out[k] = np.ascontiguousarray(np.moveaxis(v.reshape(v.shape[:-1] + (-1, 128)), -1, -2))
    return out


def build(nc, arrays, stop=None):
    from concourse import mybir as _mybir
    a = {name: nc.dram_tensor(f"in_{name}", v.shape, _mybir.dt.from_np(v.dtype), kind="ExternalInput").ap()
         for name, v in arrays.items()}
    a["out"] = nc.dram_tensor("out", (N, D), F32, kind="ExternalOutput").ap()
    a["xs"] = nc.dram_tensor("xs", (N, D), F32).ap()
    a["xn"] = nc.dram_tensor("xn", (N, D), F32).ap()
    a["xup"] = nc.dram_tensor("xup", (N, D), F32).ap()
    a["h3"] = nc.dram_tensor("h3", (HID, E), F32).ap()
    program(nc, a, stop)


def kernel(**inputs):
    import concourse.bacc as _bacc
    from concourse.bass_utils import run_bass_kernel_spmd as _run
    nc = _bacc.Bacc("TRN2", target_bir_lowering=False, num_devices=1)
    arrays = layouts(inputs)
    build(nc, arrays)
    r = _run(nc, [{f"in_{k}": v for k, v in arrays.items()}], core_ids=[0])
    return r.results[0]["out"]
```
